# Optimizing a Trainium2 kernel written in Bass

```python
import numpy as np
import jax
import jax.numpy as jnp

def _softmax(x, axis=-1):
    return jax.nn.softmax(x, axis=axis)

def _gelu(x):
    return jax.nn.gelu(x, approximate=True)

def _silu(x):
    return jax.nn.silu(x)

def _sigmoid(x):
    return jax.nn.sigmoid(x)

def _layernorm(x, axis=-1, eps=1e-05):
    m = jnp.mean(x, axis=axis, keepdims=True)
    v = jnp.var(x, axis=axis, keepdims=True)
    return (x - m) / jnp.sqrt(v + eps)

def _scatter_add(tgt, idx, src, axis=0):
    return tgt.at[idx].add(src)

def _segment_sum(src, seg, n):
    return jax.ops.segment_sum(src, seg, n)
kernel_name = 'mk_adj_preln_d2_adj_r2_c30c23'

def setup_inputs(seed: int=0):
    np.random.seed(seed)
    _w = jnp.asarray

    def _rec_inputs():
        import jax
        import jax.numpy as jnp
        _gk = jax.random.key(seed)
        x = -0.0002928 + 1 * jax.random.normal(jax.random.fold_in(_gk, 1), (8, 1024, 128), jnp.float32)
        _a = jax.random.bernoulli(jax.random.fold_in(_gk, 2), 0.00390625, (1024, 1024))
        _af = _a.astype(jnp.float32)
        adj = _af
        return (x, adj)
    x, adj = _rec_inputs()

    def _L0_gnn_setup():
        import jax, jax.numpy as jnp
        import numpy as np
        B, N, C, D = (8, 1024, 128, 128)
        NEG = -1e+16
        key = jax.random.key(seed)
        k1, k2, k3, k4, k5 = jax.random.split(key, 5)
        inputs = jax.random.normal(k1, (B, N, C), dtype=jnp.float32)
        graph = jax.random.bernoulli(k2, 0.5, (N, N)).astype(jnp.float32)
        W = jax.random.normal(k3, (C, D), dtype=jnp.float32) * (1.0 / np.sqrt(C))
        b_lin = jax.random.normal(k4, (D,), dtype=jnp.float32) * 0.02
        b = jax.random.normal(k5, (D,), dtype=jnp.float32)
        return {'inputs': inputs, 'graph': graph, 'W': W, 'b_lin': b_lin, 'b': b}
    _L0_gnn_all = _L0_gnn_setup()
    _L0_gnn_in = {k: v for k, v in _L0_gnn_all.items() if k in ('W', 'b_lin', 'b')}
    del _L0_gnn_all

    def _L1_gnn_setup():
        import jax, jax.numpy as jnp
        import numpy as np
        EPS_LN = 1e-05

        def _layernorm(x, g, b):
            mu = x.mean(-1, keepdims=True)
            var = ((x - mu) ** 2).mean(-1, keepdims=True)
            return (x - mu) / jnp.sqrt(var + EPS_LN) * g + b
        key = jax.random.key(seed)
        B, N, D, H = (4, 1024, 128, 4)
        hid = int(D * 2.0)
        ks = jax.random.split(key, 12)
        x = jax.random.normal(ks[0], (B, N, D), jnp.float32)
        Au = jax.random.uniform(ks[1], (N, N)) < 0.004
        A = jnp.logical_or(Au, Au.T)
        A = A.at[jnp.arange(N), jnp.arange(N)].set(False)
        Af = A.astype(jnp.float32)
        deg = Af.sum(axis=1)
        L = jnp.diag(deg) - Af
        adjacency = Af + jnp.eye(N, dtype=jnp.float32)
        s = lambda k, sh, f: jax.random.normal(k, sh, jnp.float32) * f
        sc = 1.0 / np.sqrt(D)
        Wc = s(ks[2], (D, D), sc)
        bc = jnp.zeros((D,), jnp.float32)
        Wq = s(ks[3], (D, D), sc)
        Wk = s(ks[4], (D, D), sc)
        Wv = s(ks[5], (D, D), sc)
        Wo = s(ks[6], (D, D), sc)
        bo = jnp.zeros((D,), jnp.float32)
        W1 = s(ks[7], (D, hid), sc)
        b1 = jnp.zeros((hid,), jnp.float32)
        W2 = s(ks[8], (hid, D), 1.0 / np.sqrt(hid))
        b2 = jnp.zeros((D,), jnp.float32)
        g1 = jnp.ones((D,), jnp.float32)
        be1 = jnp.zeros((D,), jnp.float32)
        g2 = jnp.ones((D,), jnp.float32)
        be2 = jnp.zeros((D,), jnp.float32)
        g3 = jnp.ones((D,), jnp.float32)
        be3 = jnp.zeros((D,), jnp.float32)
        return dict(x=x, L=L, adjacency=adjacency, Wc=Wc, bc=bc, g1=g1, be1=be1, Wq=Wq, Wk=Wk, Wv=Wv, Wo=Wo, bo=bo, g2=g2, be2=be2, W1=W1, b1=b1, W2=W2, b2=b2, g3=g3, be3=be3)
    _L1_gnn_all = _L1_gnn_setup()
    _L1_gnn_in = {k: v for k, v in _L1_gnn_all.items() if k in ('Wc', 'bc', 'g1', 'be1', 'Wq', 'Wk', 'Wv', 'Wo', 'bo', 'g2', 'be2', 'W1', 'b1', 'W2', 'b2', 'g3', 'be3')}
    del _L1_gnn_all
    return {'x': x, 'adj': adj, 'L0_gnn_W': _L0_gnn_in['W'], 'L0_gnn_b_lin': _L0_gnn_in['b_lin'], 'L0_gnn_b': _L0_gnn_in['b'], 'L1_gnn_Wc': _L1_gnn_in['Wc'], 'L1_gnn_bc': _L1_gnn_in['bc'], 'L1_gnn_g1': _L1_gnn_in['g1'], 'L1_gnn_be1': _L1_gnn_in['be1'], 'L1_gnn_Wq': _L1_gnn_in['Wq'], 'L1_gnn_Wk': _L1_gnn_in['Wk'], 'L1_gnn_Wv': _L1_gnn_in['Wv'], 'L1_gnn_Wo': _L1_gnn_in['Wo'], 'L1_gnn_bo': _L1_gnn_in['bo'], 'L1_gnn_g2': _L1_gnn_in['g2'], 'L1_gnn_be2': _L1_gnn_in['be2'], 'L1_gnn_W1': _L1_gnn_in['W1'], 'L1_gnn_b1': _L1_gnn_in['b1'], 'L1_gnn_W2': _L1_gnn_in['W2'], 'L1_gnn_b2': _L1_gnn_in['b2'], 'L1_gnn_g3': _L1_gnn_in['g3'], 'L1_gnn_be3': _L1_gnn_in['be3']}

def reference(x, adj, L0_gnn_W, L0_gnn_b_lin, L0_gnn_b, L1_gnn_Wc, L1_gnn_bc, L1_gnn_g1, L1_gnn_be1, L1_gnn_Wq, L1_gnn_Wk, L1_gnn_Wv, L1_gnn_Wo, L1_gnn_bo, L1_gnn_g2, L1_gnn_be2, L1_gnn_W1, L1_gnn_b1, L1_gnn_W2, L1_gnn_b2, L1_gnn_g3, L1_gnn_be3):
    import jax
    import jax.numpy as jnp

    def _L0_gnn_ref(inputs, graph, W, b_lin, b):
        import jax, jax.numpy as jnp
        import numpy as np
        B, N, C, D = (8, 1024, 128, 128)
        NEG = -1e+16
        h = jnp.einsum('bnc,cd->bnd', inputs, W) + b_lin
        scores = jnp.einsum('bnd,bmd->bnm', h, h) * graph[None, :, :]
        scores = jnp.where(scores == 0.0, NEG, scores)
        attention = jax.nn.softmax(scores, axis=2)
        return jnp.einsum('bnm,bmd->bnd', attention, h) + b

    def _L1_gnn_ref(x, L, adjacency, Wc, bc, g1, be1, Wq, Wk, Wv, Wo, bo, g2, be2, W1, b1, W2, b2, g3, be3):
        import jax, jax.numpy as jnp
        import numpy as np
        EPS_LN = 1e-05

        def _layernorm(x, g, b):
            mu = x.mean(-1, keepdims=True)
            var = ((x - mu) ** 2).mean(-1, keepdims=True)
            return (x - mu) / jnp.sqrt(var + EPS_LN) * g + b
        B, N, D = x.shape
        H = 4
        hd = D // H
        eig = jnp.linalg.eigvalsh(L)
        lam_max = eig[-1] + 1e-08
        L_norm = 2.0 * L / lam_max - jnp.eye(N, dtype=L.dtype)
        xp = jnp.einsum('mn,bnf->bmf', L_norm, x)
        h = xp @ Wc + bc
        h = _layernorm(h, g1, be1)
        h = jax.nn.relu(h)
        x1 = h + x
        q = (x1 @ Wq).reshape(B, N, H, hd).transpose(0, 2, 1, 3)
        k = (x1 @ Wk).reshape(B, N, H, hd).transpose(0, 2, 1, 3)
        v = (x1 @ Wv).reshape(B, N, H, hd).transpose(0, 2, 1, 3)
        scores = jnp.einsum('bhnd,bhmd->bhnm', q, k) / np.sqrt(hd).astype(np.float32)
        scores = jnp.where(adjacency[None, None] > 0, scores, jnp.float32(-1000000000.0))
        attn = jax.nn.softmax(scores, axis=-1)
        o = jnp.einsum('bhnm,bhmd->bhnd', attn, v)
        o = o.transpose(0, 2, 1, 3).reshape(B, N, D)
        o = o @ Wo + bo
        x2 = _layernorm(x1 + o, g2, be2)
        m = jax.nn.gelu(x2 @ W1 + b1, approximate=False) @ W2 + b2
        return _layernorm(x2 + m, g3, be3)
    h = jnp.maximum(_layernorm(x, axis=-1), 0.0)
    x = x + _L0_gnn_ref(h, adj, L0_gnn_W, L0_gnn_b_lin, L0_gnn_b)
    h = jnp.maximum(_layernorm(x, axis=-1), 0.0)
    x = x + _L1_gnn_ref(h, adj, adj, L1_gnn_Wc, L1_gnn_bc, L1_gnn_g1, L1_gnn_be1, L1_gnn_Wq, L1_gnn_Wk, L1_gnn_Wv, L1_gnn_Wo, L1_gnn_bo, L1_gnn_g2, L1_gnn_be2, L1_gnn_W1, L1_gnn_b1, L1_gnn_W2, L1_gnn_b2, L1_gnn_g3, L1_gnn_be3)
    return x

_drawn_inputs = setup_inputs


def setup_inputs(seed=0):
    import zlib

    import numpy as np

    out = dict(_drawn_inputs(seed))
    spreads = {'L1_gnn_bc': (0.0, 0.1),
     'L1_gnn_g1': (1.0, 0.2),
     'L1_gnn_be1': (0.0, 0.284),
     'L1_gnn_bo': (0.0, 0.276),
     'L1_gnn_g2': (1.0, 0.2),
     'L1_gnn_be2': (0.0, 0.1),
     'L1_gnn_b1': (0.0, 0.335),
     'L1_gnn_b2': (0.0, 0.1),
     'L1_gnn_g3': (1.0, 0.2),
     'L1_gnn_be3': (0.0, 0.1)}
    factors = {'L0_gnn_b_lin': 3.389}
    for name, (base, spread) in spreads.items():
        noise = np.random.default_rng([zlib.crc32(name.encode()), seed]).standard_normal(out[name].shape)
        drawn = base * np.exp(spread * noise) if base else spread * noise
        out[name] = jnp.asarray(drawn.astype(out[name].dtype))
    for name, factor in factors.items():
        out[name] = (out[name] * factor).astype(out[name].dtype)
    return out
```

```python
from contextlib import ExitStack

import concourse.bass as bass
from concourse import mybir

F32 = mybir.dt.float32
BF16 = mybir.dt.bfloat16
FP8 = mybir.dt.float8e4
ALU = mybir.AluOpType
ACT = mybir.ActivationFunctionType
AX = mybir.AxisListType

P = 128
B, N, D, H = 8, 1024, 128, 4
T = N // P
HALF = N // 2
HT = T // 2
HD = D // H
HID = 2 * D
HC = HID // P
EPS = 1e-5
FAR = 2.0 ** 100
TINY = 1e-30
GROUP = 4

BANK_T, BANK_O, BANK_AUX = 4, 6, 7

AUX1 = {0: ["pw0"], 1: ["pw1"], 2: ["h0T0"], 3: ["h0T1", "pw2"], 4: ["hT0"], 5: ["hT1", "norm"],
        6: ["hrow0", "ot0"], 7: ["hrow1", "ot1"]}
PREP1 = ["h0T0", "h0T1", "hT0", "hT1", "hrow0", "hrow1"]


def aux_list(table, first, last, prep, post):
    return [s for u in sorted(table) for s in table[u]
            if not (last and s in prep) and not (first and s in post)]


def bc(ap, n):
    return ap.rearrange("p (k o) -> p k o", o=1).to_broadcast([ap.shape[0], ap.shape[1], n])


def build(nc, x, adj, W, b_lin, b, Wc, bcv, g1, be1, Wq, Wk, Wv, Wo, bo, g2, be2, W1, b1, W2, b2, g3, be3, out):
    x1_dram = nc.dram_tensor("after_block1", (B, N, D), F32, kind="Internal").ap()
    with ExitStack() as ctx:
        sb = lambda n, s, d: ctx.enter_context(nc.sbuf_tensor(n, s, d))
        banks = ctx.enter_context(nc.psum_tensor("banks", [P, 8, HALF], F32))
        shared = {
            "ident": sb("ident", [P, P], F32),
            "neg_half": sb("neg_half", [P, T], F32),
            "adjT": sb("adjT", [P, T, N], FP8),
            "off": sb("off", [P, T, N], BF16),
            "two_over_lam": sb("two_over_lam", [P, 1], F32),
        }
        block1(nc, x, adj, W, b_lin, b, x1_dram, banks, shared)
        block2(nc, x1_dram, Wc, bcv, g1, be1, Wq, Wk, Wv, Wo, bo, g2, be2, W1, b1, W2, b2, g3, be3, out, banks, shared)


def arrivals(bt, par):
    return (bt // 2 + 1 if isinstance(bt, int) else (bt - par) // 2 + 1) * 16


def rows(ap):
    return ap.rearrange("(t p) d -> p t d", p=P)


def across(vec):
    return vec.rearrange("(o n) -> o n", o=1).to_broadcast([P, vec.shape[0]])


def block1(nc, x, adj, W, b_lin, b, x1_dram, banks, shared):
    with ExitStack() as ctx:
        sb = lambda n, s, d: ctx.enter_context(nc.sbuf_tensor(n, s, d))
        sem = lambda n: ctx.enter_context(nc.semaphore(n))
        ident, neg_half, adjT, off, two_over_lam = (shared[k] for k in (
            "ident", "neg_half", "adjT", "off", "two_over_lam"))

        adj_f = sb("adj_f", [P, T, N], F32)
        pt = sb("pt", [P, 2, T, HALF], F32)
        sym = sb("sym", [P, T, N], BF16)
        ones = sb("ones", [P, P], F32)
        identb = sb("identb", [P, P], BF16)
        far_diag = sb("far_diag", [P, P], BF16)
        w_sb = sb("w_sb", [P, D], F32)
        blin_col = sb("blin_col", [P, 1], F32)
        b_row = sb("b_row", [P, D], F32)
        xin = sb("xin", [P, 2, T, D], F32)
        xb = sb("xb", [P, 2, T, D], F32)
        xn = sb("xn", [P, T, D], F32)
        h0 = sb("h0", [P, T, D], F32)
        h0T = sb("h0T", [P, N], F32)
        hT = sb("hT", [P, 2, N], F32)
        hrow = sb("hrow", [P, 2, T, D], F32)
        z = sb("z", [P, 2, N], BF16)
        prob = sb("prob", [P, 2, N], F32)
        nmax = sb("nmax", [P, T], F32)
        den = sb("den", [P, 2, T], F32)
        rden = sb("rden", [P, T], F32)
        oT = sb("oT", [P, N], F32)
        stats = sb("stats", [P, T, 6], F32)
        mv = sb("mv", [P, T, 2], F32)
        ve = sb("ve", [P, T], F32)
        rstd = sb("rstd", [P, T], F32)
        nm = sb("nm", [P, T], F32)
        nmr = sb("nmr", [P, T], F32)
        v = sb("v", [P, T], F32)
        vsum = sb("vsum", [P, T], F32)
        y = sb("y", [P, T], F32)
        vr1 = sb("vr1", [P, T], F32)
        vr2 = sb("vr2", [P, T], F32)
        vp = sb("vp", [P, T, 3], BF16)
        tot = sb("tot", [P, 1], F32)
        tot2 = sb("tot2", [P, 1], F32)
        rtot = sb("rtot", [P, 1], F32)
        junk = sb("junk", [P, T], F32)
        junk2 = sb("junk2", [P, T], F32)
        nd = sb("nd", [P, 2], F32)
        fin = sb("fin", [P, 6], F32)

        consts_in = sem("consts_in")
        adj_in = [sem(f"adj_in{t}") for t in range(T)]
        x_in = [sem(f"x_in{k}") for k in range(2)]
        x1_out = sem("x1_out")
        zeroed = sem("zeroed")
        idents = sem("idents")
        adj_bf = sem("adj_bf")
        adjT_ready = sem("adjT_ready")
        adjT_copied = sem("adjT_copied")
        sym_ready = sem("sym_ready")
        off_ready = sem("off_ready")
        stats_done = sem("stats_done")
        mv_done = sem("mv_done")
        ve_done = sem("ve_done")
        rstd_done = sem("rstd_done")
        h0_done = sem("h0_done")
        xb_done = sem("xb_done")
        aux_ready = sem("aux_ready")
        aux_free = sem("aux_free")
        s_ready = sem("s_ready")
        z_done = sem("z_done")
        masked = sem("masked")
        max_done = sem("max_done")
        exp_done = sem("exp_done")
        tlo_ready = sem("tlo_ready")
        thi_ready = sem("thi_ready")
        ptlo_done = sem("ptlo_done")
        pthi_done = sem("pthi_done")
        av_done = sem("av_done")
        oT_done = sem("oT_done")
        rden_done = sem("rden_done")
        y_done = sem("y_done")
        tot_done = sem("tot_done")
        v_step = sem("v_step")
        v_ready = sem("v_ready")
        fin_step = sem("fin_step")
        lam_done = sem("lam_done")
        held_pool = sem("held_pool")
        held_dve = sem("held_dve")
        held_sp = sem("held_sp")

        aux = banks[:, BANK_AUX, :]
        obank = banks[:, BANK_O, :]
        scores = [banks[:, 2 * k:2 * k + 2, :].rearrange("p a n -> p (a n)") for k in range(2)]

        PER = 12
        VSTEPS = 16

        def lists(bk):
            first, last = bk is not None and bk == 0, bk is not None and bk == B - 1
            order = aux_list(AUX1, first, last, PREP1, ("ot0", "ot1"))
            return {u: [s for s in AUX1[u] if s in order] for u in AUX1}, order

        def base(bt):
            if isinstance(bt, int):
                return 6 if bt == 0 else 4 + PER * bt
            return bt * PER + 4

        def batches(eng, body):
            body(0, 0, 0)
            with eng.Fori(0, (B - 2) // 2) as i:
                for k in (1, 2):
                    body(i * 2 + k, k % 2, None)
            body(B - 1, (B - 1) % 2, B - 1)

        block = ctx.enter_context(nc.Block())

        @block.sync
        def _(sp):
            def hold(s, value):
                sp.wait_ge(s, value)
                sp.sem_inc(held_sp, 1)

            sp.sem_inc(x1_out, 16)
            sp.dma_start(xin[:, 0], rows(x[0])).then_inc(x_in[0], 16)
            for t in range(T):
                sp.dma_start(adj_f[:, t, :], adj[P * t:P * (t + 1), :]).then_inc(adj_in[t], 16)
            sp.dma_start(w_sb[:, :], W).then_inc(consts_in, 16)
            sp.dma_start(blin_col[:, :], b_lin.rearrange("(d o) -> d o", o=1)).then_inc(consts_in, 16)
            sp.dma_start(b_row[:, :], across(b)).then_inc(consts_in, 16)
            sp.dma_start(xin[:, 1], rows(x[1])).then_inc(x_in[1], 16)

            def body(bt, par, bk):
                if bk != 0:
                    pieces, order = lists(bk)
                    hold(aux_free, base(bt) + order.index("ot1") + 1)
                    sp.dma_start(rows(x1_dram[bt - 1] if isinstance(bt, int) else
                                      x1_dram[bass.ds(bt - 1, 1)].rearrange("o n d -> (o n) d")),
                                 xn[:, :, :]).then_inc(x1_out, 16)

            def load(bt, par):
                hold(xb_done, bt * 1)
                sp.dma_start(xin[:, 1 - par], rows(x[bt + 1] if isinstance(bt, int) else
                             x[bass.ds(bt + 1, 1)].rearrange("o n d -> (o n) d"))).then_inc(x_in[1 - par], 16)

            with sp.Fori(0, (B - 2) // 2) as i:
                for k in (1, 2):
                    load(i * 2 + k, k % 2)
                    body(i * 2 + k, k % 2, None)
            body(B - 1, (B - 1) % 2, B - 1)
            _, order = lists(B - 1)
            sp.wait_ge(aux_free, base(B - 1) + len(order) + 2)
            sp.dma_start(rows(x1_dram[B - 1]), xn[:, :, :]).then_inc(x1_out, 16)
            sp.wait_ge(x1_out, 16 * (B + 1))

        @block.gpsimd
        def _(pool):
            for m in (ident, identb, far_diag):
                nc.gpsimd.memset(m[:, :], 0.0).then_inc(zeroed, 1)
            nc.gpsimd.memset(ones[:, :], 1.0).then_inc(zeroed, 1)
            nc.gpsimd.memset(neg_half[:, :], -0.5).then_inc(zeroed, 1)
            nc.gpsimd.memset(v[:, :], 1.0 / N).then_inc(zeroed, 1)
            pool.wait_ge(zeroed, 6)
            for m, fill in ((ident, 1.0), (identb, 1.0), (far_diag, -FAR)):
                nc.gpsimd.affine_select(out=m[:, :], in_=m[:, :], compare_op=ALU.not_equal, fill=fill, base=0,
                                        pattern=[[-1, P]], channel_multiplier=1).then_inc(idents, 1)

            def hold(s, value):
                pool.wait_ge(s, value)
                pool.sem_inc(held_pool, 1)

            def split_v(n, m):
                if m is not None:
                    hold(v_step, n)
                nc.gpsimd.tensor_scalar(vp[:, :, 0], v[:, :], 1.0, 0.0, ALU.mult, ALU.add).then_inc(v_step, 1)
                hold(v_step, n + 1)
                nc.gpsimd.tensor_tensor(vr1[:, :], v[:, :], vp[:, :, 0], ALU.subtract).then_inc(v_step, 1)
                hold(v_step, n + 2)
                nc.gpsimd.tensor_scalar(vp[:, :, 1], vr1[:, :], 1.0, 0.0, ALU.mult, ALU.add).then_inc(v_step, 1)
                hold(v_step, n + 3)
                nc.gpsimd.tensor_tensor(vp[:, :, 2], vr1[:, :], vp[:, :, 1], ALU.subtract).then_inc(v_step, 1)
                hold(v_step, n + 4)
                pool.sem_inc(v_ready, 1)

            def ln_scale(n):
                hold(mv_done, n * 1 + 1)
                nc.gpsimd.tensor_scalar(ve[:, :], mv[:, :, 1], 1.0, EPS, ALU.mult, ALU.add).then_inc(ve_done, 1)
                nc.gpsimd.tensor_scalar(nm[:, :], mv[:, :, 0], -1.0, 0.0, ALU.mult, ALU.add).then_inc(ve_done, 1)
                hold(ve_done, n * 2 + 2)
                if not isinstance(n, int) or n > 0:
                    hold(h0_done, n * 1)
                nc.gpsimd.tensor_tensor(rstd[:, :], ve[:, :], neg_half[:, :], ALU.pow).then_inc(rstd_done, 1)
                hold(rstd_done, n * 2 + 1)
                nc.gpsimd.tensor_tensor(nmr[:, :], nm[:, :], rstd[:, :], ALU.mult).then_inc(rstd_done, 1)

            split_v(0, None)
            ln_scale(0)

            def body(bt, par, bk):
                pieces, order = lists(bk)
                if bk != B - 1:
                    ln_scale(bt + 1)
                if bk == 0:
                    hold(consts_in, 48)
                hold(x_in[par], arrivals(bt, par))
                if bk is None or bk > 1:
                    hold(aux_free, base(bt))
                nc.gpsimd.tensor_tensor(xb[:, par], xin[:, par], b_row[:, :].rearrange("p (o d) -> p o d", o=1)
                                        .to_broadcast([P, T, D]), ALU.add).then_inc(xb_done, 1)
                for u in range(T):
                    for s in pieces[u]:
                        k = 4 + bt * VSTEPS
                        if s in ("pw0", "pw1", "pw2"):
                            n = int(s[2])
                            hold(y_done, bt * 3 + n + 1)
                            if n < 2:
                                nc.gpsimd.tensor_tensor(v[:, :], v[:, :], y[:, :], ALU.add).then_inc(v_step, 1)
                                split_v(k + 5 * n + 1, 0)
                            else:
                                nc.gpsimd.tensor_tensor(vsum[:, :], v[:, :], y[:, :], ALU.add).then_inc(v_step, 1)
                        if s == "norm":
                            hold(tot_done, bt * 1 + 1)
                            nc.gpsimd.tensor_tensor(v[:, :], vsum[:, :], rtot[:, 0:1].to_broadcast([P, T]), ALU.mult)\
                                .then_inc(v_step, 1)
                            split_v(k + 12, 0)

            batches(pool, body)

        @block.scalar
        def _(act):
            act.sem_inc(oT_done, 1)
            for j in range(T):
                act.wait_ge(adjT_ready, j + 1)
                nc.scalar.activation(adjT[:, j, :], banks[:, j % 4, :].bitcast(BF16), ACT.Copy, saturate=False)\
                    .then_inc(adjT_copied, 1)

            def normalize(n, par):
                act.wait_ge(rstd_done, n * 2 + 2)
                for t in range(T):
                    ins = nc.scalar.activation(h0[:, t, :], xin[:, par, t, :],
                                               ACT.Relu, bias=nmr[:, t:t + 1], scale=rstd[:, t:t + 1])
                ins.then_inc(h0_done, 1)

            def prep(s, value, par):
                if s in ("h0T0", "h0T1"):
                    k = int(s[-1])
                    act.wait_ge(aux_ready, value)
                    nc.scalar.activation(h0T[:, HALF * k:HALF * (k + 1)], aux, ACT.Copy).then_inc(aux_free, 1)
                if s in ("hT0", "hT1"):
                    k = int(s[-1])
                    act.wait_ge(aux_ready, value)
                    nc.scalar.activation(hT[:, par, HALF * k:HALF * (k + 1)], aux, ACT.Identity, bias=blin_col[:, 0:1])\
                        .then_inc(aux_free, 1)
                if s in ("hrow0", "hrow1"):
                    k = int(s[-1])
                    act.wait_ge(aux_ready, value)
                    nc.scalar.activation(hrow[:, par, HT * k:HT * (k + 1), :].rearrange("p t d -> p (t d)"), aux, ACT.Copy)\
                        .then_inc(aux_free, 1)

            act.wait_ge(consts_in, 48)
            act.wait_ge(x_in[0], 16)
            normalize(0, 0)
            for n, s in enumerate(PREP1):
                prep(s, n + 1, 0)

            def exp_unit(U, u, par):
                act.wait_ge(max_done, U + 1)
                if not isinstance(U, int) or U >= 2:
                    act.wait_ge(thi_ready, U - 1)
                nc.scalar.activation(prob[:, u % 2, :], scores[u % 2], ACT.Exp, bias=nmax[:, u:u + 1],
                                     accum_out=den[:, par, u:u + 1]).then_inc(exp_done, 1)

            def evac_hi(ub, u):
                U = ub * T + u
                act.wait_ge(thi_ready, U + 1)
                g = u // GROUP
                if u % GROUP == 0 and (not isinstance(U, int) or U >= 2 * GROUP):
                    act.wait_ge(av_done, ub * 2 + g - 1)
                c = P * (u % GROUP)
                nc.scalar.activation(pt[:, g, HT:T, c:c + P],
                                     banks[:, BANK_T + 1, :].rearrange("p (t n) -> p t n", t=HT), ACT.Copy)\
                    .then_inc(pthi_done, 1)

            def copy_out(g, half, value):
                act.wait_ge(av_done, g + 1)
                if value is not None:
                    act.wait_ge(aux_ready, value)
                nc.scalar.activation(oT[:, HALF * half:HALF * (half + 1)], obank, ACT.Copy).then_inc(oT_done, 1)

            def body(bt, par, bk):
                pieces, order = lists(bk)
                U0 = bt * T
                if bk != B - 1:
                    act.wait_ge(x_in[1 - par], arrivals(bt + 1, 1 - par))
                    normalize(bt + 1, 1 - par)
                for u in range(T):
                    if bk != 0 or u >= 1:
                        exp_unit(U0 + u - 1, (u - 1) % T, par if u >= 1 else 1 - par)
                    if bk != 0 or u >= 2:
                        evac_hi(bt if u >= 2 else bt - 1, (u - 2) % T)
                    if u == 1 and bk != 0:
                        copy_out(bt * 2 - 2, 0, base(bt))
                    if u == 5 and bk != 0:
                        copy_out(bt * 2 - 1, 1, None)
                    for s in pieces[u]:
                        prep(s, base(bt) + order.index(s) + 1, 1 - par)

            batches(act, body)
            exp_unit(B * T - 1, T - 1, (B - 1) % 2)
            for u in (T - 2, T - 1):
                evac_hi(B - 1, u)
            _, order = lists(B - 1)
            copy_out(2 * B - 2, 0, base(B - 1) + len(order))
            copy_out(2 * B - 1, 1, None)

        @block.vector
        def _(dve):
            def hold(s, value):
                dve.wait_ge(s, value)
                dve.sem_inc(held_dve, 1)

            for t in range(T):
                dve.wait_ge(adj_in[t], 16)
                nc.vector.tensor_copy(off[:, t, :], adj_f[:, t, :]).then_inc(adj_bf, 1)

            def ln_stats(n, par):
                hold(x_in[par], arrivals(n, par))
                if not isinstance(n, int) or n > 0:
                    hold(rstd_done, n * 2)
                for t in range(T):
                    ins = nc.vector.bn_stats(stats[:, t, :], xin[:, par, t, :])
                ins.then_inc(stats_done, 1)
                hold(stats_done, n * 1 + 1)
                for t in range(T):
                    ins = nc.vector.bn_aggr(mv[:, t, :], stats[:, t, :])
                ins.then_inc(mv_done, 1)

            ln_stats(0, 0)
            for j in range(T):
                dve.wait_ge(adjT_copied, j + 1)
                nc.vector.tensor_tensor(sym[:, j, :], off[:, j, :], adjT[:, j, :], ALU.add).then_inc(sym_ready, 1)
            dve.wait_ge(sym_ready, T)
            for j in range(T):
                nc.vector.tensor_scalar(off[:, j, :], off[:, j, :], -1.0, 1.0, ALU.mult, ALU.add).then_inc(off_ready, 1)
            dve.wait_ge(off_ready, T)

            def mask_unit(U, u):
                dve.wait_ge(s_ready, U + 1)
                if not isinstance(U, int) or U >= 2:
                    hold(masked, U - 1)
                nc.vector.scalar_tensor_tensor(out=z[:, u % 2, :], in0=scores[u % 2], scalar=0.0, in1=off[:, u, :],
                                               op0=ALU.is_equal, op1=ALU.max).then_inc(z_done, 1)

            def max_unit(U, u):
                hold(masked, U + 1)
                if not isinstance(U, int) or U >= T:
                    hold(exp_done, U - T + 1)
                nc.vector.tensor_reduce(nmax[:, u:u + 1], scores[u % 2], AX.X, ALU.max, negate=True).then_inc(max_done, 1)

            def evac_lo(ub, u):
                U = ub * T + u
                hold(tlo_ready, U + 1)
                g = u // GROUP
                if u % GROUP == 0 and (not isinstance(U, int) or U >= 2 * GROUP):
                    dve.wait_ge(av_done, ub * 2 + g - 1)
                c = P * (u % GROUP)
                nc.vector.tensor_copy(pt[:, g, 0:HT, c:c + P],
                                      banks[:, BANK_T, :].rearrange("p (t n) -> p t n", t=HT)).then_inc(ptlo_done, 1)

            def power(s, value, bt):
                if s in ("pw0", "pw1", "pw2"):
                    hold(aux_ready, value)
                    if int(s[2]) == 0:
                        hold(v_ready, bt * 3 + 1)
                    else:
                        hold(v_ready, bt * 3 + 1 + int(s[2]))
                    nc.vector.tensor_reduce(y[:, :], aux[:, 0:3 * T].rearrange("p (t k) -> p t k", k=3), AX.X, ALU.add)\
                        .then_inc(y_done, 1)
                    hold(y_done, bt * 3 + int(s[2]) + 1)
                    dve.sem_inc(aux_free, 1)
                if s == "norm":
                    hold(aux_ready, value)
                    nc.vector.tensor_reduce(tot[:, :], aux[:, 0:T], AX.X, ALU.add).then_inc(fin_step, 1)
                    hold(fin_step, bt * 2 + 1)
                    dve.sem_inc(aux_free, 1)
                    nc.vector.tensor_scalar(tot2[:, :], tot[:, :], TINY, None, ALU.max).then_inc(fin_step, 1)
                    hold(fin_step, bt * 2 + 2)
                    nc.vector.reciprocal(rtot[:, :], tot2[:, :]).then_inc(tot_done, 1)

            def output(s, value, n, par):
                k = int(s[-1])
                if k == 0:
                    hold(exp_done, (n + 1) * T)
                    nc.vector.reciprocal(rden[:, :], den[:, par, :]).then_inc(rden_done, 1)
                    hold(rden_done, n * 1 + 1)
                    if not isinstance(n, int) or n > 0:
                        hold(x1_out, n * 16 + 16)
                hold(aux_ready, value)
                hold(xb_done, n * 1 + 1)
                for q in range(HT):
                    t = HT * k + q
                    ins = nc.vector.scalar_tensor_tensor(out=xn[:, t, :], in0=aux[:, P * q:P * (q + 1)], scalar=rden[:, t:t + 1],
                                                         in1=xb[:, par, t, :], op0=ALU.mult, op1=ALU.add)
                ins.then_inc(aux_free, 1)

            def body(bt, par, bk):
                pieces, order = lists(bk)
                U0 = bt * T
                if bk != B - 1:
                    ln_stats(bt + 1, 1 - par)
                for u in range(T):
                    mask_unit(U0 + u, u)
                    if bk != 0 or u >= 2:
                        evac_lo(bt if u >= 2 else bt - 1, (u - 2) % T)
                    for s in pieces[u]:
                        value = base(bt) + order.index(s) + 1
                        power(s, value, bt)
                        if s in ("ot0", "ot1"):
                            output(s, value, bt - 1, 1 - par)
                    max_unit(U0 + u, u)

            batches(dve, body)
            _, order = lists(B - 1)
            end = base(B - 1) + len(order)
            for u in (T - 2, T - 1):
                evac_lo(B - 1, u)
            for k in range(2):
                output(f"ot{k}", end + k + 1, B - 1, (B - 1) % 2)
            dve.wait_ge(aux_ready, end + 3)
            nc.vector.tensor_reduce(y[:, :], aux[:, 0:3 * T].rearrange("p (t k) -> p t k", k=3), AX.X, ALU.add)\
                .then_inc(aux_free, 1)
            dve.wait_ge(aux_free, end + 3)
            nc.vector.tensor_tensor_reduce(junk[:, :], v[:, :], y[:, :], 1.0, 0.0, ALU.mult, ALU.add, nd[:, 0:1])\
                .then_inc(fin_step, 1)
            nc.vector.tensor_tensor_reduce(junk2[:, :], v[:, :], v[:, :], 1.0, 0.0, ALU.mult, ALU.add, nd[:, 1:2])\
                .then_inc(fin_step, 1)
            dve.wait_ge(aux_ready, end + 4)
            nc.vector.tensor_copy(fin[:, 0:2], aux[:, 0:2]).then_inc(fin_step, 1)
            n = 2 * B + 3
            for ins in (lambda: nc.vector.tensor_scalar(fin[:, 2:3], fin[:, 1:2], TINY, None, ALU.max),
                        lambda: nc.vector.reciprocal(fin[:, 3:4], fin[:, 2:3]),
                        lambda: nc.vector.tensor_tensor(fin[:, 4:5], fin[:, 0:1], fin[:, 3:4], ALU.mult),
                        lambda: nc.vector.tensor_scalar(fin[:, 5:6], fin[:, 4:5], 0.25, 0.5e-8, ALU.mult, ALU.add)):
                dve.wait_ge(fin_step, n)
                ins().then_inc(fin_step, 1)
                n += 1
            dve.wait_ge(fin_step, n)
            nc.vector.reciprocal(two_over_lam[:, :], fin[:, 5:6]).then_inc(lam_done, 1)
            for j in range(T):
                nc.vector.tensor_scalar(off[:, j, :], off[:, j, :], -FAR, None, ALU.mult).then_inc(off_ready, 1)
            dve.wait_ge(off_ready, 2 * T)

        @block.tensor
        def _(pe):
            pe.wait_ge(idents, 3)
            for j in range(T):
                if j == 0:
                    pe.wait_ge(adj_bf, T)
                if j >= 4:
                    pe.wait_ge(adjT_copied, j - 3)
                for i in range(T):
                    ins = nc.tensor.transpose(banks[:, j % 4, :].bitcast(BF16)[:, P * i:P * (i + 1)],
                                              off[:, i, P * j:P * (j + 1)], identb[:, :])
                ins.then_inc(adjT_ready, 1)

            def prep(s, value, par, n):
                k = int(s[-1])
                if not isinstance(value, int) or value > 1:
                    pe.wait_ge(aux_free, value - 1)
                if s == "h0T0":
                    pe.wait_ge(h0_done, n * 1 + 1)
                if s in ("h0T0", "h0T1"):
                    for q in range(HT):
                        ins = nc.tensor.transpose(aux[:, P * q:P * (q + 1)], h0[:, HT * k + q, :], ident[:, :])
                if s in ("hT0", "hT1"):
                    ins = nc.tensor.matmul(aux, w_sb[:, :], h0T[:, HALF * k:HALF * (k + 1)], start=True, stop=True)
                if s in ("hrow0", "hrow1"):
                    for q in range(HT):
                        t = HT * k + q
                        ins = nc.tensor.transpose(aux[:, P * q:P * (q + 1)], hT[:, par, P * t:P * (t + 1)], ident[:, :])
                ins.then_inc(aux_ready, 1)

            def power(s, value, n):
                pe.wait_ge(aux_free, value - 1)
                pe.wait_ge(v_ready, n) if s != "norm" else pe.wait_ge(v_step, n)
                if s == "norm":
                    nc.tensor.matmul(aux[:, 0:T], ones[:, :], vsum[:, :], start=True, stop=True).then_inc(aux_ready, 1)
                    return
                for j in range(T):
                    for i in range(T):
                        ins = nc.tensor.matmul(aux[:, 3 * j:3 * j + 3], sym[:, i, P * j:P * (j + 1)], vp[:, i, :],
                                               start=(i == 0), stop=(i == T - 1))
                ins.then_inc(aux_ready, 1)

            pe.wait_ge(consts_in, 48)
            for n, s in enumerate(PREP1):
                prep(s, n + 1, 0, 0)
            pe.wait_ge(sym_ready, T)

            def scores_unit(U, u, par):
                if not isinstance(U, int) or U >= 2:
                    pe.wait_ge(exp_done, U - 1)
                else:
                    pe.wait_ge(adjT_copied, T)
                for k in range(2):
                    ins = nc.tensor.matmul(scores[u % 2][:, HALF * k:HALF * (k + 1)], hT[:, par, P * u:P * (u + 1)],
                                           hT[:, par, HALF * k:HALF * (k + 1)], start=True, stop=False, skip_group_check=True)
                ins.then_inc(s_ready, 1)

            def lower_unit(U, u):
                pe.wait_ge(z_done, U + 1)
                for k in range(2):
                    ins = nc.tensor.matmul(scores[u % 2][:, HALF * k:HALF * (k + 1)], far_diag[:, :],
                                           z[:, u % 2, HALF * k:HALF * (k + 1)], start=False, stop=True, skip_group_check=True)
                ins.then_inc(masked, 1)

            def transpose_unit(U, u):
                pe.wait_ge(exp_done, U + 1)
                for half, (free, ready) in enumerate(((ptlo_done, tlo_ready), (pthi_done, thi_ready))):
                    if not isinstance(U, int) or U >= 1:
                        pe.wait_ge(free, U * 1)
                    for q in range(HT):
                        t = HT * half + q
                        ins = nc.tensor.transpose(banks[:, BANK_T + half, P * q:P * (q + 1)],
                                                  prob[:, u % 2, P * t:P * (t + 1)], ident[:, :])
                    ins.then_inc(ready, 1)

            def values_chunk(g, gpar, par, c):
                if c == 0:
                    pe.wait_ge(ptlo_done, (g + 1) * GROUP)
                    pe.wait_ge(pthi_done, (g + 1) * GROUP)
                    pe.wait_ge(oT_done, g + 1)
                for j in (2 * c, 2 * c + 1):
                    ins = nc.tensor.matmul(obank, hrow[:, par, j, :], pt[:, gpar, j, :], start=(j == 0), stop=(j == T - 1))
                if c == 3:
                    ins.then_inc(av_done, 1)

            def output(k, value, n):
                pe.wait_ge(aux_free, value - 1)
                pe.wait_ge(oT_done, (n + 1) * 2 + 1)
                for q in range(HT):
                    t = HT * k + q
                    ins = nc.tensor.transpose(aux[:, P * q:P * (q + 1)], oT[:, P * t:P * (t + 1)], ident[:, :])
                ins.then_inc(aux_ready, 1)

            def body(bt, par, bk):
                pieces, order = lists(bk)
                U0 = bt * T
                for u in range(T):
                    if u == 0:
                        pe.wait_ge(aux_free, base(bt))
                    scores_unit(U0 + u, u, par)
                    if bk != 0 or u >= 2:
                        transpose_unit(U0 + u - 2, (u - 2) % T)
                    if u < 2 and bk != 0:
                        values_chunk(bt * 2 - 2, 0, 1 - par, u + 2)
                    if 2 <= u < 6 and bk != 0:
                        values_chunk(bt * 2 - 1, 1, 1 - par, u - 2)
                    if u >= 6:
                        values_chunk(bt * 2, 0, par, u - 6)
                    for s in pieces[u]:
                        value = base(bt) + order.index(s) + 1
                        if s in PREP1:
                            prep(s, value, 1 - par, bt + 1)
                        elif s in ("ot0", "ot1"):
                            output(int(s[-1]), value, bt - 1)
                        elif s == "norm":
                            power(s, value, bt * VSTEPS + 4 + 11)
                        else:
                            power(s, value, bt * 3 + 1 + int(s[2]))
                    lower_unit(U0 + u, u)

            batches(pe, body)
            _, order = lists(B - 1)
            end = base(B - 1) + len(order)
            for u in (T - 2, T - 1):
                transpose_unit((B - 1) * T + u, u)
            for c in (2, 3):
                values_chunk(2 * B - 2, 0, (B - 1) % 2, c)
            for c in range(4):
                values_chunk(2 * B - 1, 1, (B - 1) % 2, c)
            for k in range(2):
                output(k, end + k + 1, B - 1)
            power("last", end + 3, B * 3 + 1)
            pe.wait_ge(aux_free, end + 3)
            pe.wait_ge(fin_step, 2 * B + 2)
            nc.tensor.matmul(aux[:, 0:2], ones[:, :], nd[:, :], start=True, stop=True).then_inc(aux_ready, 1)


BESIDE = {
    0: ([], ["ln1_stats"]), 1: ([], ["ln1_relu"]),
    3: (["h1t0"], ["h1t1"]), 4: (["g0"], ["g1"]), 5: ([], ["gsplit"]),
    6: (["or0"], ["or1", "gmid"]), 7: (["ot0"], ["ot1"]), 8: (["wo0"], ["wo1", "ln2_stats"]),
    9: (["ag0a"], []), 10: (["ag0"], ["ln2_apply"]), 11: (["ag1a"], []), 12: (["ag1"], ["lng_stats"]),
    13: (["x2t0"], ["x2t1", "lng_apply"]), 14: (["w10"], ["w11"]), 15: (["w12"], ["w13", "gelu", "lng_relu"]),
    17: (["w20"], ["w21", "ln3_stats"]), 18: (["x1t0"], ["x1t1", "x1b"]),
    19: (["q0"], ["q1", "ln3_apply"]), 20: (["k0"], ["k1"]), 21: (["v0"], ["v1", "stack"]), 23: ([], ["res"]),
}
POST2 = ("or0", "or1", "ot0", "ot1", "wo0", "wo1", "ln2_stats", "ln2_apply", "x2t0", "x2t1", "w10", "w11", "w12", "w13",
         "gelu", "w20", "w21", "ln3_stats", "ln3_apply", "res")
BANKED = ("h1t0", "h1t1", "g0", "g1", "ag0", "ag1", "x1t0", "x1t1", "q0", "q1", "k0", "k1", "v0", "v1",
          "or0", "or1", "ot0", "ot1", "wo0", "wo1", "x2t0", "x2t1", "w10", "w11", "w12", "w13", "w20", "w21")
UNITS = T * H
QT = 2
QN = QT * P
QU = QT * H
AV_AT = (10, 12)
COPY_AT = 13


def block2(nc, x1_dram, Wc, bcv, g1, be1, Wq, Wk, Wv, Wo, bo, g2, be2, W1, b1, W2, b2, g3, be3, out, banks, shared):
    SCALE = float(HD) ** -0.5
    with ExitStack() as ctx:
        sb = lambda n, s, d: ctx.enter_context(nc.sbuf_tensor(n, s, d))
        sem = lambda n: ctx.enter_context(nc.semaphore(n))
        ident, neg_half, adjT, off, two_over_lam = (shared[k] for k in ("ident", "neg_half", "adjT", "off", "two_over_lam"))

        pt = sb("pt2", [P, 2, T, H, QN], F32)
        qs = sb("qs", [P, 2, H, N], BF16)
        k1s = sb("k1s", [P, 2, H, N], BF16)
        k2s = sb("k2s", [P, 2, H, N], BF16)
        vrow = sb("vrow", [P, 2, T, D], F32)
        low = sb("low", [P, 2, N], F32)
        x1b = sb("x1b", [P, 2, T, D], F32)
        h1x = sb("h1x", [P, T, D], F32)
        gf = sb("gf", [P, T, D], F32)
        parts = sb("parts", [P, 6, N], BF16)
        rem = sb("rem", [P, N], F32)
        fT = sb("fT", [P, N], F32)
        oT = sb("oT2", [P, N], F32)
        post = sb("post", [P, T, D], F32)
        wts = {n: sb("w_" + n, [P, D], F32) for n in ("c", "q", "k", "v", "o")}
        w1_sb = sb("w1_sb", [P, HID], F32)
        w2_sb = sb("w2_sb", [P, HC, D], F32)
        b1_col = sb("b1_col", [P, HC], F32)
        vecs = {n: sb("v_" + n, [P, D], F32) for n in ("bc", "g1", "be1", "bo", "g2", "be2", "b2", "g3", "be3")}
        top = sb("top", [P, UNITS], F32)
        ntop = sb("ntop", [P, UNITS], F32)
        den = sb("den2", [P, 2, UNITS], F32)
        rden = sb("rden2", [P, UNITS], F32)
        ln = {}
        for c in ("next", "last"):
            ln[c] = dict(stats=sb("stats_" + c, [P, T, 6], F32), mv=sb("mv_" + c, [P, T, 2], F32),
                         ve=sb("ve_" + c, [P, T], F32), nm=sb("nm_" + c, [P, T], F32), rstd=sb("rstd_" + c, [P, T], F32),
                         nmr=sb("nmr_" + c, [P, T], F32),
                         stats_done=sem("stats_done_" + c), mv_done=sem("mv_done_" + c), ve_done=sem("ve_done_" + c),
                         rstd_done=sem("rstd_done_" + c))

        consts_in = sem("consts_in2")
        x_in = sem("x_in2")
        res_in = sem("res_in")
        stack_in = sem("stack_in")
        out_done = sem("out_done")
        zero_done = sem("zero_done")
        aux_ready = sem("aux_ready2")
        aux_free = sem("aux_free2")
        h1_done = sem("h1_done")
        nmr_done = sem("nmr_done")
        ghi_done = sem("ghi_done")
        grem_done = sem("grem_done")
        gmid_done = sem("gmid_done")
        glo_done = sem("glo_done")
        gb_done = sem("gb_done")
        lng_applied = sem("lng_applied")
        lng_affine = sem("lng_affine")
        x1_done = sem("x1_done")
        x1b_done = sem("x1b_done")
        hi_done = sem("hi_done")
        rem_done = sem("rem_done")
        mid_done = sem("mid_done")
        lo_done = sem("lo_done")
        rden_done = sem("rden_done2")
        ln2_applied = sem("ln2_applied")
        ln2_affine = sem("ln2_affine")
        x2b_done = sem("x2b_done")
        hid_done = sem("hid_done")
        gelu_done = sem("gelu_done")
        ln3_applied = sem("ln3_applied")
        ln3_affine = sem("ln3_affine")
        res_done = sem("res_done")
        s_ready = sem("s_ready2")
        low_done = sem("low_done")
        ntop_done = sem("ntop_done")
        exp_done = sem("exp_done2")
        tlo_ready = sem("tlo_ready2")
        thi_ready = sem("thi_ready2")
        ptlo_done = sem("ptlo_done2")
        pthi_done = sem("pthi_done2")
        av_done = sem("av_done2")
        oT_done = sem("oT_done2")
        held_pool = sem("held_pool2")
        held_dve = sem("held_dve2")
        held_pe = sem("held_pe2")
        held_sp = sem("held_sp2")

        aux = banks[:, BANK_AUX, :]
        auxr = aux.rearrange("p (t d) -> p t d", t=HT)
        obank = banks[:, BANK_O, 0:QN]
        scores = [banks[:, 2 * k:2 * k + 2, :].rearrange("p a n -> p (a n)") for k in range(2)]
        hidT = parts[:, :, :].rearrange("p a n -> p (a n)")[:, 0:2 * HC * N].bitcast(F32)
        flat = lambda a: a.rearrange("p t d -> p (t d)")
        rows_b = lambda n, t=T: vecs[n][:, :].rearrange("p (o d) -> p o d", o=1).to_broadcast([P, t, D])
        gparts = [parts[:, k, :].rearrange("p (t d) -> p t d", t=T) for k in range(3)]
        NV = 5 + 2 + HC + 9
        STACKED = 16 * 11 * H
        PER = len(BANKED)
        PREP = [s for u in sorted(BESIDE) for half in BESIDE[u] for s in half if s not in POST2]
        POST = [s for u in sorted(BESIDE) for half in BESIDE[u] for s in half if s in POST2]

        def beside(bk):
            keep = lambda s: not (bk == 0 and s in POST2) and not (bk == B - 1 and s not in POST2)
            table = {u: [[s for s in half if keep(s)] for half in BESIDE.get(u, ([], []))] for u in range(UNITS)}
            order = [s for u in range(UNITS) for half in table[u] for s in half if s in BANKED]
            return table, order

        def base(bt):
            return PER // 2 if isinstance(bt, int) and bt == 0 else bt * PER

        def batches(eng, body):
            body(0, 0, 0)
            with eng.Fori(0, (B - 2) // 2) as i:
                for k in (1, 2):
                    body(i * 2 + k, k % 2, None)
            body(B - 1, (B - 1) % 2, B - 1)

        def late(bt, u, lag):
            return (bt, u - lag) if u >= lag else (bt - 1, u - lag + UNITS)

        def quarters(u, at):
            for q in range(T // QT):
                for ago in (0, 1):
                    if q * QU + at == u + ago * UNITS:
                        return q, ago
            return None

        block = ctx.enter_context(nc.Block())

        @block.sync
        def _(sp):
            def hold(s, value):
                sp.wait_ge(s, value)
                sp.sem_inc(held_sp, 1)

            sp.sem_inc(out_done, 16)
            for n, src in (("c", Wc), ("q", Wq), ("k", Wk), ("v", Wv), ("o", Wo)):
                sp.dma_start(wts[n][:, :], src).then_inc(consts_in, 16)
            sp.dma_start(w1_sb[:, :], W1).then_inc(consts_in, 16)
            sp.dma_start(w2_sb[:, :, :], W2.rearrange("(c p) d -> p c d", p=P)).then_inc(consts_in, 16)
            for c in range(HC):
                sp.dma_start(b1_col[:, c:c + 1], b1[P * c:P * (c + 1)].rearrange("(p o) -> p o", o=1)).then_inc(consts_in, 16)
            for n, src in (("bc", bcv), ("g1", g1), ("be1", be1), ("bo", bo), ("g2", g2), ("be2", be2), ("b2", b2),
                           ("g3", g3), ("be3", be3)):
                sp.dma_start(vecs[n][:, :], across(src)).then_inc(consts_in, 16)

            def one(dram, n):
                return rows(dram[n] if isinstance(n, int) else dram[bass.ds(n, 1)].rearrange("o n d -> (o n) d"))

            def step(s, n, par):
                if s == "ln1_stats":
                    if not isinstance(n, int) or n > 0:
                        hold(x1b_done, n * 1)
                    sp.dma_start(h1x[:, :, :], one(x1_dram, n)).then_inc(x_in, 16)
                if s == "stack":
                    hold(lo_done, n * 2 + 2)
                    if not isinstance(n, int) or n >= 2:
                        hold(s_ready, (n - 1) * UNITS)
                    for h in range(H):
                        rows_h = slice(HD * h, HD * (h + 1))
                        for dst, first, slots in ((qs, 0, (0, 0, 1, 2)), (k1s, 3, (0, 2, 0, 0)), (k2s, 3, (1, None, 1, 1))):
                            for at, part in enumerate(slots):
                                if part is not None:
                                    sp.dma_start(dst[HD * at:HD * (at + 1), par, h, :], parts[rows_h, first + part, :])\
                                        .then_inc(stack_in, 16)

            def post_step(s, n):
                if s == "ln3_stats":
                    hold(x1_done, n + 3 if not isinstance(n, int) or n < B - 2 else B)
                    if isinstance(n, int) and n == B - 1:
                        hold(res_done, n + 1)
                    sp.dma_start(gf[:, :, :], one(x1_dram, n)).then_inc(res_in, 16)
                if s == "res":
                    hold(res_done, n + 2)
                    sp.dma_start(one(out, n), post[:, :, :]).then_inc(out_done, 16)

            for s in PREP:
                step(s, 0, 0)

            def body(bt, par, bk):
                table, order = beside(bk)
                for u in range(UNITS):
                    for s in table[u][0] + table[u][1]:
                        step(s, bt + 1, 1 - par) if s not in POST2 else post_step(s, bt - 1)

            batches(sp, body)
            for s in POST:
                post_step(s, B - 1)
            sp.wait_ge(out_done, 16 * (B + 1))

        @block.gpsimd
        def _(pool):
            def hold(s, value):
                pool.wait_ge(s, value)
                pool.sem_inc(held_pool, 1)

            pool.sem_inc(res_done, 1)
            for par in range(2):
                nc.gpsimd.memset(k2s[HD:2 * HD, par], 0.0).then_inc(zero_done, 1)
            pool.wait_ge(zero_done, 2)
            pool.wait_ge(consts_in, 16 * NV)

            def scale(c, n, k):
                L = ln[c]
                i = n * 2 + k
                hold(L["mv_done"], i + 1)
                if c == "next" and k == 1:
                    hold(h1_done, n * 1 + 1)
                nc.gpsimd.tensor_scalar(L["ve"][:, :], L["mv"][:, :, 1], 1.0, EPS, ALU.mult, ALU.add).then_inc(L["ve_done"], 1)
                nc.gpsimd.tensor_scalar(L["nm"][:, :], L["mv"][:, :, 0], -1.0, 0.0, ALU.mult, ALU.add).then_inc(L["ve_done"], 1)
                hold(L["ve_done"], i * 2 + 2)
                nc.gpsimd.tensor_tensor(L["rstd"][:, :], L["ve"][:, :], neg_half[:, :], ALU.pow).then_inc(L["rstd_done"], 1)

            def step(s, n, par):
                if s == "ln1_stats":
                    scale("next", n, 0)
                    L = ln["next"]
                    hold(L["rstd_done"], n * 2 + 1)
                    nc.gpsimd.tensor_tensor(L["nmr"][:, :], L["nm"][:, :], L["rstd"][:, :], ALU.mult).then_inc(nmr_done, 1)
                if s == "gsplit":
                    hold(ghi_done, n * 1 + 1)
                    if not isinstance(n, int) or n > 0:
                        hold(lo_done, n * 2)
                    nc.gpsimd.tensor_tensor(rem[:, :], flat(gf[:, :, :]), parts[:, 0, :], ALU.subtract).then_inc(grem_done, 1)
                    hold(grem_done, n * 1 + 1)
                    nc.gpsimd.tensor_tensor(gf[:, :, :], gf[:, :, :], rows_b("bc"), ALU.subtract).then_inc(gb_done, 1)
                if s == "gmid":
                    hold(gmid_done, n * 1 + 1)
                    nc.gpsimd.tensor_tensor(parts[:, 2, :], rem[:, :], parts[:, 1, :], ALU.subtract).then_inc(glo_done, 1)
                if s == "lng_stats":
                    scale("next", n, 1)
                if s == "lng_apply":
                    hold(lng_applied, n * 1 + 1)
                    nc.gpsimd.tensor_tensor(gf[:, :, :], gf[:, :, :], rows_b("g1"), ALU.mult).then_inc(lng_affine, 1)
                    hold(lng_affine, n * 2 + 1)
                    nc.gpsimd.tensor_tensor(gf[:, :, :], gf[:, :, :], rows_b("be1"), ALU.add).then_inc(lng_affine, 1)
                if s == "x1b":
                    hold(x1_done, n * 1 + 1)
                    nc.gpsimd.tensor_tensor(x1b[:, par], h1x[:, :, :], rows_b("bo"), ALU.add).then_inc(x1b_done, 1)
                if s in ("q1", "k1"):
                    k = "qk".index(s[0])
                    at = 3 * k
                    hold(rem_done, n * 4 + 2 * k + 2)
                    nc.gpsimd.tensor_scalar(parts[:, at + 1, :], rem[:, :], 1.0, 0.0, ALU.mult, ALU.add).then_inc(mid_done, 1)
                    hold(mid_done, n * 2 + k + 1)
                    nc.gpsimd.tensor_tensor(parts[:, at + 2, :], rem[:, :], parts[:, at + 1, :], ALU.subtract)\
                        .then_inc(lo_done, 1)

            def post_step(s, n):
                if s == "ln2_stats":
                    scale("last", n, 0)
                if s == "ln2_apply":
                    hold(ln2_applied, n * 1 + 1)
                    nc.gpsimd.tensor_tensor(post[:, :, :], post[:, :, :], rows_b("g2"), ALU.mult).then_inc(ln2_affine, 1)
                    hold(ln2_affine, n * 2 + 1)
                    nc.gpsimd.tensor_tensor(post[:, :, :], post[:, :, :], rows_b("be2"), ALU.add).then_inc(ln2_affine, 1)
                if s == "w11":
                    hold(hid_done, n * 4 + 1)
                    nc.gpsimd.tensor_tensor(post[:, :, :], post[:, :, :], rows_b("b2"), ALU.add).then_inc(x2b_done, 1)
                if s == "ln3_stats":
                    scale("last", n, 1)
                if s == "ln3_apply":
                    hold(ln3_applied, n * 1 + 1)
                    nc.gpsimd.tensor_tensor(post[:, :, :], post[:, :, :], rows_b("g3"), ALU.mult).then_inc(ln3_affine, 1)
                    hold(ln3_affine, n * 2 + 1)
                    nc.gpsimd.tensor_tensor(post[:, :, :], post[:, :, :], rows_b("be3"), ALU.add).then_inc(ln3_affine, 1)
                    hold(ln3_affine, n * 2 + 2)
                    hold(res_in, n * 16 + 16)
                    nc.gpsimd.tensor_tensor(post[:, :, :], post[:, :, :], gf[:, :, :], ALU.add).then_inc(res_done, 1)

            for s in PREP:
                step(s, 0, 0)

            def body(bt, par, bk):
                table, order = beside(bk)
                for u in range(UNITS):
                    for s in table[u][0] + table[u][1]:
                        step(s, bt + 1, 1 - par) if s not in POST2 else post_step(s, bt - 1)

            batches(pool, body)
            for s in POST:
                post_step(s, B - 1)

        @block.scalar
        def _(act):
            def step(s, n, par, value):
                k = int(s[-1]) if s in BANKED else 0
                cols = slice(HALF * k, HALF * (k + 1))
                tiles = slice(HT * k, HT * (k + 1))
                if s == "ln1_relu":
                    act.wait_ge(nmr_done, n * 1 + 1)
                    L = ln["next"]
                    for t in range(T):
                        ins = nc.scalar.activation(h1x[:, t, :], h1x[:, t, :], ACT.Relu, bias=L["nmr"][:, t:t + 1],
                                                   scale=L["rstd"][:, t:t + 1])
                    ins.then_inc(h1_done, 1)
                if s in ("h1t0", "h1t1", "x1t0", "x1t1"):
                    act.wait_ge(aux_ready, value)
                    nc.scalar.activation(fT[:, cols], aux, ACT.Copy).then_inc(aux_free, 1)
                if s in ("g0", "g1"):
                    act.wait_ge(aux_ready, value)
                    if (not isinstance(n, int) or n >= 2) and k == 0:
                        act.wait_ge(res_done, n - 1)
                    nc.scalar.activation(gf[:, tiles, :], auxr, ACT.Copy).then_inc(aux_free, 1)
                if s in ("q0", "q1", "k0", "k1"):
                    act.wait_ge(aux_ready, value)
                    nc.scalar.activation(parts[:, 3 * "qk".index(s[0]), cols], aux, ACT.Copy).then_inc(hi_done, 1)
                if s in ("v0", "v1"):
                    act.wait_ge(aux_ready, value)
                    nc.scalar.activation(vrow[:, par, tiles, :], auxr, ACT.Copy).then_inc(aux_free, 1)

            def post_step(s, n, value):
                k = int(s[-1]) if s in BANKED else 0
                if s in ("ot0", "ot1", "x2t0", "x2t1"):
                    act.wait_ge(aux_ready, value)
                    nc.scalar.activation(fT[:, HALF * k:HALF * (k + 1)], aux, ACT.Copy).then_inc(aux_free, 1)
                if s in ("w10", "w11", "w12", "w13"):
                    act.wait_ge(aux_ready, value)
                    nc.scalar.activation(hidT[:, HALF * k:HALF * (k + 1)], aux, ACT.Identity, bias=b1_col[:, k // 2:k // 2 + 1])\
                        .then_inc(hid_done, 1)
                    act.wait_ge(hid_done, n * 4 + k + 1)
                    act.sem_inc(aux_free, 1)
                if s == "gelu":
                    act.wait_ge(hid_done, n * 4 + 4)
                    nc.scalar.activation(hidT, hidT, ACT.Gelu).then_inc(gelu_done, 1)

            def exp_unit(bt, u, par):
                U = bt * UNITS + u
                act.wait_ge(ntop_done, U + 1)
                nc.scalar.activation(low[:, u % 2, :], low[:, u % 2, :], ACT.Exp, bias=ntop[:, u:u + 1], scale=SCALE,
                                     accum_out=den[:, par, u:u + 1]).then_inc(exp_done, 1)

            def evac_hi(bt, u):
                q, i, h = u // QU, u % QU // H, u % H
                act.wait_ge(thi_ready, bt * UNITS + u + 1)
                g = bt * (T // QT) + q
                if u % QU == 0 and (not isinstance(g, int) or g >= 2):
                    act.wait_ge(av_done, g - 1)
                nc.scalar.activation(pt[:, q % 2, HT:T, h, P * i:P * (i + 1)],
                                     banks[:, BANK_T + 1, :].rearrange("p (t n) -> p t n", t=HT), ACT.Copy)\
                    .then_inc(pthi_done, 1)

            def copy_out(bt, q, value):
                act.wait_ge(av_done, bt * (T // QT) + q + 1)
                if value is not None:
                    act.wait_ge(aux_ready, value)
                nc.scalar.activation(oT[:, QN * q:QN * (q + 1)], obank, ACT.Copy).then_inc(oT_done, 1)

            act.wait_ge(consts_in, 16 * NV)
            value = 0
            for s in PREP:
                value += s in BANKED
                step(s, 0, 0, value)

            def body(bt, par, bk):
                table, order = beside(bk)

                def aside(half, u):
                    for s in table[u][half]:
                        value = base(bt) + order.index(s) + 1 if s in BANKED else None
                        step(s, bt + 1, 1 - par, value) if s not in POST2 else post_step(s, bt - 1, value)

                for u in range(UNITS):
                    if bk != 0 or u >= 1:
                        exp_unit(*late(bt, u, 1), par if u >= 1 else 1 - par)
                    aside(0, u)
                    if bk != 0 or u >= 2:
                        evac_hi(*late(bt, u, 2))
                    found = quarters(u, COPY_AT)
                    if found and not (found[1] and bk == 0):
                        q, ago = found
                        copy_out(bt - ago, q, base(bt) + order.index("or1") + 1 if q == 0 and bk != 0 else None)
                    aside(1, u)

            batches(act, body)
            exp_unit(B - 1, UNITS - 1, (B - 1) % 2)
            for u in (UNITS - 2, UNITS - 1):
                evac_hi(B - 1, u)
            copy_out(B - 1, T // QT - 1, None)
            value = base(B - 1) + PER // 2
            for s in POST:
                value += s in BANKED
                post_step(s, B - 1, value)

        @block.vector
        def _(dve):
            def hold(s, value):
                dve.wait_ge(s, value)
                dve.sem_inc(held_dve, 1)

            dve.wait_ge(consts_in, 16 * NV)

            def statistics(c, n, k, src):
                L = ln[c]
                i = n * 2 + k
                if c == "next" and k == 1:
                    dve.wait_ge(L["rstd_done"], i)
                for t in range(T):
                    ins = nc.vector.bn_stats(L["stats"][:, t, :], src[:, t, :])
                ins.then_inc(L["stats_done"], 1)
                hold(L["stats_done"], i + 1)
                for t in range(T):
                    ins = nc.vector.bn_aggr(L["mv"][:, t, :], L["stats"][:, t, :])
                ins.then_inc(L["mv_done"], 1)

            def apply(c, n, k, rows_, done):
                L = ln[c]
                dve.wait_ge(L["rstd_done"], n * 2 + k + 1)
                for t in range(T):
                    ins = nc.vector.tensor_scalar(rows_[:, t, :], rows_[:, t, :], L["nm"][:, t:t + 1], L["rstd"][:, t:t + 1],
                                                  ALU.add, ALU.mult)
                ins.then_inc(done, 1)

            def step(s, n, value):
                k = int(s[-1]) if s in BANKED else 0
                cols = slice(HALF * k, HALF * (k + 1))
                tiles = slice(HT * k, HT * (k + 1))
                if s == "ln1_stats":
                    dve.wait_ge(x_in, n * 16 + 16)
                    statistics("next", n, 0, h1x)
                if s == "gsplit":
                    dve.wait_ge(aux_free, value)
                    if not isinstance(n, int) or n > 0:
                        dve.wait_ge(stack_in, n * STACKED)
                    nc.vector.tensor_copy(parts[:, 0, :], flat(gf[:, :, :])).then_inc(ghi_done, 1)
                if s == "gmid":
                    dve.wait_ge(grem_done, n * 1 + 1)
                    nc.vector.tensor_copy(parts[:, 1, :], rem[:, :]).then_inc(gmid_done, 1)
                if s in ("ag0", "ag1"):
                    dve.wait_ge(aux_ready, value)
                    dve.wait_ge(gb_done, n * 1 + 1)
                    nc.vector.scalar_tensor_tensor(out=flat(gf[:, tiles, :]), in0=aux, scalar=two_over_lam[:, 0:1],
                                                   in1=flat(gf[:, tiles, :]), op0=ALU.mult, op1=ALU.subtract)\
                        .then_inc(aux_free, 1)
                if s == "lng_stats":
                    dve.wait_ge(aux_free, value)
                    statistics("next", n, 1, gf)
                if s == "lng_apply":
                    apply("next", n, 1, gf, lng_applied)
                if s == "lng_relu":
                    dve.wait_ge(lng_affine, n * 2 + 2)
                    nc.vector.scalar_tensor_tensor(out=flat(h1x[:, :, :]), in0=flat(gf[:, :, :]), scalar=0.0,
                                                   in1=flat(h1x[:, :, :]), op0=ALU.max, op1=ALU.add).then_inc(x1_done, 1)
                if s in ("q0", "q1", "k0", "k1"):
                    q = "qk".index(s[0])
                    dve.wait_ge(hi_done, n * 4 + 2 * q + k + 1)
                    if q:
                        dve.wait_ge(lo_done, n * 2 + 1)
                    nc.vector.tensor_tensor(rem[:, cols], aux, parts[:, 3 * q, cols], ALU.subtract).then_inc(rem_done, 1)
                    dve.wait_ge(rem_done, n * 4 + 2 * q + k + 1)
                    dve.sem_inc(aux_free, 1)

            def post_step(s, n, value, par):
                k = int(s[-1]) if s in BANKED else 0
                tiles = slice(HT * k, HT * (k + 1))
                if s == "or0":
                    dve.wait_ge(exp_done, (n + 1) * UNITS)
                    nc.vector.reciprocal(rden[:, :], den[:, par, :]).then_inc(rden_done, 1)
                    dve.wait_ge(rden_done, n * 1 + 1)
                    dve.wait_ge(out_done, n * 16 + 16)
                if s in ("or0", "or1"):
                    dve.wait_ge(aux_ready, value)
                    by_head = lambda a: a.rearrange("p (g d) -> p g d", d=HD)
                    nc.vector.tensor_tensor(by_head(flat(post[:, tiles, :])), by_head(aux),
                                            bc(rden[:, HT * H * k:HT * H * (k + 1)], HD), ALU.mult).then_inc(aux_free, 1)
                if s in ("wo0", "wo1"):
                    dve.wait_ge(aux_ready, value)
                    dve.wait_ge(x1b_done, n * 1 + 1)
                    nc.vector.tensor_tensor(flat(post[:, tiles, :]), aux, flat(x1b[:, par, tiles, :]), ALU.add)\
                        .then_inc(aux_free, 1)
                if s == "ln2_stats":
                    dve.wait_ge(aux_free, value)
                    statistics("last", n, 0, post)
                if s == "ln2_apply":
                    apply("last", n, 0, post, ln2_applied)
                if s in ("w20", "w21"):
                    dve.wait_ge(aux_ready, value)
                    dve.wait_ge(x2b_done, n * 1 + 1)
                    nc.vector.tensor_tensor(flat(post[:, tiles, :]), aux, flat(post[:, tiles, :]), ALU.add)\
                        .then_inc(aux_free, 1)
                if s == "ln3_stats":
                    dve.wait_ge(aux_free, value)
                    statistics("last", n, 1, post)
                if s == "ln3_apply":
                    apply("last", n, 1, post, ln3_applied)

            def low_unit(bt, u):
                U = bt * UNITS + u
                hold(s_ready, U + 1)
                if not isinstance(U, int) or U >= 2:
                    hold(thi_ready, U - 1)
                nc.vector.tensor_tensor_reduce(low[:, u % 2, :], scores[u % 2], off[:, u // H, :], 1.0, -3.0e38, ALU.add,
                                               ALU.max, top[:, u:u + 1]).then_inc(low_done, 1)

            def evac_lo(bt, u):
                q, i, h = u // QU, u % QU // H, u % H
                dve.wait_ge(tlo_ready, bt * UNITS + u + 1)
                g = bt * (T // QT) + q
                if u % QU == 0 and (not isinstance(g, int) or g >= 2):
                    dve.wait_ge(av_done, g - 1)
                nc.vector.tensor_copy(pt[:, q % 2, 0:HT, h, P * i:P * (i + 1)],
                                      banks[:, BANK_T, :].rearrange("p (t n) -> p t n", t=HT)).then_inc(ptlo_done, 1)

            def bias_unit(bt, u):
                dve.wait_ge(low_done, bt * UNITS + u + 1)
                nc.vector.tensor_scalar(ntop[:, u:u + 1], top[:, u:u + 1], -SCALE, None, ALU.mult).then_inc(ntop_done, 1)

            value = 0
            for s in PREP:
                value += s in BANKED
                step(s, 0, value)

            def body(bt, par, bk):
                table, order = beside(bk)
                seen = [base(bt)]

                def aside(half, u):
                    for s in table[u][half]:
                        if s in BANKED:
                            seen[0] = base(bt) + order.index(s) + 1
                        step(s, bt + 1, seen[0]) if s not in POST2 else post_step(s, bt - 1, seen[0], 1 - par)

                for u in range(UNITS):
                    aside(0, u)
                    low_unit(bt, u)
                    if bk != 0 or u >= 2:
                        evac_lo(*late(bt, u, 2))
                    bias_unit(bt, u)
                    aside(1, u)

            batches(dve, body)
            for u in (UNITS - 2, UNITS - 1):
                evac_lo(B - 1, u)
            value = base(B - 1) + PER // 2
            for s in POST:
                value += s in BANKED
                post_step(s, B - 1, value, (B - 1) % 2)

        @block.tensor
        def _(pe):
            pe.wait_ge(consts_in, 16 * NV)

            def turn(src, k, nodes_in_rows):
                for q in range(HT):
                    t = HT * k + q
                    tile = src[:, t, :] if nodes_in_rows else src[:, P * t:P * (t + 1)]
                    ins = nc.tensor.transpose(aux[:, P * q:P * (q + 1)], tile, ident[:, :])
                return ins

            def times(w, k):
                for q in range(HT):
                    t = HT * k + q
                    ins = nc.tensor.matmul(aux[:, P * q:P * (q + 1)], fT[:, P * t:P * (t + 1)], w, start=True, stop=True)
                return ins

            def bank_free(value):
                if not isinstance(value, int) or value > 1:
                    pe.wait_ge(aux_free, value - 1)

            def convolve(t):
                q = t % HT
                for j in range(T):
                    for part in range(3):
                        ins = nc.tensor.matmul(aux[:, P * q:P * (q + 1)], adjT[:, j, P * t:P * (t + 1)], gparts[part][:, j, :],
                                               start=(j == 0 and part == 0), stop=(j == T - 1 and part == 2))
                return ins

            def step(s, n, par, value):
                k = int(s[-1]) if s in BANKED else 0
                if s in BANKED and s not in ("ag0", "ag1"):
                    bank_free(value)
                if s in ("ag0a", "ag1a"):
                    bank_free(value + 1)
                    if s == "ag0a":
                        pe.wait_ge(glo_done, n * 1 + 1)
                    pe.sem_inc(held_pe, 1)
                    k = int(s[2])
                    for t in (HT * k, HT * k + 1):
                        convolve(t)
                if s in ("ag0", "ag1"):
                    for t in (HT * k + 2, HT * k + 3):
                        ins = convolve(t)
                if s in ("h1t0", "h1t1"):
                    if k == 0:
                        pe.wait_ge(h1_done, n * 1 + 1)
                    ins = turn(h1x, k, True)
                if s in ("g0", "g1"):
                    ins = times(wts["c"][:, :], k)
                if s in ("x1t0", "x1t1"):
                    if k == 0:
                        pe.wait_ge(x1_done, n * 1 + 1)
                    ins = turn(h1x, k, True)
                if s in ("q0", "q1", "k0", "k1"):
                    ins = nc.tensor.matmul(aux, wts[s[0]][:, :], fT[:, HALF * k:HALF * (k + 1)], start=True, stop=True)
                if s in ("v0", "v1"):
                    ins = times(wts["v"][:, :], k)
                if s in BANKED:
                    ins.then_inc(aux_ready, 1)

            def post_step(s, n, value):
                if s not in BANKED:
                    return
                k = int(s[-1])
                bank_free(value)
                if s in ("or0", "or1"):
                    if k == 0:
                        pe.wait_ge(oT_done, (n + 1) * (T // QT))
                    ins = turn(oT, k, False)
                if s in ("ot0", "ot1"):
                    ins = turn(post, k, True)
                if s in ("wo0", "wo1"):
                    ins = times(wts["o"][:, :], k)
                if s in ("x2t0", "x2t1"):
                    if k == 0:
                        pe.wait_ge(ln2_affine, n * 2 + 2)
                    ins = turn(post, k, True)
                if s in ("w10", "w11", "w12", "w13"):
                    c, half = k // 2, k % 2
                    ins = nc.tensor.matmul(aux, w1_sb[:, P * c:P * (c + 1)], fT[:, HALF * half:HALF * (half + 1)],
                                           start=True, stop=True)
                if s in ("w20", "w21"):
                    if k == 0:
                        pe.wait_ge(gelu_done, n * 1 + 1)
                    for q in range(HT):
                        t = HT * k + q
                        for c in range(HC):
                            ins = nc.tensor.matmul(aux[:, P * q:P * (q + 1)], hidT[:, N * c + P * t:N * c + P * (t + 1)],
                                                   w2_sb[:, c, :], start=(c == 0), stop=(c == HC - 1))
                ins.then_inc(aux_ready, 1)

            def scores_unit(bt, u, par):
                U = bt * UNITS + u
                i, h = u // H, u % H
                if not isinstance(U, int) or U >= 2:
                    pe.wait_ge(low_done, U - 1)
                for stack, first in ((k1s, True), (k2s, False)):
                    for k in range(2):
                        ins = nc.tensor.matmul(scores[u % 2][:, HALF * k:HALF * (k + 1)], qs[:, par, h, P * i:P * (i + 1)],
                                               stack[:, par, h, HALF * k:HALF * (k + 1)], start=first, stop=not first)
                ins.then_inc(s_ready, 1)

            def transpose_unit(bt, u):
                U = bt * UNITS + u
                pe.wait_ge(exp_done, U + 1)
                for half, (free, ready) in enumerate(((ptlo_done, tlo_ready), (pthi_done, thi_ready))):
                    if not isinstance(U, int) or U >= 1:
                        pe.wait_ge(free, U * 1)
                    for q in range(HT):
                        t = HT * half + q
                        ins = nc.tensor.transpose(banks[:, BANK_T + half, P * q:P * (q + 1)],
                                                  low[:, u % 2, P * t:P * (t + 1)], ident[:, :])
                    ins.then_inc(ready, 1)

            def values_half(bt, q, par, half):
                g = bt * (T // QT) + q
                if half == 0:
                    pe.wait_ge(ptlo_done, bt * UNITS + (q + 1) * QU)
                    pe.wait_ge(pthi_done, bt * UNITS + (q + 1) * QU)
                    if not isinstance(g, int) or g >= 1:
                        pe.wait_ge(oT_done, g * 1)
                for j in range(HT * half, HT * (half + 1)):
                    for h in range(H):
                        ins = nc.tensor.matmul(banks[HD * h:HD * (h + 1), BANK_O, 0:QN], vrow[:, par, j, HD * h:HD * (h + 1)],
                                               pt[:, q % 2, j, h, :], start=(j == 0), stop=(j == T - 1),
                                               tile_position=(0, HD * h))
                if half == 1:
                    ins.then_inc(av_done, 1)

            pe.wait_ge(zero_done, 2)
            value = 0
            for s in PREP:
                value += s in BANKED
                step(s, 0, 0, value)

            def body(bt, par, bk):
                table, order = beside(bk)

                def aside(half, u):
                    for s in table[u][half]:
                        if s in BANKED or s in ("ag0a", "ag1a"):
                            value = base(bt) + order.index(s) + 1 if s in BANKED else base(bt) + order.index(s[:3])
                            step(s, bt + 1, 1 - par, value) if s not in POST2 else post_step(s, bt - 1, value)

                for u in range(UNITS):
                    if u == 0:
                        pe.wait_ge(stack_in, (bt + 1) * STACKED)
                        pe.wait_ge(aux_free, base(bt))
                    scores_unit(bt, u, par)
                    aside(0, u)
                    if bk != 0 or u >= 2:
                        transpose_unit(*late(bt, u, 2))
                    for half, at in enumerate(AV_AT):
                        found = quarters(u, at)
                        if found and not (found[1] and bk == 0):
                            q, ago = found
                            values_half(bt - ago, q, par if ago == 0 else 1 - par, half)
                    aside(1, u)

            batches(pe, body)
            for u in (UNITS - 2, UNITS - 1):
                transpose_unit(B - 1, u)
            for half in range(2):
                values_half(B - 1, T // QT - 1, (B - 1) % 2, half)
            value = base(B - 1) + PER // 2
            for s in POST:
                value += s in BANKED
                post_step(s, B - 1, value)


_INS = ["x", "adj", "L0_gnn_W", "L0_gnn_b_lin", "L0_gnn_b", "L1_gnn_Wc", "L1_gnn_bc", "L1_gnn_g1", "L1_gnn_be1", "L1_gnn_Wq",
        "L1_gnn_Wk", "L1_gnn_Wv", "L1_gnn_Wo", "L1_gnn_bo", "L1_gnn_g2", "L1_gnn_be2", "L1_gnn_W1", "L1_gnn_b1", "L1_gnn_W2",
        "L1_gnn_b2", "L1_gnn_g3", "L1_gnn_be3"]


def kernel(**inputs):
    import numpy as _np
    import concourse.bacc as _bacc
    from concourse import mybir as _mybir
    from concourse.bass_utils import run_bass_kernel_spmd as _run

    nc = _bacc.Bacc("TRN2", target_bir_lowering=False, num_devices=1)
    arrays, args = {}, []
    for name in _INS:
        a = _np.ascontiguousarray(inputs[name])
        arrays[f"in_{name}"] = a
        args.append(nc.dram_tensor(f"in_{name}", a.shape, _mybir.dt.from_np(a.dtype), kind="ExternalInput").ap())
    out = nc.dram_tensor("out_x", (B, N, D), F32, kind="ExternalOutput").ap()
    build(nc, *args, out)
    r = _run(nc, [arrays], core_ids=[0])
    return r.results[0]["out_x"]
```

```python
from contextlib import ExitStack

import concourse.bass as bass
from concourse import mybir

F32 = mybir.dt.float32
BF16 = mybir.dt.bfloat16
FP8 = mybir.dt.float8e4
ALU = mybir.AluOpType
ACT = mybir.ActivationFunctionType
AX = mybir.AxisListType

P = 128
B, N, D, H = 8, 1024, 128, 4
T = N // P
HALF = N // 2
HT = T // 2
HD = D // H
HID = 2 * D
HC = HID // P
EPS = 1e-5
FAR = 2.0 ** 100
TINY = 1e-30
GROUP = 4

BANK_T, BANK_O, BANK_AUX = 4, 6, 7

AUX1 = {0: ([], ["pw0"]), 2: ([], ["ot0"]), 3: ([], ["pw1"]), 4: (["h0T0"], ["h0T1"]), 5: (["hT0"], ["hT1"]),
        6: (["hrow0"], ["norm"]), 7: (["ot1"], ["hrow1"])}
LN_AT = (0, 1)
RELU_AT = (2, 3)
PREP1 = ["h0T0", "h0T1", "hT0", "hT1", "hrow0", "hrow1"]


def aux_list(table, first, last, prep, post):
    return [s for u in sorted(table) for half in table[u] for s in half
            if not (last and s in prep) and not (first and s in post)]


def bc(ap, n):
    return ap.rearrange("p (k o) -> p k o", o=1).to_broadcast([ap.shape[0], ap.shape[1], n])


def build(nc, x, adj, W, b_lin, b, Wc, bcv, g1, be1, Wq, Wk, Wv, Wo, bo, g2, be2, W1, b1, W2, b2, g3, be3, out):
    x1_dram = nc.dram_tensor("after_block1", (B, N, D), F32, kind="Internal").ap()
    with ExitStack() as ctx:
        sb = lambda n, s, d: ctx.enter_context(nc.sbuf_tensor(n, s, d))
        banks = ctx.enter_context(nc.psum_tensor("banks", [P, 8, HALF], F32))
        shared = {
            "ident": sb("ident", [P, P], F32),
            "neg_half": sb("neg_half", [P, T], F32),
            "adjT": sb("adjT", [P, T, N], FP8),
            "off": sb("off", [P, T, N], BF16),
            "two_over_lam": sb("two_over_lam", [P, 1], F32),
        }
        block1(nc, x, adj, W, b_lin, b, x1_dram, banks, shared)
        block2(nc, x1_dram, Wc, bcv, g1, be1, Wq, Wk, Wv, Wo, bo, g2, be2, W1, b1, W2, b2, g3, be3, out, banks, shared)


def arrivals(bt, par):
    return (bt // 2 + 1 if isinstance(bt, int) else (bt - par) // 2 + 1) * 16


def rows(ap):
    return ap.rearrange("(t p) d -> p t d", p=P)


def across(vec):
    return vec.rearrange("(o n) -> o n", o=1).to_broadcast([P, vec.shape[0]])


def block1(nc, x, adj, W, b_lin, b, x1_dram, banks, shared):
    with ExitStack() as ctx:
        sb = lambda n, s, d: ctx.enter_context(nc.sbuf_tensor(n, s, d))
        sem = lambda n: ctx.enter_context(nc.semaphore(n))
        ident, neg_half, adjT, off, two_over_lam = (shared[k] for k in (
            "ident", "neg_half", "adjT", "off", "two_over_lam"))

        adj_f = sb("adj_f", [P, T, N], F32)
        pt = sb("pt", [P, 2, T, HALF], F32)
        sym = sb("sym", [P, T, N], BF16)
        ones = sb("ones", [P, P], F32)
        identb = sb("identb", [P, P], BF16)
        far_diag = sb("far_diag", [P, P], BF16)
        w_sb = sb("w_sb", [P, D], F32)
        blin_col = sb("blin_col", [P, 1], F32)
        b_row = sb("b_row", [P, D], F32)
        xin = sb("xin", [P, 2, T, D], F32)
        xb = sb("xb", [P, 2, T, D], F32)
        xn = sb("xn", [P, T, D], F32)
        h0 = sb("h0", [P, T, D], F32)
        h0T = sb("h0T", [P, N], F32)
        hT = sb("hT", [P, 2, N], F32)
        hrow = sb("hrow", [P, 2, T, D], F32)
        z = sb("z", [P, 2, N], BF16)
        prob = sb("prob", [P, 2, N], F32)
        nmax = sb("nmax", [P, T], F32)
        den = sb("den", [P, 2, T], F32)
        rden = sb("rden", [P, T], F32)
        oT = sb("oT", [P, N], F32)
        stats = sb("stats", [P, T, 6], F32)
        mv = sb("mv", [P, T, 2], F32)
        ve = sb("ve", [P, T], F32)
        rstd = sb("rstd", [P, T], F32)
        nm = sb("nm", [P, T], F32)
        nmr = sb("nmr", [P, T], F32)
        v = sb("v", [P, T], F32)
        vsum = sb("vsum", [P, T], F32)
        y = sb("y", [P, T], F32)
        vr1 = sb("vr1", [P, T], F32)
        vr2 = sb("vr2", [P, T], F32)
        vp = sb("vp", [P, T, 3], BF16)
        tot = sb("tot", [P, 1], F32)
        tot2 = sb("tot2", [P, 1], F32)
        rtot = sb("rtot", [P, 1], F32)
        junk = sb("junk", [P, T], F32)
        junk2 = sb("junk2", [P, T], F32)
        nd = sb("nd", [P, 2], F32)
        fin = sb("fin", [P, 6], F32)

        consts_in = sem("consts_in")
        adj_in = [sem(f"adj_in{t}") for t in range(T)]
        x_in = [sem(f"x_in{k}") for k in range(2)]
        x1_out = sem("x1_out")
        zeroed = sem("zeroed")
        idents = sem("idents")
        adj_bf = sem("adj_bf")
        adjT_ready = sem("adjT_ready")
        adjT_copied = sem("adjT_copied")
        sym_ready = sem("sym_ready")
        off_ready = sem("off_ready")
        stats_done = sem("stats_done")
        mv_done = sem("mv_done")
        ve_done = sem("ve_done")
        rstd_done = sem("rstd_done")
        h0_done = sem("h0_done")
        xb_done = sem("xb_done")
        aux_ready = sem("aux_ready")
        aux_free = sem("aux_free")
        s_ready = sem("s_ready")
        z_done = sem("z_done")
        masked = sem("masked")
        max_done = sem("max_done")
        exp_done = sem("exp_done")
        tlo_ready = sem("tlo_ready")
        thi_ready = sem("thi_ready")
        ptlo_done = sem("ptlo_done")
        pthi_done = sem("pthi_done")
        av_done = sem("av_done")
        oT_done = sem("oT_done")
        rden_done = sem("rden_done")
        y_done = sem("y_done")
        tot_done = sem("tot_done")
        v_step = sem("v_step")
        v_ready = sem("v_ready")
        fin_step = sem("fin_step")
        lam_done = sem("lam_done")
        held_pool = sem("held_pool")
        held_dve = sem("held_dve")
        held_sp = sem("held_sp")

        aux = banks[:, BANK_AUX, :]
        obank = banks[:, BANK_O, :]
        scores = [banks[:, 2 * k:2 * k + 2, :].rearrange("p a n -> p (a n)") for k in range(2)]

        PER = 11
        PW = 2
        VSTEPS = 5 * PW + 1

        def lists(bk):
            first, last = bk is not None and bk == 0, bk is not None and bk == B - 1
            order = aux_list(AUX1, first, last, PREP1, ("ot0", "ot1"))
            return {u: [[s for s in half if s in order] for half in AUX1.get(u, ([], []))] for u in range(T)}, order

        def base(bt):
            if isinstance(bt, int):
                return 6 if bt == 0 else 4 + PER * bt
            return bt * PER + 4

        def batches(eng, body):
            body(0, 0, 0)
            with eng.Fori(0, (B - 2) // 2) as i:
                for k in (1, 2):
                    body(i * 2 + k, k % 2, None)
            body(B - 1, (B - 1) % 2, B - 1)

        block = ctx.enter_context(nc.Block())

        @block.sync
        def _(sp):
            def hold(s, value):
                sp.wait_ge(s, value)
                sp.sem_inc(held_sp, 1)

            sp.sem_inc(x1_out, 16)
            sp.dma_start(xin[:, 0], rows(x[0])).then_inc(x_in[0], 16)
            for t in range(T):
                sp.dma_start(adj_f[:, t, :], adj[P * t:P * (t + 1), :]).then_inc(adj_in[t], 16)
            sp.dma_start(w_sb[:, :], W).then_inc(consts_in, 16)
            sp.dma_start(blin_col[:, :], b_lin.rearrange("(d o) -> d o", o=1)).then_inc(consts_in, 16)
            sp.dma_start(b_row[:, :], across(b)).then_inc(consts_in, 16)
            sp.dma_start(xin[:, 1], rows(x[1])).then_inc(x_in[1], 16)

            def body(bt, par, bk):
                if bk != 0:
                    pieces, order = lists(bk)
                    hold(aux_free, base(bt) + order.index("ot1") + 1)
                    sp.dma_start(rows(x1_dram[bt - 1] if isinstance(bt, int) else
                                      x1_dram[bass.ds(bt - 1, 1)].rearrange("o n d -> (o n) d")),
                                 xn[:, :, :]).then_inc(x1_out, 16)

            def load(bt, par):
                hold(h0_done, bt * 2)
                hold(xb_done, bt * 1)
                sp.dma_start(xin[:, 1 - par], rows(x[bt + 1] if isinstance(bt, int) else
                             x[bass.ds(bt + 1, 1)].rearrange("o n d -> (o n) d"))).then_inc(x_in[1 - par], 16)

            with sp.Fori(0, (B - 2) // 2) as i:
                for k in (1, 2):
                    load(i * 2 + k, k % 2)
                    body(i * 2 + k, k % 2, None)
            body(B - 1, (B - 1) % 2, B - 1)
            _, order = lists(B - 1)
            sp.wait_ge(aux_free, base(B - 1) + len(order) + 2)
            sp.dma_start(rows(x1_dram[B - 1]), xn[:, :, :]).then_inc(x1_out, 16)
            sp.wait_ge(x1_out, 16 * (B + 1))

        @block.gpsimd
        def _(pool):
            for m in (ident, identb, far_diag):
                nc.gpsimd.memset(m[:, :], 0.0).then_inc(zeroed, 1)
            nc.gpsimd.memset(ones[:, :], 1.0).then_inc(zeroed, 1)
            nc.gpsimd.memset(neg_half[:, :], -0.5).then_inc(zeroed, 1)
            nc.gpsimd.memset(v[:, :], 1.0 / N).then_inc(zeroed, 1)
            pool.wait_ge(zeroed, 6)
            for m, fill in ((ident, 1.0), (identb, 1.0), (far_diag, -FAR)):
                nc.gpsimd.affine_select(out=m[:, :], in_=m[:, :], compare_op=ALU.not_equal, fill=fill, base=0,
                                        pattern=[[-1, P]], channel_multiplier=1).then_inc(idents, 1)

            def hold(s, value):
                pool.wait_ge(s, value)
                pool.sem_inc(held_pool, 1)

            def split_v(n, m):
                if m is not None:
                    hold(v_step, n)
                nc.gpsimd.tensor_scalar(vp[:, :, 0], v[:, :], 1.0, 0.0, ALU.mult, ALU.add).then_inc(v_step, 1)
                hold(v_step, n + 1)
                nc.gpsimd.tensor_tensor(vr1[:, :], v[:, :], vp[:, :, 0], ALU.subtract).then_inc(v_step, 1)
                hold(v_step, n + 2)
                nc.gpsimd.tensor_scalar(vp[:, :, 1], vr1[:, :], 1.0, 0.0, ALU.mult, ALU.add).then_inc(v_step, 1)
                hold(v_step, n + 3)
                nc.gpsimd.tensor_tensor(vp[:, :, 2], vr1[:, :], vp[:, :, 1], ALU.subtract).then_inc(v_step, 1)
                hold(v_step, n + 4)
                pool.sem_inc(v_ready, 1)

            def ln_scale(n):
                hold(mv_done, n * 1 + 1)
                nc.gpsimd.tensor_scalar(ve[:, :], mv[:, :, 1], 1.0, EPS, ALU.mult, ALU.add).then_inc(ve_done, 1)
                nc.gpsimd.tensor_scalar(nm[:, :], mv[:, :, 0], -1.0, 0.0, ALU.mult, ALU.add).then_inc(ve_done, 1)
                hold(ve_done, n * 2 + 2)
                if not isinstance(n, int) or n > 0:
                    hold(h0_done, n * 2)
                nc.gpsimd.tensor_tensor(rstd[:, :], ve[:, :], neg_half[:, :], ALU.pow).then_inc(rstd_done, 1)
                hold(rstd_done, n * 2 + 1)
                nc.gpsimd.tensor_tensor(nmr[:, :], nm[:, :], rstd[:, :], ALU.mult).then_inc(rstd_done, 1)

            split_v(0, None)
            ln_scale(0)

            def body(bt, par, bk):
                pieces, order = lists(bk)
                if bk == 0:
                    hold(consts_in, 48)
                hold(x_in[par], arrivals(bt, par))
                if bk is None or bk > 1:
                    hold(aux_free, base(bt))
                nc.gpsimd.tensor_tensor(xb[:, par], xin[:, par], b_row[:, :].rearrange("p (o d) -> p o d", o=1)
                                        .to_broadcast([P, T, D]), ALU.add).then_inc(xb_done, 1)
                for u in range(T):
                    if u == LN_AT[1] and bk != B - 1:
                        ln_scale(bt + 1)
                    for s in pieces[u][0] + pieces[u][1]:
                        k = 4 + bt * VSTEPS
                        if s in ("pw0", "pw1"):
                            n = int(s[2])
                            hold(y_done, bt * PW + n + 1)
                            if n < PW - 1:
                                nc.gpsimd.tensor_tensor(v[:, :], v[:, :], y[:, :], ALU.add).then_inc(v_step, 1)
                                split_v(k + 5 * n + 1, 0)
                            else:
                                nc.gpsimd.tensor_tensor(vsum[:, :], v[:, :], y[:, :], ALU.add).then_inc(v_step, 1)
                        if s == "norm":
                            hold(tot_done, bt * 1 + 1)
                            nc.gpsimd.tensor_tensor(v[:, :], vsum[:, :], rtot[:, 0:1].to_broadcast([P, T]), ALU.mult)\
                                .then_inc(v_step, 1)
                            split_v(k + 5 * (PW - 1) + 2, 0)

            batches(pool, body)

        @block.scalar
        def _(act):
            act.sem_inc(oT_done, 1)
            for j in range(T):
                act.wait_ge(adjT_ready, j + 1)
                nc.scalar.activation(adjT[:, j, :], banks[:, j % 4, :].bitcast(BF16), ACT.Copy, saturate=False)\
                    .then_inc(adjT_copied, 1)

            def normalize(n, par, half):
                act.wait_ge(rstd_done, n * 2 + 2)
                for t in range(HT * half, HT * (half + 1)):
                    ins = nc.scalar.activation(h0[:, t, :], xin[:, par, t, :],
                                               ACT.Relu, bias=nmr[:, t:t + 1], scale=rstd[:, t:t + 1])
                ins.then_inc(h0_done, 1)

            def prep(s, value, par):
                if s in ("h0T0", "h0T1"):
                    k = int(s[-1])
                    act.wait_ge(aux_ready, value)
                    nc.scalar.activation(h0T[:, HALF * k:HALF * (k + 1)], aux, ACT.Copy).then_inc(aux_free, 1)
                if s in ("hT0", "hT1"):
                    k = int(s[-1])
                    act.wait_ge(aux_ready, value)
                    nc.scalar.activation(hT[:, par, HALF * k:HALF * (k + 1)], aux, ACT.Identity, bias=blin_col[:, 0:1])\
                        .then_inc(aux_free, 1)
                if s in ("hrow0", "hrow1"):
                    k = int(s[-1])
                    act.wait_ge(aux_ready, value)
                    nc.scalar.activation(hrow[:, par, HT * k:HT * (k + 1), :].rearrange("p t d -> p (t d)"), aux, ACT.Copy)\
                        .then_inc(aux_free, 1)

            act.wait_ge(consts_in, 48)
            act.wait_ge(x_in[0], 16)
            for half in range(2):
                normalize(0, 0, half)
            for n, s in enumerate(PREP1):
                prep(s, n + 1, 0)

            def exp_unit(U, u, par):
                act.wait_ge(max_done, U + 1)
                if not isinstance(U, int) or U >= 2:
                    act.wait_ge(thi_ready, U - 1)
                nc.scalar.activation(prob[:, u % 2, :], scores[u % 2], ACT.Exp, bias=nmax[:, u:u + 1],
                                     accum_out=den[:, par, u:u + 1]).then_inc(exp_done, 1)

            def evac_hi(ub, u):
                U = ub * T + u
                act.wait_ge(thi_ready, U + 1)
                g = u // GROUP
                if u % GROUP == 0 and (not isinstance(U, int) or U >= 2 * GROUP):
                    act.wait_ge(av_done, ub * 2 + g - 1)
                c = P * (u % GROUP)
                nc.scalar.activation(pt[:, g, HT:T, c:c + P],
                                     banks[:, BANK_T + 1, :].rearrange("p (t n) -> p t n", t=HT), ACT.Copy)\
                    .then_inc(pthi_done, 1)

            def copy_out(g, half, value):
                act.wait_ge(av_done, g + 1)
                if value is not None:
                    act.wait_ge(aux_ready, value)
                nc.scalar.activation(oT[:, HALF * half:HALF * (half + 1)], obank, ACT.Copy).then_inc(oT_done, 1)

            def body(bt, par, bk):
                pieces, order = lists(bk)
                U0 = bt * T
                for u in range(T):
                    if bk != 0 or u >= 1:
                        exp_unit(U0 + u - 1, (u - 1) % T, par if u >= 1 else 1 - par)
                    for s in pieces[u][0]:
                        prep(s, base(bt) + order.index(s) + 1, 1 - par)
                    if bk != 0 or u >= 2:
                        evac_hi(bt if u >= 2 else bt - 1, (u - 2) % T)
                    if u == 1 and bk != 0:
                        copy_out(bt * 2 - 2, 0, base(bt))
                    if u == 5 and bk != 0:
                        copy_out(bt * 2 - 1, 1, None)
                    if u in RELU_AT and bk != B - 1:
                        act.wait_ge(x_in[1 - par], arrivals(bt + 1, 1 - par))
                        normalize(bt + 1, 1 - par, RELU_AT.index(u))
                    for s in pieces[u][1]:
                        prep(s, base(bt) + order.index(s) + 1, 1 - par)

            batches(act, body)
            exp_unit(B * T - 1, T - 1, (B - 1) % 2)
            for u in (T - 2, T - 1):
                evac_hi(B - 1, u)
            _, order = lists(B - 1)
            copy_out(2 * B - 2, 0, base(B - 1) + len(order))
            copy_out(2 * B - 1, 1, None)

        @block.vector
        def _(dve):
            def hold(s, value):
                dve.wait_ge(s, value)
                dve.sem_inc(held_dve, 1)

            for t in range(T):
                dve.wait_ge(adj_in[t], 16)
                nc.vector.tensor_copy(off[:, t, :], adj_f[:, t, :]).then_inc(adj_bf, 1)

            def ln_stats(n, par, half):
                hold(x_in[par], arrivals(n, par))
                for t in range(HT * half, HT * (half + 1)):
                    ins = nc.vector.bn_stats(stats[:, t, :], xin[:, par, t, :])
                if half == 0:
                    return
                if not isinstance(n, int) or n > 0:
                    hold(rstd_done, n * 2)
                ins.then_inc(stats_done, 1)
                hold(stats_done, n * 1 + 1)
                for t in range(T):
                    ins = nc.vector.bn_aggr(mv[:, t, :], stats[:, t, :])
                ins.then_inc(mv_done, 1)

            for half in range(2):
                ln_stats(0, 0, half)
            for j in range(T):
                dve.wait_ge(adjT_copied, j + 1)
                nc.vector.tensor_tensor(sym[:, j, :], off[:, j, :], adjT[:, j, :], ALU.add).then_inc(sym_ready, 1)
            dve.wait_ge(sym_ready, T)
            for j in range(T):
                nc.vector.tensor_scalar(off[:, j, :], off[:, j, :], -1.0, 1.0, ALU.mult, ALU.add).then_inc(off_ready, 1)
            dve.wait_ge(off_ready, T)

            def mask_unit(U, u):
                dve.wait_ge(s_ready, U + 1)
                if not isinstance(U, int) or U >= 2:
                    hold(masked, U - 1)
                nc.vector.scalar_tensor_tensor(out=z[:, u % 2, :], in0=scores[u % 2], scalar=0.0, in1=off[:, u, :],
                                               op0=ALU.is_equal, op1=ALU.max).then_inc(z_done, 1)

            def max_unit(U, u):
                hold(masked, U + 1)
                if not isinstance(U, int) or U >= T:
                    hold(exp_done, U - T + 1)
                nc.vector.tensor_reduce(nmax[:, u:u + 1], scores[u % 2], AX.X, ALU.max, negate=True).then_inc(max_done, 1)

            def evac_lo(ub, u):
                U = ub * T + u
                hold(tlo_ready, U + 1)
                g = u // GROUP
                if u % GROUP == 0 and (not isinstance(U, int) or U >= 2 * GROUP):
                    dve.wait_ge(av_done, ub * 2 + g - 1)
                c = P * (u % GROUP)
                nc.vector.tensor_copy(pt[:, g, 0:HT, c:c + P],
                                      banks[:, BANK_T, :].rearrange("p (t n) -> p t n", t=HT)).then_inc(ptlo_done, 1)

            def power(s, value, bt):
                if s in ("pw0", "pw1"):
                    hold(aux_ready, value)
                    hold(v_ready, bt * PW + 1 + int(s[2]))
                    nc.vector.tensor_reduce(y[:, :], aux[:, 0:3 * T].rearrange("p (t k) -> p t k", k=3), AX.X, ALU.add)\
                        .then_inc(y_done, 1)
                    hold(y_done, bt * PW + int(s[2]) + 1)
                    dve.sem_inc(aux_free, 1)
                if s == "norm":
                    hold(aux_ready, value)
                    nc.vector.tensor_reduce(tot[:, :], aux[:, 0:T], AX.X, ALU.add).then_inc(fin_step, 1)
                    hold(fin_step, bt * 2 + 1)
                    dve.sem_inc(aux_free, 1)
                    nc.vector.tensor_scalar(tot2[:, :], tot[:, :], TINY, None, ALU.max).then_inc(fin_step, 1)
                    hold(fin_step, bt * 2 + 2)
                    nc.vector.reciprocal(rtot[:, :], tot2[:, :]).then_inc(tot_done, 1)

            def output(s, value, n, par):
                k = int(s[-1])
                if k == 0:
                    hold(exp_done, (n + 1) * T)
                    nc.vector.reciprocal(rden[:, :], den[:, par, :]).then_inc(rden_done, 1)
                    hold(rden_done, n * 1 + 1)
                    if not isinstance(n, int) or n > 0:
                        hold(x1_out, n * 16 + 16)
                hold(aux_ready, value)
                hold(xb_done, n * 1 + 1)
                for q in range(HT):
                    t = HT * k + q
                    ins = nc.vector.scalar_tensor_tensor(out=xn[:, t, :], in0=aux[:, P * q:P * (q + 1)], scalar=rden[:, t:t + 1],
                                                         in1=xb[:, par, t, :], op0=ALU.mult, op1=ALU.add)
                ins.then_inc(aux_free, 1)

            def body(bt, par, bk):
                pieces, order = lists(bk)
                U0 = bt * T
                def aside(half, u):
                    for s in pieces[u][half]:
                        value = base(bt) + order.index(s) + 1
                        power(s, value, bt)
                        if s in ("ot0", "ot1"):
                            output(s, value, bt - 1, 1 - par)

                for u in range(T):
                    mask_unit(U0 + u, u)
                    aside(0, u)
                    if bk != 0 or u >= 2:
                        evac_lo(bt if u >= 2 else bt - 1, (u - 2) % T)
                    max_unit(U0 + u, u)
                    aside(1, u)
                    if u in LN_AT and bk != B - 1:
                        ln_stats(bt + 1, 1 - par, LN_AT.index(u))

            batches(dve, body)
            _, order = lists(B - 1)
            end = base(B - 1) + len(order)
            for u in (T - 2, T - 1):
                evac_lo(B - 1, u)
            for k in range(2):
                output(f"ot{k}", end + k + 1, B - 1, (B - 1) % 2)
            dve.wait_ge(aux_ready, end + 3)
            nc.vector.tensor_reduce(y[:, :], aux[:, 0:3 * T].rearrange("p (t k) -> p t k", k=3), AX.X, ALU.add)\
                .then_inc(aux_free, 1)
            dve.wait_ge(aux_free, end + 3)
            nc.vector.tensor_tensor_reduce(junk[:, :], v[:, :], y[:, :], 1.0, 0.0, ALU.mult, ALU.add, nd[:, 0:1])\
                .then_inc(fin_step, 1)
            nc.vector.tensor_tensor_reduce(junk2[:, :], v[:, :], v[:, :], 1.0, 0.0, ALU.mult, ALU.add, nd[:, 1:2])\
                .then_inc(fin_step, 1)
            dve.wait_ge(aux_ready, end + 4)
            nc.vector.tensor_copy(fin[:, 0:2], aux[:, 0:2]).then_inc(fin_step, 1)
            n = 2 * B + 3
            for ins in (lambda: nc.vector.tensor_scalar(fin[:, 2:3], fin[:, 1:2], TINY, None, ALU.max),
                        lambda: nc.vector.reciprocal(fin[:, 3:4], fin[:, 2:3]),
                        lambda: nc.vector.tensor_tensor(fin[:, 4:5], fin[:, 0:1], fin[:, 3:4], ALU.mult),
                        lambda: nc.vector.tensor_scalar(fin[:, 5:6], fin[:, 4:5], 0.25, 0.5e-8, ALU.mult, ALU.add)):
                dve.wait_ge(fin_step, n)
                ins().then_inc(fin_step, 1)
                n += 1
            dve.wait_ge(fin_step, n)
            nc.vector.reciprocal(two_over_lam[:, :], fin[:, 5:6]).then_inc(lam_done, 1)
            for j in range(T):
                nc.vector.tensor_scalar(off[:, j, :], off[:, j, :], -FAR, None, ALU.mult).then_inc(off_ready, 1)
            dve.wait_ge(off_ready, 2 * T)

        @block.tensor
        def _(pe):
            pe.wait_ge(idents, 3)
            for j in range(T):
                if j == 0:
                    pe.wait_ge(adj_bf, T)
                if j >= 4:
                    pe.wait_ge(adjT_copied, j - 3)
                for i in range(T):
                    ins = nc.tensor.transpose(banks[:, j % 4, :].bitcast(BF16)[:, P * i:P * (i + 1)],
                                              off[:, i, P * j:P * (j + 1)], identb[:, :])
                ins.then_inc(adjT_ready, 1)

            def prep(s, value, par, n):
                k = int(s[-1])
                if not isinstance(value, int) or value > 1:
                    pe.wait_ge(aux_free, value - 1)
                if s == "h0T0":
                    pe.wait_ge(h0_done, n * 2 + 2)
                if s in ("h0T0", "h0T1"):
                    for q in range(HT):
                        ins = nc.tensor.transpose(aux[:, P * q:P * (q + 1)], h0[:, HT * k + q, :], ident[:, :])
                if s in ("hT0", "hT1"):
                    ins = nc.tensor.matmul(aux, w_sb[:, :], h0T[:, HALF * k:HALF * (k + 1)], start=True, stop=True)
                if s in ("hrow0", "hrow1"):
                    for q in range(HT):
                        t = HT * k + q
                        ins = nc.tensor.transpose(aux[:, P * q:P * (q + 1)], hT[:, par, P * t:P * (t + 1)], ident[:, :])
                ins.then_inc(aux_ready, 1)

            def power(s, value, n):
                pe.wait_ge(aux_free, value - 1)
                pe.wait_ge(v_ready, n) if s != "norm" else pe.wait_ge(v_step, n)
                if s == "norm":
                    nc.tensor.matmul(aux[:, 0:T], ones[:, :], vsum[:, :], start=True, stop=True).then_inc(aux_ready, 1)
                    return
                for j in range(T):
                    for i in range(T):
                        ins = nc.tensor.matmul(aux[:, 3 * j:3 * j + 3], sym[:, i, P * j:P * (j + 1)], vp[:, i, :],
                                               start=(i == 0), stop=(i == T - 1))
                ins.then_inc(aux_ready, 1)

            pe.wait_ge(consts_in, 48)
            for n, s in enumerate(PREP1):
                prep(s, n + 1, 0, 0)
            pe.wait_ge(sym_ready, T)

            def scores_unit(U, u, par):
                if not isinstance(U, int) or U >= 2:
                    pe.wait_ge(exp_done, U - 1)
                else:
                    pe.wait_ge(adjT_copied, T)
                for k in range(2):
                    ins = nc.tensor.matmul(scores[u % 2][:, HALF * k:HALF * (k + 1)], hT[:, par, P * u:P * (u + 1)],
                                           hT[:, par, HALF * k:HALF * (k + 1)], start=True, stop=False, skip_group_check=True)
                ins.then_inc(s_ready, 1)

            def lower_unit(U, u):
                pe.wait_ge(z_done, U + 1)
                for k in range(2):
                    ins = nc.tensor.matmul(scores[u % 2][:, HALF * k:HALF * (k + 1)], far_diag[:, :],
                                           z[:, u % 2, HALF * k:HALF * (k + 1)], start=False, stop=True, skip_group_check=True)
                ins.then_inc(masked, 1)

            def transpose_unit(U, u):
                pe.wait_ge(exp_done, U + 1)
                for half, (free, ready) in enumerate(((ptlo_done, tlo_ready), (pthi_done, thi_ready))):
                    if not isinstance(U, int) or U >= 1:
                        pe.wait_ge(free, U * 1)
                    for q in range(HT):
                        t = HT * half + q
                        ins = nc.tensor.transpose(banks[:, BANK_T + half, P * q:P * (q + 1)],
                                                  prob[:, u % 2, P * t:P * (t + 1)], ident[:, :])
                    ins.then_inc(ready, 1)

            def values_chunk(g, gpar, par, c):
                if c == 0:
                    pe.wait_ge(ptlo_done, (g + 1) * GROUP)
                    pe.wait_ge(pthi_done, (g + 1) * GROUP)
                    pe.wait_ge(oT_done, g + 1)
                for j in (2 * c, 2 * c + 1):
                    ins = nc.tensor.matmul(obank, hrow[:, par, j, :], pt[:, gpar, j, :], start=(j == 0), stop=(j == T - 1))
                if c == 3:
                    ins.then_inc(av_done, 1)

            def output(k, value, n):
                pe.wait_ge(aux_free, value - 1)
                pe.wait_ge(oT_done, n * 2 + 2 + k)
                for q in range(HT):
                    t = HT * k + q
                    ins = nc.tensor.transpose(aux[:, P * q:P * (q + 1)], oT[:, P * t:P * (t + 1)], ident[:, :])
                ins.then_inc(aux_ready, 1)

            def body(bt, par, bk):
                pieces, order = lists(bk)
                U0 = bt * T

                def aside(half, u):
                    for s in pieces[u][half]:
                        value = base(bt) + order.index(s) + 1
                        if s in PREP1:
                            prep(s, value, 1 - par, bt + 1)
                        elif s in ("ot0", "ot1"):
                            output(int(s[-1]), value, bt - 1)
                        elif s == "norm":
                            power(s, value, bt * VSTEPS + 4 + 5 * (PW - 1) + 1)
                        else:
                            power(s, value, bt * PW + 1 + int(s[2]))

                for u in range(T):
                    if u == 0:
                        pe.wait_ge(aux_free, base(bt) - (2 if bk == 0 else 3))
                    scores_unit(U0 + u, u, par)
                    aside(0, u)
                    if bk != 0 or u >= 2:
                        transpose_unit(U0 + u - 2, (u - 2) % T)
                    if u < 2 and bk != 0:
                        values_chunk(bt * 2 - 2, 0, 1 - par, u + 2)
                    if 2 <= u < 6 and bk != 0:
                        values_chunk(bt * 2 - 1, 1, 1 - par, u - 2)
                    if u >= 6:
                        values_chunk(bt * 2, 0, par, u - 6)
                    lower_unit(U0 + u, u)
                    aside(1, u)

            batches(pe, body)
            _, order = lists(B - 1)
            end = base(B - 1) + len(order)
            for u in (T - 2, T - 1):
                transpose_unit((B - 1) * T + u, u)
            for c in (2, 3):
                values_chunk(2 * B - 2, 0, (B - 1) % 2, c)
            for c in range(4):
                values_chunk(2 * B - 1, 1, (B - 1) % 2, c)
            for k in range(2):
                output(k, end + k + 1, B - 1)
            power("last", end + 3, B * PW + 1)
            pe.wait_ge(aux_free, end + 3)
            pe.wait_ge(fin_step, 2 * B + 2)
            nc.tensor.matmul(aux[:, 0:2], ones[:, :], nd[:, :], start=True, stop=True).then_inc(aux_ready, 1)


BESIDE = {
    0: ([], ["ln1_stats0"]), 1: ([], ["ln1_stats1"]), 2: ([], ["ln1_relu0"]), 3: ([], ["ln1_relu1"]), 4: ([], ["h1t0"]),
    5: (["h1t1"], ["g0"]), 6: (["g1"], ["or0", "gsplit"]), 7: (["or1"], ["ot0"]), 8: (["ot1"], ["wo0", "gmid"]),
    9: (["wo1"], ["ln2_stats0"]), 10: ([], ["ln2_stats1"]), 11: (["ag0a"], []), 12: (["ag0"], ["ln2_apply0"]),
    13: (["ag1a"], ["ln2_apply1"]), 14: (["ag1"], ["lng_stats0"]), 15: ([], ["lng_stats1"]), 17: ([], ["lng_apply0"]), 18: ([], ["lng_apply1"]),
    20: ([], ["lng_relu"]), 21: (["x1t0"], ["x1t1"]), 22: (["q0"], ["q1", "qstack"]), 23: (["v0"], ["v1"]),
    24: (["k0"], ["k1", "kstack", "x1b"]), 25: ([], ["x2t0"]), 26: (["x2t1"], ["w10"]), 27: (["w11"], ["w12"]), 28: (["w13"], ["gelu"]),
    29: ([], ["w20"]), 30: (["w21"], ["ln3_stats0", "ln3_stats1"]), 31: (["ln3_apply0"], ["ln3_apply1", "res"]),
}
POST2 = ("or0", "or1", "ot0", "ot1", "wo0", "wo1", "ln2_stats0", "ln2_stats1", "ln2_apply0", "ln2_apply1", "x2t0", "x2t1",
         "w10", "w11", "w12", "w13", "gelu", "w20", "w21", "ln3_stats0", "ln3_stats1", "ln3_apply0", "ln3_apply1", "res")
BANKED = ("h1t0", "h1t1", "g0", "g1", "ag0", "ag1", "x1t0", "x1t1", "q0", "q1", "k0", "k1", "v0", "v1",
          "or0", "or1", "ot0", "ot1", "wo0", "wo1", "x2t0", "x2t1", "w10", "w11", "w12", "w13", "w20", "w21")
UNITS = T * H
QT = 2
QN = QT * P
QU = QT * H
AV_AT = (10, 12)
COPY_AT = 13


def block2(nc, x1_dram, Wc, bcv, g1, be1, Wq, Wk, Wv, Wo, bo, g2, be2, W1, b1, W2, b2, g3, be3, out, banks, shared):
    SCALE = float(HD) ** -0.5
    parts_dram = nc.dram_tensor("parts_of_q_and_k", (2, 3, D, N), BF16, kind="Internal").ap()
    with ExitStack() as ctx:
        sb = lambda n, s, d: ctx.enter_context(nc.sbuf_tensor(n, s, d))
        sem = lambda n: ctx.enter_context(nc.semaphore(n))
        ident, neg_half, adjT, off, two_over_lam = (shared[k] for k in ("ident", "neg_half", "adjT", "off", "two_over_lam"))

        pt = sb("pt2", [P, 2, T, H, QN], F32)
        qs = sb("qs", [P, 2, H, N], BF16)
        k1s = sb("k1s", [P, 2, H, N], BF16)
        k2s = sb("k2s", [P, 2, H, N], BF16)
        vrow = sb("vrow", [P, 2, T, D], F32)
        prob = sb("prob2", [P, 2, N], F32)
        x1b = sb("x1b", [P, 2, T, D], F32)
        h1x = sb("h1x", [P, T, D], F32)
        parts = sb("parts", [P, 6, N], BF16)
        work = sb("work", [P, 2, N], F32)
        fT = sb("fT", [P, N], F32)
        oT = sb("oT2", [P, N], F32)
        post = sb("post", [P, T, D], F32)
        wts = {n: sb("w_" + n, [P, D], F32) for n in ("c", "q", "k", "v", "o")}
        w1_sb = sb("w1_sb", [P, HID], F32)
        w2_sb = sb("w2_sb", [P, HC, D], F32)
        b1_col = sb("b1_col", [P, HC], F32)
        vecs = {n: sb("v_" + n, [P, D], F32) for n in ("bc", "g1", "be1", "bo", "g2", "be2", "b2", "g3", "be3")}
        top = sb("top", [P, UNITS], F32)
        ntop = sb("ntop", [P, UNITS], F32)
        den = sb("den2", [P, 2, UNITS], F32)
        rden = sb("rden2", [P, UNITS], F32)
        ln = {}
        for c in ("next", "last"):
            ln[c] = dict(stats=sb("stats_" + c, [P, T, 6], F32), mv=sb("mv_" + c, [P, T, 2], F32),
                         ve=sb("ve_" + c, [P, T], F32), nm=sb("nm_" + c, [P, T], F32), rstd=sb("rstd_" + c, [P, T], F32),
                         nmr=sb("nmr_" + c, [P, T], F32),
                         stats_done=sem("stats_done_" + c), mv_done=sem("mv_done_" + c), ve_done=sem("ve_done_" + c),
                         rstd_done=sem("rstd_done_" + c))

        consts_in = sem("consts_in2")
        x_in = sem("x_in2")
        res_in = sem("res_in")
        parts_out = sem("parts_out")
        stack_in = sem("stack_in")
        out_done = sem("out_done")
        zero_done = sem("zero_done")
        aux_ready = sem("aux_ready2")
        aux_free = sem("aux_free2")
        h1_done = sem("h1_done")
        nmr_done = sem("nmr_done")
        ghi_done = sem("ghi_done")
        grem_done = sem("grem_done")
        gmid_done = sem("gmid_done")
        glo_done = sem("glo_done")
        gb_done = sem("gb_done")
        lng_applied = sem("lng_applied")
        lng_affine = sem("lng_affine")
        x1_done = sem("x1_done")
        x1b_done = sem("x1b_done")
        hi_done = sem("hi_done")
        rem_done = sem("rem_done")
        mid_done = sem("mid_done")
        lo_done = sem("lo_done")
        rden_done = sem("rden_done2")
        ln2_applied = sem("ln2_applied")
        ln2_affine = sem("ln2_affine")
        x2b_done = sem("x2b_done")
        hid_done = sem("hid_done")
        gelu_done = sem("gelu_done")
        ln3_applied = sem("ln3_applied")
        ln3_affine = sem("ln3_affine")
        res_done = sem("res_done")
        s_ready = sem("s_ready2")
        low_done = sem("low_done")
        ntop_done = sem("ntop_done")
        exp_done = sem("exp_done2")
        tlo_ready = sem("tlo_ready2")
        thi_ready = sem("thi_ready2")
        ptlo_done = sem("ptlo_done2")
        pthi_done = sem("pthi_done2")
        av_done = sem("av_done2")
        oT_done = sem("oT_done2")
        held_pool = sem("held_pool2")
        held_dve = sem("held_dve2")
        held_act = sem("held_act2")
        held_pe = sem("held_pe2")
        held_sp = sem("held_sp2")

        aux = banks[:, BANK_AUX, :]
        auxr = aux.rearrange("p (t d) -> p t d", t=HT)
        obank = banks[:, BANK_O, 0:QN]
        scores = [banks[:, 2 * k:2 * k + 2, :].rearrange("p a n -> p (a n)") for k in range(2)]
        rem = work[:, 0, :]
        gf = work[:, 1, :].rearrange("p (t d) -> p t d", t=T)
        hidT = work[:, :, :].rearrange("p c n -> p (c n)")
        flat = lambda a: a.rearrange("p t d -> p (t d)")
        rows_b = lambda n, t=T: vecs[n][:, :].rearrange("p (o d) -> p o d", o=1).to_broadcast([P, t, D])
        gparts = [parts[:, k, :].rearrange("p (t d) -> p t d", t=T) for k in range(3)]
        NV = 5 + 2 + HC + 9
        STACKS = (((qs, (0, 0, 1, 2)),), ((k1s, (0, 2, 0, 0)), (k2s, (1, None, 1, 1))))
        STACKED = 16 * sum(part is not None for k in STACKS for _, slots in k for part in slots)
        PER = len(BANKED)
        PREP = [s for u in sorted(BESIDE) for half in BESIDE[u] for s in half if s not in POST2]
        POST = [s for u in sorted(BESIDE) for half in BESIDE[u] for s in half if s in POST2]

        def beside(bk):
            keep = lambda s: not (bk == 0 and s in POST2) and not (bk == B - 1 and s not in POST2)
            table = {u: [[s for s in half if keep(s)] for half in BESIDE.get(u, ([], []))] for u in range(UNITS)}
            order = [s for u in range(UNITS) for half in table[u] for s in half if s in BANKED]
            return table, order

        def base(bt):
            return PER // 2 if isinstance(bt, int) and bt == 0 else bt * PER

        def batches(eng, body):
            body(0, 0, 0)
            with eng.Fori(0, (B - 2) // 2) as i:
                for k in (1, 2):
                    body(i * 2 + k, k % 2, None)
            body(B - 1, (B - 1) % 2, B - 1)

        def late(bt, u, lag):
            return (bt, u - lag) if u >= lag else (bt - 1, u - lag + UNITS)

        def quarters(u, at):
            for q in range(T // QT):
                for ago in (0, 1):
                    if q * QU + at == u + ago * UNITS:
                        return q, ago
            return None

        def one(dram, n):
            return rows(dram[n] if isinstance(n, int) else dram[bass.ds(n, 1)].rearrange("o n d -> (o n) d"))

        block = ctx.enter_context(nc.Block())

        @block.sync
        def _(sp):
            def hold(s, value):
                sp.wait_ge(s, value)
                sp.sem_inc(held_sp, 1)

            sp.sem_inc(out_done, 16)
            for n, src in (("c", Wc), ("q", Wq), ("k", Wk), ("v", Wv), ("o", Wo)):
                sp.dma_start(wts[n][:, :], src).then_inc(consts_in, 16)
            sp.dma_start(w1_sb[:, :], W1).then_inc(consts_in, 16)
            sp.dma_start(w2_sb[:, :, :], W2.rearrange("(c p) d -> p c d", p=P)).then_inc(consts_in, 16)
            for c in range(HC):
                sp.dma_start(b1_col[:, c:c + 1], b1[P * c:P * (c + 1)].rearrange("(p o) -> p o", o=1)).then_inc(consts_in, 16)
            for n, src in (("bc", bcv), ("g1", g1), ("be1", be1), ("bo", bo), ("g2", g2), ("be2", be2), ("b2", b2),
                           ("g3", g3), ("be3", be3)):
                sp.dma_start(vecs[n][:, :], across(src)).then_inc(consts_in, 16)


            def step(s, n, par):
                if s == "ln1_stats0":
                    if not isinstance(n, int) or n > 0:
                        hold(x1b_done, n * 1)
                    sp.dma_start(h1x[:, :, :], one(x1_dram, n)).then_inc(x_in, 16)
                if s in ("qstack", "kstack"):
                    k = "qk".index(s[0])
                    if k == 0 and (not isinstance(n, int) or n >= 2):
                        hold(s_ready, (n - 1) * UNITS)
                    hold(lo_done, n * 2 + k + 1)
                    sp.dma_start(parts_dram[k].rearrange("a p n -> p a n"), parts[:, 3 * k:3 * k + 3, :]).then_inc(parts_out, 16)
                    hold(parts_out, n * 32 + 16 * (k + 1))
                    for dst, slots in STACKS[k]:
                        for at, part in enumerate(slots):
                            if part is not None:
                                sp.dma_start(dst[HD * at:HD * (at + 1), par, :, :],
                                             parts_dram[k, part].rearrange("(h r) n -> r h n", r=HD)).then_inc(stack_in, 16)

            def post_step(s, n, value):
                if s == "ln3_stats0":
                    hold(aux_free, value)
                    sp.dma_start(gf, one(x1_dram, n)).then_inc(res_in, 16)

            for s in PREP:
                step(s, 0, 0)

            def body(bt, par, bk):
                table, order = beside(bk)
                for u in range(UNITS):
                    for s in table[u][0] + table[u][1]:
                        step(s, bt + 1, 1 - par) if s not in POST2 else \
                            post_step(s, bt - 1, base(bt) + order.index("w21") + 1)

            batches(sp, body)
            for s in POST:
                post_step(s, B - 1, base(B - 1) + PER)
            sp.wait_ge(out_done, 16 * (B + 1))

        @block.gpsimd
        def _(pool):
            def hold(s, value):
                pool.wait_ge(s, value)
                pool.sem_inc(held_pool, 1)

            pool.sem_inc(res_done, 1)
            for par in range(2):
                nc.gpsimd.memset(k2s[HD:2 * HD, par], 0.0).then_inc(zero_done, 1)
            pool.wait_ge(zero_done, 2)
            pool.wait_ge(consts_in, 16 * NV)

            def scale(c, n, k):
                L = ln[c]
                i = n * 2 + k
                hold(L["mv_done"], i + 1)
                if c == "next" and k == 1:
                    hold(h1_done, n * 2 + 2)
                nc.gpsimd.tensor_scalar(L["ve"][:, :], L["mv"][:, :, 1], 1.0, EPS, ALU.mult, ALU.add).then_inc(L["ve_done"], 1)
                nc.gpsimd.tensor_scalar(L["nm"][:, :], L["mv"][:, :, 0], -1.0, 0.0, ALU.mult, ALU.add).then_inc(L["ve_done"], 1)
                hold(L["ve_done"], i * 2 + 2)
                nc.gpsimd.tensor_tensor(L["rstd"][:, :], L["ve"][:, :], neg_half[:, :], ALU.pow).then_inc(L["rstd_done"], 1)

            def step(s, n, par):
                if s == "ln1_stats1":
                    scale("next", n, 0)
                    L = ln["next"]
                    hold(L["rstd_done"], n * 2 + 1)
                    nc.gpsimd.tensor_tensor(L["nmr"][:, :], L["nm"][:, :], L["rstd"][:, :], ALU.mult).then_inc(nmr_done, 1)
                if s == "gsplit":
                    hold(ghi_done, n * 1 + 1)
                    if not isinstance(n, int) or n > 0:
                        hold(lo_done, n * 2)
                    nc.gpsimd.tensor_tensor(rem, flat(gf), parts[:, 0, :], ALU.subtract).then_inc(grem_done, 1)
                if s == "gmid":
                    hold(gmid_done, n * 1 + 1)
                    nc.gpsimd.tensor_tensor(parts[:, 2, :], rem, parts[:, 1, :], ALU.subtract).then_inc(glo_done, 1)
                    nc.gpsimd.tensor_tensor(gf, gf, rows_b("bc"), ALU.subtract).then_inc(gb_done, 1)
                if s == "lng_stats1":
                    scale("next", n, 1)
                if s == "lng_apply1":
                    hold(lng_applied, n * 1 + 1)
                    nc.gpsimd.tensor_tensor(gf, gf, rows_b("g1"), ALU.mult).then_inc(lng_affine, 1)
                    hold(lng_affine, n * 2 + 1)
                    nc.gpsimd.tensor_tensor(gf, gf, rows_b("be1"), ALU.add).then_inc(lng_affine, 1)
                if s == "x1b":
                    hold(x1_done, n * 1 + 1)
                    nc.gpsimd.tensor_tensor(x1b[:, par], h1x[:, :, :], rows_b("bo"), ALU.add).then_inc(x1b_done, 1)
                if s in ("q1", "k1"):
                    k = "qk".index(s[0])
                    at = 3 * k
                    hold(rem_done, n * 4 + 2 * k + 2)
                    nc.gpsimd.tensor_scalar(parts[:, at + 1, :], rem, 1.0, 0.0, ALU.mult, ALU.add).then_inc(mid_done, 1)
                    hold(mid_done, n * 2 + k + 1)
                    nc.gpsimd.tensor_tensor(parts[:, at + 2, :], rem, parts[:, at + 1, :], ALU.subtract)\
                        .then_inc(lo_done, 1)

            def post_step(s, n):
                if s == "ln2_stats1":
                    scale("last", n, 0)
                if s == "ln2_apply1":
                    hold(ln2_applied, n * 1 + 1)
                    nc.gpsimd.tensor_tensor(post[:, :, :], post[:, :, :], rows_b("g2"), ALU.mult).then_inc(ln2_affine, 1)
                    hold(ln2_affine, n * 2 + 1)
                    nc.gpsimd.tensor_tensor(post[:, :, :], post[:, :, :], rows_b("be2"), ALU.add).then_inc(ln2_affine, 1)
                if s == "w11":
                    hold(hid_done, n * 4 + 1)
                    nc.gpsimd.tensor_tensor(post[:, :, :], post[:, :, :], rows_b("b2"), ALU.add).then_inc(x2b_done, 1)
                if s == "ln3_stats1":
                    scale("last", n, 1)
                if s == "ln3_apply1":
                    hold(res_in, n * 16 + 16)
                    nc.gpsimd.tensor_tensor(gf, gf, rows_b("be3"), ALU.add).then_inc(ln3_affine, 1)
                    hold(ln3_applied, n * 1 + 1)
                    nc.gpsimd.tensor_tensor(post[:, :, :], post[:, :, :], rows_b("g3"), ALU.mult).then_inc(ln3_affine, 1)
                    hold(ln3_affine, n * 2 + 2)
                    nc.gpsimd.tensor_tensor(post[:, :, :], post[:, :, :], gf, ALU.add).then_inc(res_done, 1)

            for s in PREP:
                step(s, 0, 0)

            def body(bt, par, bk):
                table, order = beside(bk)
                for u in range(UNITS):
                    for s in table[u][0] + table[u][1]:
                        step(s, bt + 1, 1 - par) if s not in POST2 else post_step(s, bt - 1)

            batches(pool, body)
            for s in POST:
                post_step(s, B - 1)

        @block.scalar
        def _(act):
            def step(s, n, par, value):
                k = int(s[-1]) if s in BANKED else 0
                cols = slice(HALF * k, HALF * (k + 1))
                tiles = slice(HT * k, HT * (k + 1))
                if s in ("ln1_relu0", "ln1_relu1"):
                    act.wait_ge(nmr_done, n * 1 + 1)
                    L = ln["next"]
                    half = int(s[-1])
                    for t in range(HT * half, HT * (half + 1)):
                        ins = nc.scalar.activation(h1x[:, t, :], h1x[:, t, :], ACT.Relu, bias=L["nmr"][:, t:t + 1],
                                                   scale=L["rstd"][:, t:t + 1])
                    ins.then_inc(h1_done, 1)
                if s in ("h1t0", "h1t1", "x1t0", "x1t1"):
                    act.wait_ge(aux_ready, value)
                    nc.scalar.activation(fT[:, cols], aux, ACT.Copy).then_inc(aux_free, 1)
                if s in ("g0", "g1"):
                    act.wait_ge(aux_ready, value)
                    if (not isinstance(n, int) or n >= 2) and k == 0:
                        act.wait_ge(res_done, n - 1)
                    nc.scalar.activation(gf[:, tiles, :], auxr, ACT.Copy).then_inc(aux_free, 1)
                if s in ("q0", "q1", "k0", "k1"):
                    act.wait_ge(aux_ready, value)
                    nc.scalar.activation(parts[:, 3 * "qk".index(s[0]), cols], aux, ACT.Copy).then_inc(hi_done, 1)
                if s in ("v0", "v1"):
                    act.wait_ge(aux_ready, value)
                    nc.scalar.activation(vrow[:, par, tiles, :], auxr, ACT.Copy).then_inc(aux_free, 1)

            def post_step(s, n, value):
                k = int(s[-1]) if s in BANKED else 0
                if s in ("ot0", "ot1", "x2t0", "x2t1"):
                    act.wait_ge(aux_ready, value)
                    nc.scalar.activation(fT[:, HALF * k:HALF * (k + 1)], aux, ACT.Copy).then_inc(aux_free, 1)
                if s in ("w10", "w11", "w12", "w13"):
                    act.wait_ge(aux_ready, value)
                    if k == 0:
                        ahead = lambda m, most: min(m, most) if isinstance(n, int) else m
                        act.wait_ge(lo_done, ahead(n * 2 + 6, 2 * B))
                        act.wait_ge(x1_done, ahead(n + 3, B))
                        act.wait_ge(res_done, n + 1)
                    nc.scalar.activation(hidT[:, HALF * k:HALF * (k + 1)], aux, ACT.Identity, bias=b1_col[:, k // 2:k // 2 + 1])\
                        .then_inc(hid_done, 1)
                    act.wait_ge(hid_done, n * 4 + k + 1)
                    act.sem_inc(aux_free, 1)
                if s == "gelu":
                    act.wait_ge(hid_done, n * 4 + 4)
                    nc.scalar.activation(hidT, hidT, ACT.Gelu).then_inc(gelu_done, 1)
                if s == "res":
                    act.wait_ge(res_done, n + 2)
                    act.sem_inc(held_act, 1)
                    act.dma_start(one(out, n), post[:, :, :]).then_inc(out_done, 16)

            def exp_unit(bt, u, par):
                U = bt * UNITS + u
                act.wait_ge(ntop_done, U + 1)
                if not isinstance(U, int) or U >= 2:
                    act.wait_ge(thi_ready, U - 1)
                nc.scalar.activation(prob[:, u % 2, :], scores[u % 2], ACT.Exp, bias=ntop[:, u:u + 1], scale=SCALE,
                                     accum_out=den[:, par, u:u + 1]).then_inc(exp_done, 1)

            def evac_hi(bt, u):
                q, i, h = u // QU, u % QU // H, u % H
                act.wait_ge(thi_ready, bt * UNITS + u + 1)
                g = bt * (T // QT) + q
                if u % QU == 0 and (not isinstance(g, int) or g >= 2):
                    act.wait_ge(av_done, g - 1)
                nc.scalar.activation(pt[:, q % 2, HT:T, h, P * i:P * (i + 1)],
                                     banks[:, BANK_T + 1, :].rearrange("p (t n) -> p t n", t=HT), ACT.Copy)\
                    .then_inc(pthi_done, 1)

            def copy_out(bt, q, value):
                act.wait_ge(av_done, bt * (T // QT) + q + 1)
                if value is not None:
                    act.wait_ge(aux_ready, value)
                nc.scalar.activation(oT[:, QN * q:QN * (q + 1)], obank, ACT.Copy).then_inc(oT_done, 1)

            act.wait_ge(consts_in, 16 * NV)
            value = 0
            for s in PREP:
                value += s in BANKED
                step(s, 0, 0, value)

            def body(bt, par, bk):
                table, order = beside(bk)

                def aside(half, u):
                    for s in table[u][half]:
                        value = base(bt) + order.index(s) + 1 if s in BANKED else None
                        step(s, bt + 1, 1 - par, value) if s not in POST2 else post_step(s, bt - 1, value)

                for u in range(UNITS):
                    if bk != 0 or u >= 1:
                        exp_unit(*late(bt, u, 1), par if u >= 1 else 1 - par)
                    aside(0, u)
                    if bk != 0 or u >= 2:
                        evac_hi(*late(bt, u, 2))
                    found = quarters(u, COPY_AT)
                    if found and not (found[1] and bk == 0):
                        q, ago = found
                        copy_out(bt - ago, q, base(bt) + order.index("or1") + 1 if q == 0 and bk != 0 else None)
                    aside(1, u)

            batches(act, body)
            exp_unit(B - 1, UNITS - 1, (B - 1) % 2)
            for u in (UNITS - 2, UNITS - 1):
                evac_hi(B - 1, u)
            copy_out(B - 1, T // QT - 1, None)
            value = base(B - 1) + PER // 2
            for s in POST:
                value += s in BANKED
                post_step(s, B - 1, value)

        @block.vector
        def _(dve):
            def hold(s, value):
                dve.wait_ge(s, value)
                dve.sem_inc(held_dve, 1)

            dve.wait_ge(consts_in, 16 * NV)

            def statistics(c, n, k, src, half):
                L = ln[c]
                i = n * 2 + k
                for t in range(HT * half, HT * (half + 1)):
                    ins = nc.vector.bn_stats(L["stats"][:, t, :], src[:, t, :])
                if half == 0:
                    return
                if c == "next" and k == 1:
                    hold(L["rstd_done"], i)
                ins.then_inc(L["stats_done"], 1)
                hold(L["stats_done"], i + 1)
                for t in range(T):
                    ins = nc.vector.bn_aggr(L["mv"][:, t, :], L["stats"][:, t, :])
                ins.then_inc(L["mv_done"], 1)

            def apply(c, n, k, rows_, half, done):
                L = ln[c]
                dve.wait_ge(L["rstd_done"], n * 2 + k + 1)
                for t in range(HT * half, HT * (half + 1)):
                    ins = nc.vector.tensor_scalar(rows_[:, t, :], rows_[:, t, :], L["nm"][:, t:t + 1], L["rstd"][:, t:t + 1],
                                                  ALU.add, ALU.mult)
                if half == 1:
                    ins.then_inc(done, 1)

            def step(s, n, value):
                k = int(s[-1]) if s[-1] in "01" else 0
                cols = slice(HALF * k, HALF * (k + 1))
                tiles = slice(HT * k, HT * (k + 1))
                if s in ("ln1_stats0", "ln1_stats1"):
                    dve.wait_ge(x_in, n * 16 + 16)
                    statistics("next", n, 0, h1x, k)
                if s == "gsplit":
                    dve.wait_ge(aux_free, value)
                    if not isinstance(n, int) or n > 0:
                        dve.wait_ge(stack_in, n * STACKED)
                    nc.vector.tensor_copy(parts[:, 0, :], flat(gf)).then_inc(ghi_done, 1)
                if s == "gmid":
                    dve.wait_ge(grem_done, n * 1 + 1)
                    nc.vector.tensor_copy(parts[:, 1, :], rem).then_inc(gmid_done, 1)
                if s in ("ag0", "ag1"):
                    dve.wait_ge(aux_ready, value)
                    dve.wait_ge(gb_done, n * 1 + 1)
                    nc.vector.scalar_tensor_tensor(out=flat(gf[:, tiles, :]), in0=aux, scalar=two_over_lam[:, 0:1],
                                                   in1=flat(gf[:, tiles, :]), op0=ALU.mult, op1=ALU.subtract)\
                        .then_inc(aux_free, 1)
                if s in ("lng_stats0", "lng_stats1"):
                    dve.wait_ge(aux_free, value)
                    statistics("next", n, 1, gf, k)
                if s in ("lng_apply0", "lng_apply1"):
                    apply("next", n, 1, gf, k, lng_applied)
                if s == "lng_relu":
                    dve.wait_ge(lng_affine, n * 2 + 2)
                    nc.vector.scalar_tensor_tensor(out=flat(h1x[:, :, :]), in0=flat(gf), scalar=0.0,
                                                   in1=flat(h1x[:, :, :]), op0=ALU.max, op1=ALU.add).then_inc(x1_done, 1)
                if s in ("q0", "q1", "k0", "k1"):
                    q = "qk".index(s[0])
                    dve.wait_ge(hi_done, n * 4 + 2 * q + k + 1)
                    if q:
                        dve.wait_ge(lo_done, n * 2 + 1)
                    nc.vector.tensor_tensor(rem[:, cols], aux, parts[:, 3 * q, cols], ALU.subtract).then_inc(rem_done, 1)
                    dve.wait_ge(rem_done, n * 4 + 2 * q + k + 1)
                    dve.sem_inc(aux_free, 1)

            def post_step(s, n, value, par):
                k = int(s[-1]) if s[-1] in "01" else 0
                tiles = slice(HT * k, HT * (k + 1))
                if s == "or0":
                    dve.wait_ge(exp_done, (n + 1) * UNITS)
                    nc.vector.reciprocal(rden[:, :], den[:, par, :]).then_inc(rden_done, 1)
                    dve.wait_ge(rden_done, n * 1 + 1)
                    dve.wait_ge(out_done, n * 16 + 16)
                if s in ("or0", "or1"):
                    dve.wait_ge(aux_ready, value)
                    by_head = lambda a: a.rearrange("p (g d) -> p g d", d=HD)
                    nc.vector.tensor_tensor(by_head(flat(post[:, tiles, :])), by_head(aux),
                                            bc(rden[:, HT * H * k:HT * H * (k + 1)], HD), ALU.mult).then_inc(aux_free, 1)
                if s in ("wo0", "wo1"):
                    dve.wait_ge(aux_ready, value)
                    dve.wait_ge(x1b_done, n * 1 + 1)
                    nc.vector.tensor_tensor(flat(post[:, tiles, :]), aux, flat(x1b[:, par, tiles, :]), ALU.add)\
                        .then_inc(aux_free, 1)
                if s in ("ln2_stats0", "ln2_stats1"):
                    dve.wait_ge(aux_free, value)
                    statistics("last", n, 0, post, k)
                if s in ("ln2_apply0", "ln2_apply1"):
                    apply("last", n, 0, post, k, ln2_applied)
                if s in ("w20", "w21"):
                    dve.wait_ge(aux_ready, value)
                    dve.wait_ge(x2b_done, n * 1 + 1)
                    nc.vector.tensor_tensor(flat(post[:, tiles, :]), aux, flat(post[:, tiles, :]), ALU.add)\
                        .then_inc(aux_free, 1)
                if s in ("ln3_stats0", "ln3_stats1"):
                    dve.wait_ge(aux_free, value)
                    statistics("last", n, 1, post, k)
                if s in ("ln3_apply0", "ln3_apply1"):
                    apply("last", n, 1, post, k, ln3_applied)

            def low_unit(bt, u):
                U = bt * UNITS + u
                hold(s_ready, U + 1)
                nc.vector.tensor_tensor_reduce(scores[u % 2], scores[u % 2], off[:, u // H, :], 1.0, -3.0e38, ALU.add,
                                               ALU.max, top[:, u:u + 1]).then_inc(low_done, 1)

            def evac_lo(bt, u):
                q, i, h = u // QU, u % QU // H, u % H
                dve.wait_ge(tlo_ready, bt * UNITS + u + 1)
                g = bt * (T // QT) + q
                if u % QU == 0 and (not isinstance(g, int) or g >= 2):
                    dve.wait_ge(av_done, g - 1)
                nc.vector.tensor_copy(pt[:, q % 2, 0:HT, h, P * i:P * (i + 1)],
                                      banks[:, BANK_T, :].rearrange("p (t n) -> p t n", t=HT)).then_inc(ptlo_done, 1)

            def bias_unit(bt, u):
                dve.wait_ge(low_done, bt * UNITS + u + 1)
                nc.vector.tensor_scalar(ntop[:, u:u + 1], top[:, u:u + 1], -SCALE, None, ALU.mult).then_inc(ntop_done, 1)

            value = 0
            for s in PREP:
                value += s in BANKED
                step(s, 0, value)

            def body(bt, par, bk):
                table, order = beside(bk)
                seen = [base(bt)]

                def aside(half, u):
                    for s in table[u][half]:
                        if s in BANKED:
                            seen[0] = base(bt) + order.index(s) + 1
                        step(s, bt + 1, seen[0]) if s not in POST2 else post_step(s, bt - 1, seen[0], 1 - par)

                for u in range(UNITS):
                    low_unit(bt, u)
                    bias_unit(bt, u)
                    aside(0, u)
                    if bk != 0 or u >= 2:
                        evac_lo(*late(bt, u, 2))
                    aside(1, u)

            batches(dve, body)
            for u in (UNITS - 2, UNITS - 1):
                evac_lo(B - 1, u)
            value = base(B - 1) + PER // 2
            for s in POST:
                value += s in BANKED
                post_step(s, B - 1, value, (B - 1) % 2)

        @block.tensor
        def _(pe):
            pe.wait_ge(consts_in, 16 * NV)

            def turn(src, k, nodes_in_rows):
                for q in range(HT):
                    t = HT * k + q
                    tile = src[:, t, :] if nodes_in_rows else src[:, P * t:P * (t + 1)]
                    ins = nc.tensor.transpose(aux[:, P * q:P * (q + 1)], tile, ident[:, :])
                return ins

            def times(w, k):
                for q in range(HT):
                    t = HT * k + q
                    ins = nc.tensor.matmul(aux[:, P * q:P * (q + 1)], fT[:, P * t:P * (t + 1)], w, start=True, stop=True)
                return ins

            def bank_free(value):
                if not isinstance(value, int) or value > 1:
                    pe.wait_ge(aux_free, value - 1)

            def convolve(t):
                q = t % HT
                for j in range(T):
                    for part in range(3):
                        ins = nc.tensor.matmul(aux[:, P * q:P * (q + 1)], adjT[:, j, P * t:P * (t + 1)], gparts[part][:, j, :],
                                               start=(j == 0 and part == 0), stop=(j == T - 1 and part == 2))
                return ins

            def step(s, n, par, value):
                k = int(s[-1]) if s in BANKED else 0
                if s in BANKED and s not in ("ag0", "ag1"):
                    bank_free(value)
                if s in ("ag0a", "ag1a"):
                    bank_free(value + 1)
                    if s == "ag0a":
                        pe.wait_ge(glo_done, n * 1 + 1)
                    pe.sem_inc(held_pe, 1)
                    k = int(s[2])
                    for t in (HT * k, HT * k + 1):
                        convolve(t)
                if s in ("ag0", "ag1"):
                    for t in (HT * k + 2, HT * k + 3):
                        ins = convolve(t)
                if s in ("h1t0", "h1t1"):
                    if k == 0:
                        pe.wait_ge(h1_done, n * 2 + 2)
                    ins = turn(h1x, k, True)
                if s in ("g0", "g1"):
                    ins = times(wts["c"][:, :], k)
                if s in ("x1t0", "x1t1"):
                    if k == 0:
                        pe.wait_ge(x1_done, n * 1 + 1)
                    ins = turn(h1x, k, True)
                if s in ("q0", "q1", "k0", "k1"):
                    ins = nc.tensor.matmul(aux, wts[s[0]][:, :], fT[:, HALF * k:HALF * (k + 1)], start=True, stop=True)
                if s in ("v0", "v1"):
                    ins = times(wts["v"][:, :], k)
                if s in BANKED:
                    ins.then_inc(aux_ready, 1)

            def post_step(s, n, value):
                if s not in BANKED:
                    return
                k = int(s[-1])
                bank_free(value)
                if s in ("or0", "or1"):
                    if k == 0:
                        pe.wait_ge(oT_done, (n + 1) * (T // QT))
                    ins = turn(oT, k, False)
                if s in ("ot0", "ot1"):
                    ins = turn(post, k, True)
                if s in ("wo0", "wo1"):
                    ins = times(wts["o"][:, :], k)
                if s in ("x2t0", "x2t1"):
                    if k == 0:
                        pe.wait_ge(ln2_affine, n * 2 + 2)
                    ins = turn(post, k, True)
                if s in ("w10", "w11", "w12", "w13"):
                    c, half = k // 2, k % 2
                    ins = nc.tensor.matmul(aux, w1_sb[:, P * c:P * (c + 1)], fT[:, HALF * half:HALF * (half + 1)],
                                           start=True, stop=True)
                if s in ("w20", "w21"):
                    if k == 0:
                        pe.wait_ge(gelu_done, n * 1 + 1)
                    for q in range(HT):
                        t = HT * k + q
                        for c in range(HC):
                            ins = nc.tensor.matmul(aux[:, P * q:P * (q + 1)], hidT[:, N * c + P * t:N * c + P * (t + 1)],
                                                   w2_sb[:, c, :], start=(c == 0), stop=(c == HC - 1))
                ins.then_inc(aux_ready, 1)

            def scores_unit(bt, u, par):
                U = bt * UNITS + u
                i, h = u // H, u % H
                if not isinstance(U, int) or U >= 2:
                    pe.wait_ge(exp_done, U - 1)
                for stack, first in ((k1s, True), (k2s, False)):
                    for k in range(2):
                        ins = nc.tensor.matmul(scores[u % 2][:, HALF * k:HALF * (k + 1)], qs[:, par, h, P * i:P * (i + 1)],
                                               stack[:, par, h, HALF * k:HALF * (k + 1)], start=first, stop=not first)
                ins.then_inc(s_ready, 1)

            def transpose_unit(bt, u):
                U = bt * UNITS + u
                pe.wait_ge(exp_done, U + 1)
                for half, (free, ready) in enumerate(((ptlo_done, tlo_ready), (pthi_done, thi_ready))):
                    if not isinstance(U, int) or U >= 1:
                        pe.wait_ge(free, U * 1)
                    for q in range(HT):
                        t = HT * half + q
                        ins = nc.tensor.transpose(banks[:, BANK_T + half, P * q:P * (q + 1)],
                                                  prob[:, u % 2, P * t:P * (t + 1)], ident[:, :])
                    ins.then_inc(ready, 1)

            def values_half(bt, q, par, half):
                g = bt * (T // QT) + q
                if half == 0:
                    pe.wait_ge(ptlo_done, bt * UNITS + (q + 1) * QU)
                    pe.wait_ge(pthi_done, bt * UNITS + (q + 1) * QU)
                    if not isinstance(g, int) or g >= 1:
                        pe.wait_ge(oT_done, g * 1)
                for j in range(HT * half, HT * (half + 1)):
                    for h in range(H):
                        ins = nc.tensor.matmul(banks[HD * h:HD * (h + 1), BANK_O, 0:QN], vrow[:, par, j, HD * h:HD * (h + 1)],
                                               pt[:, q % 2, j, h, :], start=(j == 0), stop=(j == T - 1),
                                               tile_position=(0, HD * h))
                if half == 1:
                    ins.then_inc(av_done, 1)

            pe.wait_ge(zero_done, 2)
            value = 0
            for s in PREP:
                value += s in BANKED
                step(s, 0, 0, value)

            def body(bt, par, bk):
                table, order = beside(bk)

                def aside(half, u):
                    for s in table[u][half]:
                        if s in BANKED or s in ("ag0a", "ag1a"):
                            value = base(bt) + order.index(s) + 1 if s in BANKED else base(bt) + order.index(s[:3])
                            step(s, bt + 1, 1 - par, value) if s not in POST2 else post_step(s, bt - 1, value)

                for u in range(UNITS):
                    if u == 0:
                        pe.wait_ge(stack_in, (bt + 1) * STACKED)
                        pe.wait_ge(aux_free, base(bt))
                    scores_unit(bt, u, par)
                    aside(0, u)
                    if bk != 0 or u >= 2:
                        transpose_unit(*late(bt, u, 2))
                    for half, at in enumerate(AV_AT):
                        found = quarters(u, at)
                        if found and not (found[1] and bk == 0):
                            q, ago = found
                            values_half(bt - ago, q, par if ago == 0 else 1 - par, half)
                    aside(1, u)

            batches(pe, body)
            for u in (UNITS - 2, UNITS - 1):
                transpose_unit(B - 1, u)
            for half in range(2):
                values_half(B - 1, T // QT - 1, (B - 1) % 2, half)
            value = base(B - 1) + PER // 2
            for s in POST:
                value += s in BANKED
                post_step(s, B - 1, value)


_INS = ["x", "adj", "L0_gnn_W", "L0_gnn_b_lin", "L0_gnn_b", "L1_gnn_Wc", "L1_gnn_bc", "L1_gnn_g1", "L1_gnn_be1", "L1_gnn_Wq",
        "L1_gnn_Wk", "L1_gnn_Wv", "L1_gnn_Wo", "L1_gnn_bo", "L1_gnn_g2", "L1_gnn_be2", "L1_gnn_W1", "L1_gnn_b1", "L1_gnn_W2",
        "L1_gnn_b2", "L1_gnn_g3", "L1_gnn_be3"]


def kernel(**inputs):
    import numpy as _np
    import concourse.bacc as _bacc
    from concourse import mybir as _mybir
    from concourse.bass_utils import run_bass_kernel_spmd as _run

    nc = _bacc.Bacc("TRN2", target_bir_lowering=False, num_devices=1)
    arrays, args = {}, []
    for name in _INS:
        a = _np.ascontiguousarray(inputs[name])
        arrays[f"in_{name}"] = a
        args.append(nc.dram_tensor(f"in_{name}", a.shape, _mybir.dt.from_np(a.dtype), kind="ExternalInput").ap())
    out = nc.dram_tensor("out_x", (B, N, D), F32, kind="ExternalOutput").ap()
    build(nc, *args, out)
    r = _run(nc, [arrays], core_ids=[0])
    return r.results[0]["out_x"]
```

```python
from contextlib import ExitStack

import concourse.bass as bass
from concourse import mybir

F32 = mybir.dt.float32
BF16 = mybir.dt.bfloat16
FP8 = mybir.dt.float8e4
ALU = mybir.AluOpType
ACT = mybir.ActivationFunctionType
AX = mybir.AxisListType

P = 128
B, N, D, H = 8, 1024, 128, 4
T = N // P
HALF = N // 2
HT = T // 2
HD = D // H
HID = 2 * D
HC = HID // P
EPS = 1e-5
FAR = 2.0 ** 100
TINY = 1e-30
GROUP = 4

BANK_T, BANK_O, BANK_AUX = 4, 6, 7

AUX1 = {1: ([], ["pw0"]), 2: ([], ["ot0"]), 3: ([], ["pw1"]), 4: (["h0T0"], ["h0T1"]), 5: (["hT0"], ["hT1"]),
        6: (["hrow0"], ["norm"]), 7: (["ot1"], ["hrow1"])}
LN_AT = (0, 1)
SCALE_AT = 2
XB_AT = 4
RELU_AT = (3, 3)
AUX1_LAST = {0: ([], ["pw0", "ln1_stats0"]), 1: (["ln1_stats1"], ["pw1"]), 2: (["ot0"], ["norm", "ln1_relu0"]),
             3: (["ln1_relu1"], ["last"]), 4: (["h1t0"], ["h1t1", "nd"]), 5: (["g0"], ["g1", "gsplit"]),
             6: (["ot1"], ["gmid"]), 7: ([], ["ag0a"])}
TAIL1 = ["attn0", "ag0", "ag1a", "ag1", "attn1", "lng_stats0", "lng_stats1", "fo0", "lng_apply0", "lng_apply1", "fo1",
         "lng_relu", "x1t0", "x1t1", "q0", "q1", "qstack", "v0", "v1", "k0", "k1", "kstack"]
PREP1 = ["h0T0", "h0T1", "hT0", "hT1", "hrow0", "hrow1"]


def aux_list(table, first, post):
    return [s for u in sorted(table) for half in table[u] for s in half
            if not (first and s in post)]


def bc(ap, n):
    return ap.rearrange("p (k o) -> p k o", o=1).to_broadcast([ap.shape[0], ap.shape[1], n])


def build(nc, x, adj, W, b_lin, b, Wc, bcv, g1, be1, Wq, Wk, Wv, Wo, bo, g2, be2, W1, b1, W2, b2, g3, be3, out):
    x1_dram = nc.dram_tensor("after_block1", (B, N, D), F32, kind="Internal").ap()
    parts_dram = nc.dram_tensor("parts_of_q_and_k", (2, 3, D, N), BF16, kind="Internal").ap()
    kept_dram = nc.dram_tensor("x1_of_two_batches", (2, N, D), F32, kind="Internal").ap()
    with ExitStack() as ctx:
        sb = lambda n, s, d: ctx.enter_context(nc.sbuf_tensor(n, s, d))
        banks = ctx.enter_context(nc.psum_tensor("banks", [P, 8, HALF], F32))
        shared = {
            "ident": sb("ident", [P, P], F32),
            "neg_half": sb("neg_half", [P, T], F32),
            "adjT": sb("adjT", [P, T, N], FP8),
            "off": sb("off", [P, T, N], BF16),
            "two_over_lam": sb("two_over_lam", [P, 1], F32),
        }
        prep = prep_buffers(sb, lambda n: ctx.enter_context(nc.semaphore(n)))
        weights = dict(c=Wc, q=Wq, k=Wk, v=Wv, o=Wo, bc=bcv, g1=g1, be1=be1, bo=bo, g2=g2, be2=be2, W1=W1, b1=b1, W2=W2,
                       b2=b2, g3=g3, be3=be3)
        block1(nc, x, adj, W, b_lin, b, weights, x1_dram, parts_dram, kept_dram, banks, shared, prep)
        block2(nc, x1_dram, parts_dram, kept_dram, out, banks, shared, prep)


def arrivals(bt, par):
    return (bt // 2 + 1 if isinstance(bt, int) else (bt - par) // 2 + 1) * 16


def rows(ap):
    return ap.rearrange("(t p) d -> p t d", p=P)


def across(vec):
    return vec.rearrange("(o n) -> o n", o=1).to_broadcast([P, vec.shape[0]])


BESIDE = {
    0: (["ln1_stats0"], []), 1: ([], ["ln1_stats1"]), 3: (["ln1_relu0"], ["ln1_relu1"]), 4: ([], ["h1t0"]),
    5: (["h1t1"], ["x1b"]), 6: (["g0"], ["g1", "or0", "gsplit", "or1"]), 7: ([], ["ot0"]),
    8: (["ot1"], ["wo0", "gmid"]), 10: (["wo1"], ["ln2_stats0", "ln2_stats1"]), 11: (["ag0a"], []),
    12: (["ag0"], ["ln2_apply0"]), 13: ([], ["ag1a", "ln2_apply1", "ag1"]), 15: (["lng_stats0"], ["x2t0"]),
    16: (["lng_stats1", "x2t1"], ["w10"]), 17: (["w11"], ["lng_apply0", "lng_apply1"]), 18: ([], ["w12"]),
    19: (["w13"], ["lng_relu", "keep"]), 20: (["gelu"], []), 21: (["w20"], ["w21"]),
    22: (["x1t0"], ["x1t1", "ln3_stats0"]), 23: (["q0"], ["q1", "qstack"]), 24: (["v0"], ["ln3_stats1", "v1"]),
    25: (["k0"], ["k1", "kstack"]), 27: ([], ["ln3_apply0"]), 28: (["ln3_apply1"], []),
}
POST2 = ("x1b", "or0", "or1", "ot0", "ot1", "wo0", "wo1", "ln2_stats0", "ln2_stats1", "ln2_apply0", "ln2_apply1", "x2t0", "x2t1",
         "w10", "w11", "w12", "w13", "gelu", "w20", "w21", "ln3_stats0", "ln3_stats1", "ln3_apply0", "ln3_apply1")
BANKED = ("h1t0", "h1t1", "g0", "g1", "ag0", "ag1", "x1t0", "x1t1", "q0", "q1", "k0", "k1", "v0", "v1",
          "or0", "or1", "ot0", "ot1", "wo0", "wo1", "x2t0", "x2t1", "w10", "w11", "w12", "w13", "w20", "w21")
PREP2 = [s for u in sorted(BESIDE) for half in BESIDE[u] for s in half if s not in POST2]
UNITS = T * H
QT = 2
QN = QT * P
QU = QT * H
AV_AT = (10, 12)
LO_BY_SCALAR = (1, 9, 12, 14, 23, 25, 26, 27, 28, 29, 30, 31)
COPY_AT = 12
SLOTS = (((0, 0, 1, 2),), ((0, 2, 0, 0), (1, None, 1, 1)))
STACKED = 16 * sum(part is not None for stacks in SLOTS for slots in stacks for part in slots)
NV = 5 + 2 + HC + 9


def norm_buffers(c, sb, sem):
    return dict(stats=sb("stats_" + c, [P, T, 6], F32), mv=sb("mv_" + c, [P, T, 2], F32), ve=sb("ve_" + c, [P, T], F32),
                nm=sb("nm_" + c, [P, T], F32), rstd=sb("rstd_" + c, [P, T], F32), nmr=sb("nmr_" + c, [P, T], F32),
                stats_done=sem("stats_done_" + c), mv_done=sem("mv_done_" + c), ve_done=sem("ve_done_" + c),
                rstd_done=sem("rstd_done_" + c))


PREP_NAMES = (
    "vrow", "hid", "h1x", "parts", "work", "fT", "wts", "w1_sb", "w2_sb", "b1_col", "vecs", "ln", "weights_in",
    "x_in", "stack_in", "parts_out", "h1_done", "nmr_done", "ghi_done", "grem_done", "gmid_done", "glo_done",
    "gb_done", "lng_applied", "lng_affine", "x1_done", "x1_kept", "hi_done", "rem_done", "mid_done", "res_done",
    "lo_done")


def prep_views(work, vecs):
    rem = work[:, 0, :]
    gf = work[:, 1, :].rearrange("p (t d) -> p t d", t=T)
    flat = lambda a: a.rearrange("p t d -> p (t d)")
    rows_b = lambda n, t=T: vecs[n][:, :].rearrange("p (o d) -> p o d", o=1).to_broadcast([P, t, D])
    return rem, gf, flat, rows_b


def prep_buffers(sb, sem):
    vrow = sb("vrow", [P, 2, T, D], F32)
    hid = sb("hid", [P, 2, N], F32)
    h1x = sb("h1x", [P, T, D], F32)
    parts = sb("parts", [P, 6, N], BF16)
    work = sb("work", [P, 2, N], F32)
    fT = sb("fT", [P, N], F32)
    wts = {n: sb("w_" + n, [P, D], F32) for n in ("c", "q", "k", "v", "o")}
    w1_sb = sb("w1_sb", [P, HID], F32)
    w2_sb = sb("w2_sb", [P, HC, D], F32)
    b1_col = sb("b1_col", [P, HC], F32)
    vecs = {n: sb("v_" + n, [P, D], F32) for n in ("bc", "g1", "be1", "bo", "g2", "be2", "b2", "g3", "be3")}
    ln = {"next": norm_buffers("next", sb, sem)}
    weights_in = sem("consts_in2")
    x_in = sem("x_in2")
    stack_in = sem("stack_in")
    parts_out = sem("parts_out")
    h1_done = sem("h1_done")
    nmr_done = sem("nmr_done")
    ghi_done = sem("ghi_done")
    grem_done = sem("grem_done")
    gmid_done = sem("gmid_done")
    glo_done = sem("glo_done")
    gb_done = sem("gb_done")
    lng_applied = sem("lng_applied")
    lng_affine = sem("lng_affine")
    x1_done = sem("x1_done")
    x1_kept = sem("x1_kept")
    hi_done = sem("hi_done")
    rem_done = sem("rem_done")
    mid_done = sem("mid_done")
    res_done = sem("res_done")
    lo_done = sem("lo_done")
    return dict(zip(PREP_NAMES, (
        vrow, hid, h1x, parts, work, fT, wts, w1_sb, w2_sb, b1_col, vecs, ln, weights_in, x_in, stack_in,
        parts_out, h1_done, nmr_done, ghi_done, grem_done, gmid_done, glo_done, gb_done, lng_applied,
        lng_affine, x1_done, x1_kept, hi_done, rem_done, mid_done, res_done, lo_done)))


def one(dram, n):
    return rows(dram[n] if isinstance(n, int) else dram[bass.ds(n, 1)].rearrange("o n d -> (o n) d"))


class Preparation:

    def __init__(self, nc, banks, shared, prep, aux_ready, aux_free, held_pool, held_dve, held_pe):
        neg_half, adjT, two_over_lam, ident = (shared[k] for k in ("neg_half", "adjT", "two_over_lam", "ident"))
        (vrow, hid, h1x, parts, work, fT, wts, w1_sb, w2_sb, b1_col, vecs, ln, weights_in, x_in, stack_in,
         parts_out, h1_done, nmr_done, ghi_done, grem_done, gmid_done, glo_done, gb_done, lng_applied,
         lng_affine, x1_done, x1_kept, hi_done, rem_done, mid_done, res_done, lo_done) = (
            prep[k] for k in PREP_NAMES)
        aux = banks[:, BANK_AUX, :]
        rem, gf, flat, rows_b = prep_views(work, vecs)
        gparts = [parts[:, k, :].rearrange("p (t d) -> p t d", t=T) for k in range(3)]

        def bank_of(s, n):
            spare = isinstance(n, int) and n == 0 and s in ("x1t1", "q1", "k1", "v1")
            return banks[:, 0, :] if spare else aux

        def hold(s, value):
            nc.gpsimd.wait_ge(s, value)
            nc.gpsimd.sem_inc(held_pool, 1)

        def scale(c, n, k):
            L = ln[c]
            i = n * 2 + k
            hold(L["mv_done"], i + 1)
            if c == "next" and k == 1:
                hold(h1_done, n * 2 + 2)
            nc.gpsimd.tensor_scalar(L["ve"][:, :], L["mv"][:, :, 1], 1.0, EPS, ALU.mult, ALU.add).then_inc(L["ve_done"], 1)
            nc.gpsimd.tensor_scalar(L["nm"][:, :], L["mv"][:, :, 0], -1.0, 0.0, ALU.mult, ALU.add).then_inc(L["ve_done"], 1)
            hold(L["ve_done"], i * 2 + 2)
            nc.gpsimd.tensor_tensor(L["rstd"][:, :], L["ve"][:, :], neg_half[:, :], ALU.pow).then_inc(L["rstd_done"], 1)

        def pool_step(s, n, par):
            if isinstance(n, int) and n == 0 and s in ("lng_apply1", "q1", "k1"):
                return
            if s == "ln1_stats1":
                scale("next", n, 0)
                L = ln["next"]
                hold(L["rstd_done"], n * 2 + 1)
                nc.gpsimd.tensor_tensor(L["nmr"][:, :], L["nm"][:, :], L["rstd"][:, :], ALU.mult).then_inc(nmr_done, 1)
            if s == "gsplit":
                hold(ghi_done, n * 1 + 1)
                if not isinstance(n, int) or n > 0:
                    hold(lo_done, n * 2)
                nc.gpsimd.tensor_tensor(rem, flat(gf), parts[:, 0, :], ALU.subtract).then_inc(grem_done, 1)
            if s == "gmid":
                hold(gmid_done, n * 1 + 1)
                nc.gpsimd.tensor_tensor(parts[:, 2, :], rem, parts[:, 1, :], ALU.subtract).then_inc(glo_done, 1)
                nc.gpsimd.tensor_tensor(gf, gf, rows_b("bc"), ALU.subtract).then_inc(gb_done, 1)
            if s == "lng_stats1":
                scale("next", n, 1)
            if s == "lng_apply1":
                hold(lng_applied, n * 1 + 1)
                nc.gpsimd.tensor_tensor(gf, gf, rows_b("g1"), ALU.mult).then_inc(lng_affine, 1)
                hold(lng_affine, n * 2 + 1)
                nc.gpsimd.tensor_tensor(gf, gf, rows_b("be1"), ALU.add).then_inc(lng_affine, 1)
            if s in ("q1", "k1"):
                k = "qk".index(s[0])
                at = 3 * k
                hold(rem_done, n * 4 + 2 * k + 2)
                nc.gpsimd.tensor_scalar(parts[:, at + 1, :], rem, 1.0, 0.0, ALU.mult, ALU.add).then_inc(mid_done, 1)
                hold(mid_done, n * 2 + k + 1)
                nc.gpsimd.tensor_tensor(parts[:, at + 2, :], rem, parts[:, at + 1, :], ALU.subtract)\
                    .then_inc(lo_done, 1)

        def act_step(s, n, par, value):
            bank = bank_of(s, n)
            k = int(s[-1]) if s in BANKED else 0
            cols = slice(HALF * k, HALF * (k + 1))
            tiles = slice(HT * k, HT * (k + 1))
            if s in ("ln1_relu0", "ln1_relu1"):
                nc.scalar.wait_ge(nmr_done, n * 1 + 1)
                L = ln["next"]
                half = int(s[-1])
                for t in range(HT * half, HT * (half + 1)):
                    ins = nc.scalar.activation(h1x[:, t, :], h1x[:, t, :], ACT.Relu, bias=L["nmr"][:, t:t + 1],
                                               scale=L["rstd"][:, t:t + 1])
                ins.then_inc(h1_done, 1)
            if s in ("h1t0", "h1t1", "x1t0", "x1t1"):
                nc.scalar.wait_ge(aux_ready, value)
                nc.scalar.activation(fT[:, cols], bank, ACT.Copy).then_inc(aux_free, 1)
            if s in ("g0", "g1"):
                nc.scalar.wait_ge(aux_ready, value)
                nc.scalar.activation(gf[:, tiles, :], bank.rearrange("p (t d) -> p t d", t=HT), ACT.Copy)\
                    .then_inc(aux_free, 1)
            if s in ("q0", "q1", "k0", "k1"):
                nc.scalar.wait_ge(aux_ready, value)
                nc.scalar.activation(parts[:, 3 * "qk".index(s[0]), cols], bank, ACT.Copy).then_inc(hi_done, 1)
            if s in ("v0", "v1"):
                nc.scalar.wait_ge(aux_ready, value)
                nc.scalar.activation(vrow[:, par, tiles, :], bank.rearrange("p (t d) -> p t d", t=HT), ACT.Copy)\
                    .then_inc(aux_free, 1)

        def hold_dve(s, value):
            nc.vector.wait_ge(s, value)
            nc.vector.sem_inc(held_dve, 1)

        def statistics(c, n, k, src, half):
            L = ln[c]
            i = n * 2 + k
            for t in range(HT * half, HT * (half + 1)):
                ins = nc.vector.bn_stats(L["stats"][:, t, :], src[:, t, :])
            if half == 0:
                return
            if c == "next" and k == 1:
                hold_dve(L["rstd_done"], i)
            ins.then_inc(L["stats_done"], 1)
            hold_dve(L["stats_done"], i + 1)
            for t in range(T):
                ins = nc.vector.bn_aggr(L["mv"][:, t, :], L["stats"][:, t, :])
            ins.then_inc(L["mv_done"], 1)

        def apply(c, n, k, rows_, half, done):
            L = ln[c]
            nc.vector.wait_ge(L["rstd_done"], n * 2 + k + 1)
            for t in range(HT * half, HT * (half + 1)):
                ins = nc.vector.tensor_scalar(rows_[:, t, :], rows_[:, t, :], L["nm"][:, t:t + 1], L["rstd"][:, t:t + 1],
                                              ALU.add, ALU.mult)
            if half == 1:
                ins.then_inc(done, 1)

        def dve_step(s, n, value):
            bank = bank_of(s, n)
            k = int(s[-1]) if s[-1] in "01" else 0
            cols = slice(HALF * k, HALF * (k + 1))
            tiles = slice(HT * k, HT * (k + 1))
            if s in ("ln1_stats0", "ln1_stats1"):
                nc.vector.wait_ge(x_in, n * 16 + 16)
                statistics("next", n, 0, h1x, k)
            if s == "gsplit":
                nc.vector.wait_ge(aux_free, value)
                if not isinstance(n, int) or n > 0:
                    nc.vector.wait_ge(stack_in, n * STACKED)
                nc.vector.tensor_copy(parts[:, 0, :], flat(gf)).then_inc(ghi_done, 1)
            if s == "gmid":
                nc.vector.wait_ge(grem_done, n * 1 + 1)
                nc.vector.tensor_copy(parts[:, 1, :], rem).then_inc(gmid_done, 1)
            if s in ("ag0", "ag1"):
                nc.vector.wait_ge(aux_ready, value)
                nc.vector.wait_ge(gb_done, n * 1 + 1)
                nc.vector.scalar_tensor_tensor(out=flat(gf[:, tiles, :]), in0=bank, scalar=two_over_lam[:, 0:1],
                                               in1=flat(gf[:, tiles, :]), op0=ALU.mult, op1=ALU.subtract)\
                    .then_inc(aux_free, 1)
            if s in ("lng_stats0", "lng_stats1"):
                nc.vector.wait_ge(aux_free, value)
                statistics("next", n, 1, gf, k)
            if s in ("lng_apply0", "lng_apply1"):
                apply("next", n, 1, gf, k, lng_applied)
                if isinstance(n, int) and n == 0 and k == 1:
                    nc.vector.wait_ge(lng_applied, 1)
                    nc.vector.tensor_tensor(gf, gf, rows_b("g1"), ALU.mult).then_inc(lng_affine, 1)
                    nc.vector.wait_ge(lng_affine, 1)
                    nc.vector.tensor_tensor(gf, gf, rows_b("be1"), ALU.add).then_inc(lng_affine, 1)
            if s == "lng_relu":
                nc.vector.wait_ge(lng_affine, n * 2 + 2)
                nc.vector.scalar_tensor_tensor(out=flat(h1x[:, :, :]), in0=flat(gf), scalar=0.0,
                                               in1=flat(h1x[:, :, :]), op0=ALU.max, op1=ALU.add).then_inc(x1_done, 1)
            if s in ("q0", "q1", "k0", "k1"):
                q = "qk".index(s[0])
                nc.vector.wait_ge(hi_done, n * 4 + 2 * q + k + 1)
                if q:
                    nc.vector.wait_ge(lo_done, n * 2 + 1)
                nc.vector.tensor_tensor(rem[:, cols], bank, parts[:, 3 * q, cols], ALU.subtract).then_inc(rem_done, 1)
                nc.vector.wait_ge(rem_done, n * 4 + 2 * q + k + 1)
                nc.vector.sem_inc(aux_free, 1)
                if isinstance(n, int) and n == 0 and k == 1:
                    nc.vector.tensor_copy(parts[:, 3 * q + 1, :], rem).then_inc(mid_done, 1)
                    nc.vector.wait_ge(mid_done, q + 1)
                    nc.vector.tensor_tensor(parts[:, 3 * q + 2, :], rem, parts[:, 3 * q + 1, :], ALU.subtract)\
                        .then_inc(lo_done, 1)

        def turn(src, k, nodes_in_rows, bank=aux):
            for q in range(HT):
                t = HT * k + q
                tile = src[:, t, :] if nodes_in_rows else src[:, P * t:P * (t + 1)]
                ins = nc.tensor.transpose(bank[:, P * q:P * (q + 1)], tile, ident[:, :])
            return ins

        def times(w, k, bank=aux):
            for q in range(HT):
                t = HT * k + q
                ins = nc.tensor.matmul(bank[:, P * q:P * (q + 1)], fT[:, P * t:P * (t + 1)], w, start=True, stop=True)
            return ins

        def bank_free(value):
            if not isinstance(value, int) or value > 1:
                nc.tensor.wait_ge(aux_free, value - 1)

        def convolve(t):
            q = t % HT
            for j in range(T):
                for part in range(3):
                    ins = nc.tensor.matmul(aux[:, P * q:P * (q + 1)], adjT[:, j, P * t:P * (t + 1)], gparts[part][:, j, :],
                                           start=(j == 0 and part == 0), stop=(j == T - 1 and part == 2))
            return ins

        def pe_step(s, n, par, value):
            bank = bank_of(s, n)
            k = int(s[-1]) if s in BANKED else 0
            if s in BANKED and s not in ("ag0", "ag1") and bank is aux:
                bank_free(value)
            if s in ("ag0a", "ag1a"):
                bank_free(value + 1)
                if s == "ag0a":
                    nc.tensor.wait_ge(glo_done, n * 1 + 1)
                nc.tensor.sem_inc(held_pe, 1)
                k = int(s[2])
                for t in (HT * k, HT * k + 1):
                    convolve(t)
            if s in ("ag0", "ag1"):
                for t in (HT * k + 2, HT * k + 3):
                    ins = convolve(t)
            if s in ("h1t0", "h1t1"):
                if k == 0:
                    nc.tensor.wait_ge(h1_done, n * 2 + 2)
                ins = turn(h1x, k, True, bank)
            if s in ("g0", "g1"):
                ins = times(wts["c"][:, :], k, bank)
            if s in ("x1t0", "x1t1"):
                if k == 0:
                    nc.tensor.wait_ge(x1_done, n * 1 + 1)
                ins = turn(h1x, k, True, bank)
            if s in ("q0", "q1", "k0", "k1"):
                ins = nc.tensor.matmul(bank, wts[s[0]][:, :], fT[:, HALF * k:HALF * (k + 1)], start=True, stop=True)
            if s in ("v0", "v1"):
                ins = times(wts["v"][:, :], k, bank)
            if s in BANKED:
                ins.then_inc(aux_ready, 1)

        self.scale, self.pool_step, self.act_step = scale, pool_step, act_step
        self.statistics, self.apply, self.dve_step = statistics, apply, dve_step
        self.turn, self.times, self.bank_free, self.pe_step = turn, times, bank_free, pe_step


def block1(nc, x, adj, W, b_lin, b, weights, x1_dram, parts_dram, kept_dram, banks, shared, prep):
    with ExitStack() as ctx:
        sb = lambda n, s, d: ctx.enter_context(nc.sbuf_tensor(n, s, d))
        sem = lambda n: ctx.enter_context(nc.semaphore(n))
        ident, neg_half, adjT, off, two_over_lam = (shared[k] for k in (
            "ident", "neg_half", "adjT", "off", "two_over_lam"))

        pt = sb("pt", [P, 2, T, HALF], F32)
        adj_f = pt[:, :, :, :].rearrange("p g t n -> p (g t n)").rearrange("p (t n) -> p t n", t=T)
        sym = sb("sym", [P, T, N], BF16)
        ones = sb("ones", [P, P], F32)
        identb = sb("identb", [P, P], BF16)
        (vrow, hid, h1x, parts, work, fT, wts, w1_sb, w2_sb, b1_col, vecs, ln, weights_in, x_in2, stack_in,
         parts_out, *_, x1_done, x1_kept, _, _, _, _, lo_done) = (prep[k] for k in PREP_NAMES)
        w_sb = sb("w_sb", [P, D], F32)
        blin_col = sb("blin_col", [P, 1], F32)
        b_row = sb("b_row", [P, D], F32)
        xin = sb("xin", [P, 2, T, D], F32)
        xb = sb("xb", [P, 2, T, D], F32)
        xn = sb("xn", [P, T, D], F32)
        h0 = sb("h0", [P, T, D], F32)
        h0T = sb("h0T", [P, N], F32)
        hT = sb("hT", [P, 2, N], F32)
        hrow = sb("hrow", [P, 2, T, D], F32)
        z = sb("z", [P, 2, N], BF16)
        prob = sb("prob", [P, 2, N], F32)
        top = sb("top1", [P, T], F32)
        nmax = sb("nmax", [P, T], F32)
        den = sb("den", [P, 2, T], F32)
        rden = sb("rden", [P, T], F32)
        oT = sb("oT", [P, N], F32)
        stats = sb("stats", [P, T, 6], F32)
        mv = sb("mv", [P, T, 2], F32)
        ve = sb("ve", [P, T], F32)
        rstd = sb("rstd", [P, T], F32)
        nm = sb("nm", [P, T], F32)
        nmr = sb("nmr", [P, T], F32)
        v = sb("v", [P, T], F32)
        vsum = sb("vsum", [P, T], F32)
        y = sb("y", [P, T], F32)
        vr1 = sb("vr1", [P, T], F32)
        vr2 = sb("vr2", [P, T], F32)
        vp = sb("vp", [P, T, 3], BF16)
        tot = sb("tot", [P, 1], F32)
        tot2 = sb("tot2", [P, 1], F32)
        rtot = sb("rtot", [P, 1], F32)
        junk = sb("junk", [P, T], F32)
        junk2 = sb("junk2", [P, T], F32)
        nd = sb("nd", [P, 2], F32)
        fin = sb("fin", [P, 6], F32)

        consts_in = sem("consts_in")
        adj_in = [sem(f"adj_in{t}") for t in range(T)]
        x_in = [sem(f"x_in{k}") for k in range(2)]
        x1_out = sem("x1_out")
        zeroed = sem("zeroed")
        idents = sem("idents")
        adjT_ready = sem("adjT_ready")
        adjT_copied = sem("adjT_copied")
        adjT_copied2 = sem("adjT_copied2")
        sym_ready = sem("sym_ready")
        off_ready = sem("off_ready")
        stats_done = sem("stats_done")
        mv_done = sem("mv_done")
        ve_done = sem("ve_done")
        rstd_done = sem("rstd_done")
        h0_done = sem("h0_done")
        xb_done = sem("xb_done")
        aux_ready = sem("aux_ready")
        aux_free = sem("aux_free")
        s_ready = sem("s_ready")
        z_done = sem("z_done")
        zfar_done = sem("zfar_done")
        top_done = sem("top_done")
        max_done = sem("max_done")
        exp_done = sem("exp_done")
        tlo_ready = sem("tlo_ready")
        thi_ready = sem("thi_ready")
        ptlo_done = sem("ptlo_done")
        pthi_done = sem("pthi_done")
        av_done = sem("av_done")
        oT_done = sem("oT_done")
        rden_done = sem("rden_done")
        y_done = sem("y_done")
        tot_done = sem("tot_done")
        v_step = sem("v_step")
        v_ready = sem("v_ready")
        fin_step = sem("fin_step")
        lam_done = sem("lam_done")
        held_pool = sem("held_pool")
        held_dve = sem("held_dve")
        held_pe = sem("held_pe")
        held_sp = sem("held_sp")

        aux = banks[:, BANK_AUX, :]
        obank = banks[:, BANK_O, :]
        scores = [banks[:, 2 * k:2 * k + 2, :].rearrange("p a n -> p (a n)") for k in range(2)]

        PER = 11
        PW = 2
        SYM_POOL = 3
        VSTEPS = 5 * PW + 1

        def lists(bk):
            if bk == B - 1:
                steps = [s for u in range(T) for half in AUX1_LAST[u] for s in half] + TAIL1
                banked = [s for s in steps if (s in BANKED and s not in POST2)
                          or s in ("pw0", "pw1", "norm", "last", "nd", "ot0", "ot1", "fo0", "fo1")]
                return AUX1_LAST, banked
            order = aux_list(AUX1, bk == 0, ("ot0", "ot1"))
            return {u: [[s for s in half if s in order] for half in AUX1.get(u, ([], []))] for u in range(T)}, order

        def base(bt):
            if isinstance(bt, int):
                return 6 if bt == 0 else 4 + PER * bt
            return bt * PER + 4

        def batches(eng, body):
            body(0, 0, 0)
            with eng.Fori(0, (B - 2) // 2) as i:
                for k in (1, 2):
                    body(i * 2 + k, k % 2, None)
            body(B - 1, (B - 1) % 2, B - 1)

        P2 = Preparation(nc, banks, shared, prep, aux_ready, aux_free, held_pool, held_dve, held_pe)

        block = ctx.enter_context(nc.Block())

        @block.sync
        def _(sp):
            def hold(s, value):
                sp.wait_ge(s, value)
                sp.sem_inc(held_sp, 1)

            sp.sem_inc(x1_out, 16)
            sp.dma_start(xin[:, 0], rows(x[0])).then_inc(x_in[0], 16)
            sp.dma_start(w_sb[:, :], W).then_inc(consts_in, 16)
            sp.dma_start(blin_col[:, :], b_lin.rearrange("(d o) -> d o", o=1)).then_inc(consts_in, 16)
            sp.dma_start(b_row[:, :], across(b)).then_inc(consts_in, 16)
            for t in range(T):
                sp.dma_start(adj_f[:, t, :], adj[P * t:P * (t + 1), :]).then_inc(adj_in[t], 16)
            sp.dma_start(xin[:, 1], rows(x[1])).then_inc(x_in[1], 16)
            for n in "cqkvo":
                sp.dma_start(wts[n][:, :], weights[n]).then_inc(weights_in, 16)
            sp.dma_start(w1_sb[:, :], weights["W1"]).then_inc(weights_in, 16)
            sp.dma_start(w2_sb[:, :, :], weights["W2"].rearrange("(c p) d -> p c d", p=P)).then_inc(weights_in, 16)
            for c in range(HC):
                sp.dma_start(b1_col[:, c:c + 1], weights["b1"][P * c:P * (c + 1)].rearrange("(p o) -> p o", o=1))\
                    .then_inc(weights_in, 16)
            for n in vecs:
                sp.dma_start(vecs[n][:, :], across(weights[n])).then_inc(weights_in, 16)

            def body(bt, par, bk):
                if bk != 0:
                    pieces, order = lists(bk)
                    hold(aux_free, base(bt) + order.index("ot1") + 1)
                    sp.dma_start(rows(x1_dram[bt - 1] if isinstance(bt, int) else
                                      x1_dram[bass.ds(bt - 1, 1)].rearrange("o n d -> (o n) d")),
                                 xn[:, :, :]).then_inc(x1_out, 16)

            def load(bt, par):
                hold(h0_done, bt * 2)
                hold(xb_done, bt * 1)
                sp.dma_start(xin[:, 1 - par], rows(x[bt + 1] if isinstance(bt, int) else
                             x[bass.ds(bt + 1, 1)].rearrange("o n d -> (o n) d"))).then_inc(x_in[1 - par], 16)

            with sp.Fori(0, (B - 2) // 2) as i:
                for k in (1, 2):
                    load(i * 2 + k, k % 2)
                    body(i * 2 + k, k % 2, None)
            sp.wait_ge(x1_out, 16 * (B - 1))
            sp.dma_start(h1x[:, :, :], one(x1_dram, 0)).then_inc(x_in2, 16)
            body(B - 1, (B - 1) % 2, B - 1)
            _, order = lists(B - 1)
            sp.wait_ge(aux_free, base(B - 1) + order.index("fo1") + 1)
            sp.dma_start(rows(x1_dram[B - 1]), xn[:, :, :]).then_inc(x1_out, 16)
            sp.wait_ge(x1_done, 1)
            sp.dma_start(rows(kept_dram[0]), h1x[:, :, :]).then_inc(x1_kept, 16)
            for k in range(2):
                sp.wait_ge(lo_done, k + 1)
                if k == 1:
                    sp.wait_ge(parts_out, 16)
                sp.dma_start(parts_dram[k].rearrange("a p n -> p a n"), parts[:, 3 * k:3 * k + 3, :]).then_inc(parts_out, 16)
            sp.wait_ge(x1_kept, 16)
            sp.wait_ge(x1_out, 16 * (B + 1))

        @block.gpsimd
        def _(pool):
            for m in (ident, identb):
                nc.gpsimd.memset(m[:, :], 0.0).then_inc(zeroed, 1)
            nc.gpsimd.memset(ones[:, :], 1.0).then_inc(zeroed, 1)
            nc.gpsimd.memset(neg_half[:, :], -0.5).then_inc(zeroed, 1)
            nc.gpsimd.memset(v[:, :], 1.0 / N).then_inc(zeroed, 1)
            pool.wait_ge(zeroed, 5)
            for m in (ident, identb):
                nc.gpsimd.affine_select(out=m[:, :], in_=m[:, :], compare_op=ALU.not_equal, fill=1.0, base=0,
                                        pattern=[[-1, P]], channel_multiplier=1).then_inc(idents, 1)

            def hold(s, value):
                pool.wait_ge(s, value)
                pool.sem_inc(held_pool, 1)

            def split_v(n, m):
                if m is not None:
                    hold(v_step, n)
                nc.gpsimd.tensor_scalar(vp[:, :, 0], v[:, :], 1.0, 0.0, ALU.mult, ALU.add).then_inc(v_step, 1)
                hold(v_step, n + 1)
                nc.gpsimd.tensor_tensor(vr1[:, :], v[:, :], vp[:, :, 0], ALU.subtract).then_inc(v_step, 1)
                hold(v_step, n + 2)
                nc.gpsimd.tensor_scalar(vp[:, :, 1], vr1[:, :], 1.0, 0.0, ALU.mult, ALU.add).then_inc(v_step, 1)
                hold(v_step, n + 3)
                nc.gpsimd.tensor_tensor(vp[:, :, 2], vr1[:, :], vp[:, :, 1], ALU.subtract).then_inc(v_step, 1)
                hold(v_step, n + 4)
                pool.sem_inc(v_ready, 1)

            def ln_scale(n):
                hold(mv_done, n * 1 + 1)
                nc.gpsimd.tensor_scalar(ve[:, :], mv[:, :, 1], 1.0, EPS, ALU.mult, ALU.add).then_inc(ve_done, 1)
                nc.gpsimd.tensor_scalar(nm[:, :], mv[:, :, 0], -1.0, 0.0, ALU.mult, ALU.add).then_inc(ve_done, 1)
                hold(ve_done, n * 2 + 2)
                if not isinstance(n, int) or n > 0:
                    hold(h0_done, n * 2)
                nc.gpsimd.tensor_tensor(rstd[:, :], ve[:, :], neg_half[:, :], ALU.pow).then_inc(rstd_done, 1)
                hold(rstd_done, n * 2 + 1)
                nc.gpsimd.tensor_tensor(nmr[:, :], nm[:, :], rstd[:, :], ALU.mult).then_inc(rstd_done, 1)

            split_v(0, None)
            ln_scale(0)
            for j in range(SYM_POOL):
                pool.wait_ge(adjT_copied, j + 1)
                nc.gpsimd.tensor_tensor(sym[:, j, :], adj_f[:, j, :], adjT[:, j, :], ALU.add).then_inc(sym_ready, 1)

            def add_b(bt, par, bk):
                if bk == 0:
                    hold(consts_in, 48)
                hold(x_in[par], arrivals(bt, par))
                if bk is None or bk > 1:
                    hold(aux_free, base(bt))
                nc.gpsimd.tensor_tensor(xb[:, par], xin[:, par], b_row[:, :].rearrange("p (o d) -> p o d", o=1)
                                        .to_broadcast([P, T, D]), ALU.add).then_inc(xb_done, 1)

            def body(bt, par, bk):
                pieces, order = lists(bk)
                if bk == B - 1:
                    pool.wait_ge(weights_in, 16 * NV)
                for u in range(T):
                    hold(z_done, bt * T + u + 1)
                    nc.gpsimd.tensor_scalar(z[:, u % 2, :], z[:, u % 2, :], -FAR, 0.0, ALU.mult, ALU.add).then_inc(zfar_done, 1)
                    if u == SCALE_AT and bk != B - 1:
                        ln_scale(bt + 1)
                    if u == XB_AT:
                        add_b(bt, par, bk)
                    for s in pieces[u][0] + pieces[u][1]:
                        k = 4 + bt * VSTEPS
                        if s in ("pw0", "pw1"):
                            n = int(s[2])
                            hold(y_done, bt * PW + n + 1)
                            if n < PW - 1:
                                nc.gpsimd.tensor_tensor(v[:, :], v[:, :], y[:, :], ALU.add).then_inc(v_step, 1)
                                split_v(k + 5 * n + 1, 0)
                            else:
                                nc.gpsimd.tensor_tensor(vsum[:, :], v[:, :], y[:, :], ALU.add).then_inc(v_step, 1)
                        if s == "norm":
                            hold(tot_done, bt * 1 + 1)
                            nc.gpsimd.tensor_tensor(v[:, :], vsum[:, :], rtot[:, 0:1].to_broadcast([P, T]), ALU.mult)\
                                .then_inc(v_step, 1)
                            split_v(k + 5 * (PW - 1) + 2, 0)
                        if bk == B - 1 and s in PREP2:
                            P2.pool_step(s, 0, 0)

            batches(pool, body)
            for s in TAIL1:
                if s in PREP2:
                    P2.pool_step(s, 0, 0)

        @block.scalar
        def _(act):
            act.sem_inc(oT_done, 1)
            def normalize(n, par, half):
                act.wait_ge(rstd_done, n * 2 + 2)
                for t in range(HT * half, HT * (half + 1)):
                    ins = nc.scalar.activation(h0[:, t, :], xin[:, par, t, :],
                                               ACT.Relu, bias=nmr[:, t:t + 1], scale=rstd[:, t:t + 1])
                ins.then_inc(h0_done, 1)

            def prep(s, value, par):
                if s in ("h0T0", "h0T1"):
                    k = int(s[-1])
                    act.wait_ge(aux_ready, value)
                    nc.scalar.activation(h0T[:, HALF * k:HALF * (k + 1)], aux, ACT.Copy).then_inc(aux_free, 1)
                if s in ("hT0", "hT1"):
                    k = int(s[-1])
                    act.wait_ge(aux_ready, value)
                    nc.scalar.activation(hT[:, par, HALF * k:HALF * (k + 1)], aux, ACT.Identity, bias=blin_col[:, 0:1])\
                        .then_inc(aux_free, 1)
                if s in ("hrow0", "hrow1"):
                    k = int(s[-1])
                    act.wait_ge(aux_ready, value)
                    nc.scalar.activation(hrow[:, par, HT * k:HT * (k + 1), :].rearrange("p t d -> p (t d)"), aux, ACT.Copy)\
                        .then_inc(aux_free, 1)

            act.wait_ge(consts_in, 48)
            act.wait_ge(x_in[0], 16)
            for half in range(2):
                normalize(0, 0, half)
            for n, s in enumerate(PREP1):
                prep(s, n + 1, 0)
            for j in range(HT):
                act.wait_ge(adjT_ready, j + 1)
                nc.scalar.activation(adjT[:, j, :], banks[:, j, :].bitcast(BF16), ACT.Identity, bias=ones[:, 0:1], scale=-1.0,
                                     saturate=False).then_inc(adjT_copied, 1)

            def exp_unit(U, u, par):
                act.wait_ge(max_done, U + 1)
                if not isinstance(U, int) or U >= 2:
                    act.wait_ge(thi_ready, U - 1)
                nc.scalar.activation(prob[:, u % 2, :], scores[u % 2], ACT.Exp, bias=nmax[:, u:u + 1],
                                     accum_out=den[:, par, u:u + 1]).then_inc(exp_done, 1)

            def evac_hi(ub, u):
                U = ub * T + u
                act.wait_ge(thi_ready, U + 1)
                g = u // GROUP
                if u % GROUP == 0 and (not isinstance(U, int) or U >= 2 * GROUP):
                    act.wait_ge(av_done, ub * 2 + g - 1)
                c = P * (u % GROUP)
                nc.scalar.activation(pt[:, g, HT:T, c:c + P],
                                     banks[:, BANK_T + 1, :].rearrange("p (t n) -> p t n", t=HT), ACT.Copy)\
                    .then_inc(pthi_done, 1)

            def copy_out(g, half, value):
                act.wait_ge(av_done, g + 1)
                if value is not None:
                    act.wait_ge(aux_ready, value)
                nc.scalar.activation(oT[:, HALF * half:HALF * (half + 1)], obank, ACT.Copy).then_inc(oT_done, 1)

            def body(bt, par, bk):
                pieces, order = lists(bk)
                U0 = bt * T

                def aside(s):
                    value = base(bt) + order.index(s) + 1 if s in order else None
                    if bk == B - 1:
                        P2.act_step(s, 0, 0, value)
                    else:
                        prep(s, value, 1 - par)

                for u in range(T):
                    if bk != 0 or u >= 1:
                        exp_unit(U0 + u - 1, (u - 1) % T, par if u >= 1 else 1 - par)
                    for s in pieces[u][0]:
                        aside(s)
                    if bk != 0 or u >= 2:
                        evac_hi(bt if u >= 2 else bt - 1, (u - 2) % T)
                    if u == 1 and bk != 0:
                        copy_out(bt * 2 - 2, 0, base(bt))
                    if u == 5 and bk != 0:
                        copy_out(bt * 2 - 1, 1, None)
                    for half, at in enumerate(RELU_AT):
                        if at == u and bk != B - 1:
                            act.wait_ge(x_in[1 - par], arrivals(bt + 1, 1 - par))
                            normalize(bt + 1, 1 - par, half)
                    for s in pieces[u][1]:
                        aside(s)

            batches(act, body)
            _, order = lists(B - 1)
            for s in TAIL1:
                if s == "attn0":
                    exp_unit(B * T - 1, T - 1, (B - 1) % 2)
                    evac_hi(B - 1, T - 2)
                if s == "attn1":
                    copy_out(2 * B - 2, 0, base(B - 1) + order.index("ot1") + 1)
                    evac_hi(B - 1, T - 1)
                    copy_out(2 * B - 1, 1, None)
                if s in PREP2:
                    P2.act_step(s, 0, 0, base(B - 1) + order.index(s) + 1 if s in order else None)

        @block.vector
        def _(dve):
            def hold(s, value):
                dve.wait_ge(s, value)
                dve.sem_inc(held_dve, 1)

            def ln_stats(n, par, half):
                hold(x_in[par], arrivals(n, par))
                for t in range(HT * half, HT * (half + 1)):
                    ins = nc.vector.bn_stats(stats[:, t, :], xin[:, par, t, :])
                if half == 0:
                    return
                if not isinstance(n, int) or n > 0:
                    hold(rstd_done, n * 2)
                ins.then_inc(stats_done, 1)
                hold(stats_done, n * 1 + 1)
                for t in range(T):
                    ins = nc.vector.bn_aggr(mv[:, t, :], stats[:, t, :])
                ins.then_inc(mv_done, 1)

            for half in range(2):
                ln_stats(0, 0, half)
            for t in range(T):
                dve.wait_ge(adj_in[t], 16)
                nc.vector.tensor_scalar(off[:, t, :], adj_f[:, t, :], -1.0, 1.0, ALU.mult, ALU.add).then_inc(off_ready, 1)
            for j in range(HT, T):
                dve.wait_ge(adjT_ready, j + 1)
                nc.vector.tensor_scalar(adjT[:, j, :], banks[:, j, :].bitcast(BF16), -1.0, 1.0, ALU.mult, ALU.add,
                                        saturate=False)\
                    .then_inc(adjT_copied2, 1)
            dve.wait_ge(adjT_copied2, HT)
            dve.wait_ge(adjT_copied, HT)
            for j in range(SYM_POOL, T):
                nc.vector.tensor_tensor(sym[:, j, :], adj_f[:, j, :], adjT[:, j, :], ALU.add).then_inc(sym_ready, 1)
            dve.wait_ge(off_ready, T)

            def mask_unit(U, u):
                dve.wait_ge(s_ready, U + 1)
                nc.vector.scalar_tensor_tensor(out=z[:, u % 2, :], in0=scores[u % 2], scalar=0.0, in1=off[:, u, :],
                                               op0=ALU.is_equal, op1=ALU.max).then_inc(z_done, 1)

            def max_unit(U, u):
                hold(zfar_done, U + 1)
                nc.vector.tensor_tensor_reduce(scores[u % 2], scores[u % 2], z[:, u % 2, :], 1.0, -3.0e38, ALU.add, ALU.max,
                                               top[:, u:u + 1]).then_inc(top_done, 1)
                if not isinstance(U, int) or U >= T:
                    hold(exp_done, U - T + 1)
                dve.wait_ge(top_done, U + 1)
                nc.vector.tensor_scalar(nmax[:, u:u + 1], top[:, u:u + 1], -1.0, None, ALU.mult).then_inc(max_done, 1)

            def evac_lo(ub, u):
                U = ub * T + u
                hold(tlo_ready, U + 1)
                g = u // GROUP
                if u % GROUP == 0 and (not isinstance(U, int) or U >= 2 * GROUP):
                    dve.wait_ge(av_done, ub * 2 + g - 1)
                c = P * (u % GROUP)
                nc.vector.tensor_copy(pt[:, g, 0:HT, c:c + P],
                                      banks[:, BANK_T, :].rearrange("p (t n) -> p t n", t=HT)).then_inc(ptlo_done, 1)

            def power(s, value, bt):
                if s in ("pw0", "pw1"):
                    hold(aux_ready, value)
                    hold(v_ready, bt * PW + 1 + int(s[2]))
                    nc.vector.tensor_reduce(y[:, :], aux[:, 0:3 * T].rearrange("p (t k) -> p t k", k=3), AX.X, ALU.add)\
                        .then_inc(y_done, 1)
                    hold(y_done, bt * PW + int(s[2]) + 1)
                    dve.sem_inc(aux_free, 1)
                if s == "norm":
                    hold(aux_ready, value)
                    nc.vector.tensor_reduce(tot[:, :], aux[:, 0:T], AX.X, ALU.add).then_inc(fin_step, 1)
                    hold(fin_step, bt * 2 + 1)
                    dve.sem_inc(aux_free, 1)
                    nc.vector.tensor_scalar(tot2[:, :], tot[:, :], TINY, None, ALU.max).then_inc(fin_step, 1)
                    hold(fin_step, bt * 2 + 2)
                    nc.vector.reciprocal(rtot[:, :], tot2[:, :]).then_inc(tot_done, 1)

            def eigenvalue(s, value):
                if s == "last":
                    dve.wait_ge(aux_ready, value)
                    nc.vector.tensor_reduce(y[:, :], aux[:, 0:3 * T].rearrange("p (t k) -> p t k", k=3), AX.X, ALU.add)\
                        .then_inc(aux_free, 1)
                    dve.wait_ge(aux_free, value)
                    nc.vector.tensor_tensor_reduce(junk[:, :], v[:, :], y[:, :], 1.0, 0.0, ALU.mult, ALU.add, nd[:, 0:1])\
                        .then_inc(fin_step, 1)
                    nc.vector.tensor_tensor_reduce(junk2[:, :], v[:, :], v[:, :], 1.0, 0.0, ALU.mult, ALU.add, nd[:, 1:2])\
                        .then_inc(fin_step, 1)
                    return
                dve.wait_ge(aux_ready, value)
                nc.vector.tensor_copy(fin[:, 0:2], aux[:, 0:2]).then_inc(fin_step, 1)
                n = 2 * B + 3
                dve.wait_ge(fin_step, n)
                dve.sem_inc(aux_free, 1)
                for ins in (lambda: nc.vector.tensor_scalar(fin[:, 2:3], fin[:, 1:2], TINY, None, ALU.max),
                            lambda: nc.vector.reciprocal(fin[:, 3:4], fin[:, 2:3]),
                            lambda: nc.vector.tensor_tensor(fin[:, 4:5], fin[:, 0:1], fin[:, 3:4], ALU.mult),
                            lambda: nc.vector.tensor_scalar(fin[:, 5:6], fin[:, 4:5], 0.25, 0.5e-8, ALU.mult, ALU.add)):
                    dve.wait_ge(fin_step, n)
                    ins().then_inc(fin_step, 1)
                    n += 1
                dve.wait_ge(fin_step, n)
                nc.vector.reciprocal(two_over_lam[:, :], fin[:, 5:6]).then_inc(lam_done, 1)

            def output(s, value, n, par):
                k = int(s[-1])
                if k == 0:
                    hold(exp_done, (n + 1) * T)
                    nc.vector.reciprocal(rden[:, :], den[:, par, :]).then_inc(rden_done, 1)
                    hold(rden_done, n * 1 + 1)
                    if not isinstance(n, int) or n > 0:
                        hold(x1_out, n * 16 + 16)
                hold(aux_ready, value)
                hold(xb_done, n * 1 + 1)
                for q in range(HT):
                    t = HT * k + q
                    ins = nc.vector.scalar_tensor_tensor(out=xn[:, t, :], in0=aux[:, P * q:P * (q + 1)], scalar=rden[:, t:t + 1],
                                                         in1=xb[:, par, t, :], op0=ALU.mult, op1=ALU.add)
                ins.then_inc(aux_free, 1)

            def body(bt, par, bk):
                pieces, order = lists(bk)
                U0 = bt * T
                def aside(half, u):
                    for s in pieces[u][half]:
                        value = base(bt) + order.index(s) + 1 if s in order else None
                        power(s, value, bt)
                        if s in ("ot0", "ot1"):
                            output(s, value, bt - 1, 1 - par)
                        if bk == B - 1 and s in ("last", "nd"):
                            eigenvalue(s, value)
                        if bk == B - 1 and s in PREP2:
                            P2.dve_step(s, 0, value or base(bt) + order.index("g1") + 1)

                for u in range(T):
                    mask_unit(U0 + u, u)
                    aside(0, u)
                    if bk != 0 or u >= 2:
                        evac_lo(bt if u >= 2 else bt - 1, (u - 2) % T)
                    max_unit(U0 + u, u)
                    aside(1, u)
                    if u in LN_AT and bk != B - 1:
                        ln_stats(bt + 1, 1 - par, LN_AT.index(u))

            batches(dve, body)
            _, order = lists(B - 1)
            for s in TAIL1:
                value = base(B - 1) + order.index(s) + 1 if s in order else None
                if s == "attn0":
                    evac_lo(B - 1, T - 2)
                if s == "attn1":
                    evac_lo(B - 1, T - 1)
                    for j in range(T):
                        nc.vector.tensor_scalar(off[:, j, :], off[:, j, :], -FAR, None, ALU.mult).then_inc(off_ready, 1)
                if s in ("fo0", "fo1"):
                    output(s, value, B - 1, (B - 1) % 2)
                if s in ("ag0", "ag1"):
                    dve.wait_ge(lam_done, 1)
                if s in PREP2:
                    P2.dve_step(s, 0, value or base(B - 1) + order.index("ag1") + 1)
            dve.wait_ge(off_ready, 2 * T)

        @block.tensor
        def _(pe):
            pe.wait_ge(idents, 2)

            def turn_off(i, j):
                return nc.tensor.transpose(banks[:, j, :].bitcast(BF16)[:, P * i:P * (i + 1)],
                                           off[:, i, P * j:P * (j + 1)], identb[:, :])

            def prep(s, value, par, n):
                k = int(s[-1])
                if not isinstance(value, int) or value > 1:
                    pe.wait_ge(aux_free, value - 1)
                if s == "h0T0":
                    pe.wait_ge(h0_done, n * 2 + 2)
                if s in ("h0T0", "h0T1"):
                    for q in range(HT):
                        ins = nc.tensor.transpose(aux[:, P * q:P * (q + 1)], h0[:, HT * k + q, :], ident[:, :])
                if s in ("hT0", "hT1"):
                    ins = nc.tensor.matmul(aux, w_sb[:, :], h0T[:, HALF * k:HALF * (k + 1)], start=True, stop=True)
                if s in ("hrow0", "hrow1"):
                    for q in range(HT):
                        t = HT * k + q
                        ins = nc.tensor.transpose(aux[:, P * q:P * (q + 1)], hT[:, par, P * t:P * (t + 1)], ident[:, :])
                ins.then_inc(aux_ready, 1)

            def power(s, value, n):
                pe.wait_ge(aux_free, value - 1)
                pe.wait_ge(v_ready, n) if s != "norm" else pe.wait_ge(v_step, n)
                if s == "norm":
                    nc.tensor.matmul(aux[:, 0:T], ones[:, :], vsum[:, :], start=True, stop=True).then_inc(aux_ready, 1)
                    return
                for j in range(T):
                    for i in range(T):
                        ins = nc.tensor.matmul(aux[:, 3 * j:3 * j + 3], sym[:, i, P * j:P * (j + 1)], vp[:, i, :],
                                               start=(i == 0), stop=(i == T - 1))
                ins.then_inc(aux_ready, 1)

            for i in range(T):
                pe.wait_ge(off_ready, i + 1)
                for j in range(T - 1):
                    ins = turn_off(i, j)
                if i == T - 1:
                    ins.then_inc(adjT_ready, T - 1)
                n = i - (T - len(PREP1))
                if n >= 0:
                    if n == 0:
                        pe.wait_ge(consts_in, 48)
                    prep(PREP1[n], n + 1, 0, 0)
            pe.wait_ge(aux_free, len(PREP1))
            for i in range(T):
                ins = turn_off(i, T - 1)
            ins.then_inc(adjT_ready, 1)

            def scores_unit(U, u, par):
                if not isinstance(U, int) or U >= 2:
                    pe.wait_ge(exp_done, U - 1)
                else:
                    pe.wait_ge(adjT_copied, 2 * U + 2)
                for k in range(2):
                    ins = nc.tensor.matmul(scores[u % 2][:, HALF * k:HALF * (k + 1)], hT[:, par, P * u:P * (u + 1)],
                                           hT[:, par, HALF * k:HALF * (k + 1)], start=True, stop=True)
                ins.then_inc(s_ready, 1)

            def transpose_unit(U, u):
                pe.wait_ge(exp_done, U + 1)
                for half, (free, ready) in enumerate(((ptlo_done, tlo_ready), (pthi_done, thi_ready))):
                    if not isinstance(U, int) or U >= 1:
                        pe.wait_ge(free, U * 1)
                    for q in range(HT):
                        t = HT * half + q
                        ins = nc.tensor.transpose(banks[:, BANK_T + half, P * q:P * (q + 1)],
                                                  prob[:, u % 2, P * t:P * (t + 1)], ident[:, :])
                    ins.then_inc(ready, 1)

            def values_chunk(g, gpar, par, c):
                if c == 0:
                    pe.wait_ge(ptlo_done, (g + 1) * GROUP)
                    pe.wait_ge(pthi_done, (g + 1) * GROUP)
                    pe.wait_ge(oT_done, g + 1)
                for j in (2 * c, 2 * c + 1):
                    ins = nc.tensor.matmul(obank, hrow[:, par, j, :], pt[:, gpar, j, :], start=(j == 0), stop=(j == T - 1))
                if c == 3:
                    ins.then_inc(av_done, 1)

            def output(k, value, n):
                pe.wait_ge(aux_free, value - 1)
                pe.wait_ge(oT_done, n * 2 + 2 + k)
                for q in range(HT):
                    t = HT * k + q
                    ins = nc.tensor.transpose(aux[:, P * q:P * (q + 1)], oT[:, P * t:P * (t + 1)], ident[:, :])
                ins.then_inc(aux_ready, 1)

            def body(bt, par, bk):
                pieces, order = lists(bk)
                U0 = bt * T

                def aside(half, u):
                    for s in pieces[u][half]:
                        if bk == B - 1 and s.startswith("ag"):
                            P2.pe_step(s, 0, 0, base(bt) + order.index(s[:3]))
                            continue
                        if s not in order:
                            continue
                        value = base(bt) + order.index(s) + 1
                        if bk == B - 1 and s in PREP2:
                            P2.pe_step(s, 0, 0, value)
                        elif s == "last":
                            power(s, value, B * PW + 1)
                        elif s == "nd":
                            pe.wait_ge(aux_free, value - 1)
                            pe.wait_ge(fin_step, 2 * B + 2)
                            nc.tensor.matmul(aux[:, 0:2], ones[:, :], nd[:, :], start=True, stop=True).then_inc(aux_ready, 1)
                        elif s in PREP1:
                            prep(s, value, 1 - par, bt + 1)
                        elif s in ("ot0", "ot1"):
                            output(int(s[-1]), value, bt - 1)
                        elif s == "norm":
                            power(s, value, bt * VSTEPS + 4 + 5 * (PW - 1) + 1)
                        else:
                            if bk == 0 and s == "pw0":
                                pe.wait_ge(sym_ready, T)
                            power(s, value, bt * PW + 1 + int(s[2]))

                if bk == B - 1:
                    pe.wait_ge(weights_in, 16 * NV)
                for u in range(T):
                    if u == 0:
                        pe.wait_ge(aux_free, base(bt) - (2 if bk == 0 else 3))
                    scores_unit(U0 + u, u, par)
                    aside(0, u)
                    if bk != 0 or u >= 2:
                        transpose_unit(U0 + u - 2, (u - 2) % T)
                    if u < 2 and bk != 0:
                        values_chunk(bt * 2 - 2, 0, 1 - par, u + 2)
                    if 2 <= u < 6 and bk != 0:
                        values_chunk(bt * 2 - 1, 1, 1 - par, u - 2)
                    if u >= 6:
                        values_chunk(bt * 2, 0, par, u - 6)
                    aside(1, u)

            batches(pe, body)
            _, order = lists(B - 1)
            for s in TAIL1:
                if s == "attn0":
                    transpose_unit(B * T - 2, T - 2)
                    for c in (2, 3):
                        values_chunk(2 * B - 2, 0, (B - 1) % 2, c)
                if s == "attn1":
                    transpose_unit(B * T - 1, T - 1)
                    for c in range(4):
                        values_chunk(2 * B - 1, 1, (B - 1) % 2, c)
                if s in ("fo0", "fo1"):
                    output(int(s[-1]), base(B - 1) + order.index(s) + 1, B - 1)
                if s == "ag1a":
                    P2.pe_step(s, 0, 0, base(B - 1) + order.index("ag1"))
                elif s in order and s in PREP2:
                    P2.pe_step(s, 0, 0, base(B - 1) + order.index(s) + 1)


def block2(nc, x1_dram, parts_dram, kept_dram, out, banks, shared, prep):
    SCALE = float(HD) ** -0.5
    with ExitStack() as ctx:
        sb = lambda n, s, d: ctx.enter_context(nc.sbuf_tensor(n, s, d))
        sem = lambda n: ctx.enter_context(nc.semaphore(n))
        ident, neg_half, adjT, off, two_over_lam = (shared[k] for k in ("ident", "neg_half", "adjT", "off", "two_over_lam"))

        (vrow, hid, h1x, parts, work, fT, wts, w1_sb, w2_sb, b1_col, vecs, ln, weights_in, x_in, stack_in,
         parts_out, h1_done, nmr_done, ghi_done, grem_done, gmid_done, glo_done, gb_done, lng_applied,
         lng_affine, x1_done, x1_kept, hi_done, rem_done, mid_done, res_done, lo_done) = (
            prep[k] for k in PREP_NAMES)
        pt = sb("pt2", [P, 2, T, H, QN], F32)
        qs = sb("qs", [P, 2, H, N], BF16)
        k1s = sb("k1s", [P, 2, H, N], BF16)
        k2s = sb("k2s", [P, 2, H, N], BF16)
        prob = sb("prob2", [P, 2, N], F32)
        oT = sb("oT2", [P, N], F32)
        post = sb("post", [P, T, D], F32)
        top = sb("top", [P, UNITS], F32)
        ntop = sb("ntop", [P, UNITS], F32)
        den = sb("den2", [P, 2, UNITS], F32)
        rden = sb("rden2", [P, UNITS], F32)
        ln = prep["ln"]
        ln["last"] = norm_buffers("last", sb, sem)

        res_in = sem("res_in")
        out_done = sem("out_done")
        zero_done = sem("zero_done")
        aux_ready = sem("aux_ready2")
        aux_free = sem("aux_free2")
        rden_done = sem("rden_done2")
        ln2_applied = sem("ln2_applied")
        ln2_affine = sem("ln2_affine")
        x2b_done = sem("x2b_done")
        hid_done = sem("hid_done")
        gelu_done = sem("gelu_done")
        ln3_applied = sem("ln3_applied")
        ln3_affine = sem("ln3_affine")
        x1_back = sem("x1_back")
        x1b_done = sem("x1b_done")
        s_ready = sem("s_ready2")
        low_done = sem("low_done")
        ntop_done = sem("ntop_done")
        exp_done = sem("exp_done2")
        tlo_ready = sem("tlo_ready2")
        thi_ready = sem("thi_ready2")
        ptlo_done = sem("ptlo_done2")
        pthi_done = sem("pthi_done2")
        av_done = sem("av_done2")
        oT_done = sem("oT_done2")
        held_pool = sem("held_pool2")
        held_dve = sem("held_dve2")
        held_pe = sem("held_pe2")
        held_sp = sem("held_sp2")

        aux = banks[:, BANK_AUX, :]
        obank = banks[:, BANK_O, 0:QN]
        scores = [banks[:, 2 * k:2 * k + 2, :].rearrange("p a n -> p (a n)") for k in range(2)]
        rem, gf, flat, rows_b = prep_views(work, vecs)
        hidT = hid[:, :, :].rearrange("p c n -> p (c n)")
        x1b = hid[:, 0, :].rearrange("p (t d) -> p t d", t=T)
        res = hid[:, 1, :].rearrange("p (t d) -> p t d", t=T)
        STACKS = (tuple(zip((qs,), SLOTS[0])), tuple(zip((k1s, k2s), SLOTS[1])))
        PER = len(BANKED)
        POST = [s for u in sorted(BESIDE) for half in BESIDE[u] for s in half if s in POST2]

        def beside(bk):
            keep = lambda s: not (bk == 0 and s in POST2) and not (bk == B - 1 and s not in POST2)
            table = {u: [[s for s in half if keep(s)] for half in BESIDE.get(u, ([], []))] for u in range(UNITS)}
            order = [s for u in range(UNITS) for half in table[u] for s in half if s in BANKED]
            return table, order

        def base(bt):
            return 0 if isinstance(bt, int) and bt == 0 else bt * PER - PER // 2

        P2 = Preparation(nc, banks, shared, prep, aux_ready, aux_free, held_pool, held_dve, held_pe)

        def batches(eng, body):
            body(0, 0, 0)
            with eng.Fori(0, (B - 2) // 2) as i:
                for k in (1, 2):
                    body(i * 2 + k, k % 2, None)
            body(B - 1, (B - 1) % 2, B - 1)

        def bank_of(s, n):
            spare = isinstance(n, int) and n == B - 1 and s[-1] in "13"
            return banks[:, 0, :] if spare else aux

        def late(bt, u, lag):
            return (bt, u - lag) if u >= lag else (bt - 1, u - lag + UNITS)

        def quarters(u, at):
            for q in range(T // QT):
                for ago in (0, 1):
                    if q * QU + at == u + ago * UNITS:
                        return q, ago
            return None

        block = ctx.enter_context(nc.Block())

        @block.sync
        def _(sp):
            def hold(s, value):
                sp.wait_ge(s, value)
                sp.sem_inc(held_sp, 1)

            sp.sem_inc(out_done, 16)
            def step(s, n, par):
                if s == "ln1_stats0":
                    if not isinstance(n, int) or n > 0:
                        hold(x1_kept, n * 16)
                    sp.dma_start(h1x[:, :, :], one(x1_dram, n)).then_inc(x_in, 16)
                if s == "keep":
                    hold(x1_done, n * 1 + 1)
                    sp.dma_start(rows(kept_dram[par]), h1x[:, :, :]).then_inc(x1_kept, 16)
                if s in ("qstack", "kstack"):
                    k = "qk".index(s[0])
                    if k == 0 and (not isinstance(n, int) or n >= 2):
                        hold(s_ready, (n - 1) * UNITS)
                    hold(lo_done, n * 2 + k + 1)
                    sp.dma_start(parts_dram[k].rearrange("a p n -> p a n"), parts[:, 3 * k:3 * k + 3, :]).then_inc(parts_out, 16)
                    hold(parts_out, n * 32 + 16 * (k + 1))
                    read_stack(k, par)

            def read_stack(k, par):
                for dst, slots in STACKS[k]:
                    for at, part in enumerate(slots):
                        if part is not None:
                            sp.dma_start(dst[HD * at:HD * (at + 1), par, :, :],
                                         parts_dram[k, part].rearrange("(h r) n -> r h n", r=HD)).then_inc(stack_in, 16)

            def post_step(s, n, value):
                if s == "ln3_stats0":
                    hold(aux_free, value)
                    sp.dma_start(res, one(x1_dram, n)).then_inc(res_in, 16)

            def store(n):
                hold(res_done, n + 2)
                sp.dma_start(one(out, n), post[:, :, :]).then_inc(out_done, 16)

            for k in range(2):
                if k == 1:
                    hold(parts_out, 32)
                read_stack(k, 0)

            def body(bt, par, bk):
                table, order = beside(bk)
                if bk != B - 1:
                    step("ln1_stats0", bt + 1, 1 - par)
                if bk is None or bk > 1:
                    store(bt - 2)
                if bk != 0:
                    hold(aux_free, base(bt))
                    sp.dma_start(x1b, rows(kept_dram[1 - par])).then_inc(x1_back, 16)
                for u in range(UNITS):
                    for s in table[u][0] + table[u][1]:
                        if s in POST2:
                            post_step(s, bt - 1, base(bt) + order.index("w21") + 1)
                        elif s != "ln1_stats0":
                            step(s, bt + 1, 1 - par)

            for bt in (0, 1):
                body(bt, bt % 2, bt)
            with sp.Fori(0, (B - 4) // 2) as i:
                for k in (2, 3):
                    body(i * 2 + k, k % 2, None)
            for bt in (B - 2, B - 1):
                body(bt, bt % 2, bt)
            store(B - 2)
            hold(aux_free, base(B - 1) + PER // 2)
            sp.dma_start(x1b, rows(kept_dram[(B - 1) % 2])).then_inc(x1_back, 16)
            for s in POST:
                post_step(s, B - 1, base(B - 1) + PER)
            store(B - 1)
            sp.wait_ge(out_done, 16 * (B + 1))

        @block.gpsimd
        def _(pool):
            def hold(s, value):
                pool.wait_ge(s, value)
                pool.sem_inc(held_pool, 1)

            pool.sem_inc(res_done, 1)
            for par in range(2):
                nc.gpsimd.memset(k2s[HD:2 * HD, par], 0.0).then_inc(zero_done, 1)
            pool.wait_ge(zero_done, 2)
            pool.wait_ge(weights_in, 16 * NV)

            def post_step(s, n):
                if isinstance(n, int) and n == B - 1 and s == "ln2_apply1":
                    return
                if s == "x1b":
                    hold(x1_back, n * 16 + 16)
                    nc.gpsimd.tensor_tensor(x1b, x1b, rows_b("bo"), ALU.add).then_inc(x1b_done, 1)
                if s == "ln2_stats1":
                    P2.scale("last", n, 0)
                if s == "ln2_apply1":
                    hold(ln2_applied, n * 1 + 1)
                    nc.gpsimd.tensor_tensor(post[:, :, :], post[:, :, :], rows_b("g2"), ALU.mult).then_inc(ln2_affine, 1)
                    hold(ln2_affine, n * 2 + 1)
                    nc.gpsimd.tensor_tensor(post[:, :, :], post[:, :, :], rows_b("be2"), ALU.add).then_inc(ln2_affine, 1)
                if s == "w11":
                    hold(hid_done, n * 4 + 1)
                    nc.gpsimd.tensor_tensor(post[:, :, :], post[:, :, :], rows_b("b2"), ALU.add).then_inc(x2b_done, 1)
                if s == "ln3_stats1":
                    P2.scale("last", n, 1)
                if s == "ln3_apply1":
                    hold(res_in, n * 16 + 16)
                    nc.gpsimd.tensor_tensor(res, res, rows_b("be3"), ALU.add).then_inc(ln3_affine, 1)
                    if isinstance(n, int) and n == B - 1:
                        return
                    hold(ln3_applied, n * 1 + 1)
                    nc.gpsimd.tensor_tensor(post[:, :, :], post[:, :, :], rows_b("g3"), ALU.mult).then_inc(ln3_affine, 1)
                    hold(ln3_affine, n * 2 + 2)
                    nc.gpsimd.tensor_tensor(post[:, :, :], post[:, :, :], res, ALU.add).then_inc(res_done, 1)

            def body(bt, par, bk):
                table, order = beside(bk)
                for u in range(UNITS):
                    for s in table[u][0] + table[u][1]:
                        P2.pool_step(s, bt + 1, 1 - par) if s not in POST2 else post_step(s, bt - 1)

            batches(pool, body)
            for s in POST:
                post_step(s, B - 1)

        @block.scalar
        def _(act):
            def post_step(s, n, value):
                bank = bank_of(s, n)
                k = int(s[-1]) if s in BANKED else 0
                if s in ("ot0", "ot1", "x2t0", "x2t1"):
                    act.wait_ge(aux_ready, value)
                    nc.scalar.activation(fT[:, HALF * k:HALF * (k + 1)], bank, ACT.Copy).then_inc(aux_free, 1)
                if s in ("w10", "w11", "w12", "w13"):
                    act.wait_ge(aux_ready, value)
                    if k == 2:
                        act.wait_ge(res_done, n + 1)
                    nc.scalar.activation(hidT[:, HALF * k:HALF * (k + 1)], bank, ACT.Identity, bias=b1_col[:, k // 2:k // 2 + 1])\
                        .then_inc(hid_done, 1)
                    act.wait_ge(hid_done, n * 4 + k + 1)
                    act.sem_inc(aux_free, 1)
                if s == "gelu":
                    act.wait_ge(hid_done, n * 4 + 4)
                    nc.scalar.activation(hidT, hidT, ACT.Gelu).then_inc(gelu_done, 1)

            def exp_unit(bt, u, par):
                U = bt * UNITS + u
                act.wait_ge(ntop_done, U + 1)
                if not isinstance(U, int) or U >= 2:
                    act.wait_ge(thi_ready, U - 1)
                nc.scalar.activation(prob[:, u % 2, :], scores[u % 2], ACT.Exp, bias=ntop[:, u:u + 1], scale=SCALE,
                                     accum_out=den[:, par, u:u + 1]).then_inc(exp_done, 1)

            def evac_lo(bt, u):
                q, i, h = u // QU, u % QU // H, u % H
                act.wait_ge(tlo_ready, bt * UNITS + u + 1)
                g = bt * (T // QT) + q
                if u % QU == 0 and (not isinstance(g, int) or g >= 2):
                    act.wait_ge(av_done, g - 1)
                nc.scalar.activation(pt[:, q % 2, 0:HT, h, P * i:P * (i + 1)],
                                     banks[:, BANK_T, :].rearrange("p (t n) -> p t n", t=HT), ACT.Copy)\
                    .then_inc(ptlo_done, 1)

            def evac_hi(bt, u):
                q, i, h = u // QU, u % QU // H, u % H
                act.wait_ge(thi_ready, bt * UNITS + u + 1)
                g = bt * (T // QT) + q
                if u % QU == 0 and (not isinstance(g, int) or g >= 2):
                    act.wait_ge(av_done, g - 1)
                nc.scalar.activation(pt[:, q % 2, HT:T, h, P * i:P * (i + 1)],
                                     banks[:, BANK_T + 1, :].rearrange("p (t n) -> p t n", t=HT), ACT.Copy)\
                    .then_inc(pthi_done, 1)

            def copy_out(bt, q, value):
                act.wait_ge(av_done, bt * (T // QT) + q + 1)
                if value is not None:
                    act.wait_ge(aux_ready, value)
                nc.scalar.activation(oT[:, QN * q:QN * (q + 1)], obank, ACT.Copy).then_inc(oT_done, 1)

            act.wait_ge(weights_in, 16 * NV)

            def body(bt, par, bk):
                table, order = beside(bk)

                def aside(half, u):
                    for s in table[u][half]:
                        value = base(bt) + order.index(s) + 1 if s in BANKED else None
                        P2.act_step(s, bt + 1, 1 - par, value) if s not in POST2 else post_step(s, bt - 1, value)

                for u in range(UNITS):
                    if bk != 0 or u >= 1:
                        exp_unit(*late(bt, u, 1), par if u >= 1 else 1 - par)
                    aside(0, u)
                    if bk != 0 or u >= 2:
                        if late(0, u, 2)[1] in LO_BY_SCALAR:
                            evac_lo(*late(bt, u, 2))
                        evac_hi(*late(bt, u, 2))
                    found = quarters(u, COPY_AT)
                    if found and not (found[1] and bk == 0):
                        q, ago = found
                        copy_out(bt - ago, q, base(bt) + order.index("or1") + 1 if q == 0 and bk != 0 else None)
                    aside(1, u)

            batches(act, body)
            exp_unit(B - 1, UNITS - 1, (B - 1) % 2)
            for u in (UNITS - 2, UNITS - 1):
                if u in LO_BY_SCALAR:
                    evac_lo(B - 1, u)
                evac_hi(B - 1, u)
            copy_out(B - 1, T // QT - 1, None)
            value = base(B - 1) + PER // 2
            for s in POST:
                value += s in BANKED
                post_step(s, B - 1, value)

        @block.vector
        def _(dve):
            def hold(s, value):
                dve.wait_ge(s, value)
                dve.sem_inc(held_dve, 1)

            dve.wait_ge(weights_in, 16 * NV)

            def post_step(s, n, value, par):
                bank = bank_of(s, n)
                k = int(s[-1]) if s[-1] in "01" else 0
                tiles = slice(HT * k, HT * (k + 1))
                if s == "or0":
                    dve.wait_ge(exp_done, (n + 1) * UNITS)
                    nc.vector.reciprocal(rden[:, :], den[:, par, :]).then_inc(rden_done, 1)
                    dve.wait_ge(rden_done, n * 1 + 1)
                    dve.wait_ge(out_done, n * 16 + 16)
                if s in ("or0", "or1"):
                    dve.wait_ge(aux_ready, value)
                    by_head = lambda a: a.rearrange("p (g d) -> p g d", d=HD)
                    nc.vector.tensor_tensor(by_head(flat(post[:, tiles, :])), by_head(bank),
                                            bc(rden[:, HT * H * k:HT * H * (k + 1)], HD), ALU.mult).then_inc(aux_free, 1)
                if s in ("wo0", "wo1"):
                    dve.wait_ge(aux_ready, value)
                    dve.wait_ge(x1b_done, n * 1 + 1)
                    nc.vector.tensor_tensor(flat(post[:, tiles, :]), bank, flat(x1b[:, tiles, :]), ALU.add)\
                        .then_inc(aux_free, 1)
                if s in ("ln2_stats0", "ln2_stats1"):
                    dve.wait_ge(aux_free, value)
                    P2.statistics("last", n, 0, post, k)
                if s in ("ln2_apply0", "ln2_apply1"):
                    P2.apply("last", n, 0, post, k, ln2_applied)
                    if isinstance(n, int) and n == B - 1 and k == 1:
                        dve.wait_ge(ln2_applied, B)
                        nc.vector.tensor_tensor(post[:, :, :], post[:, :, :], rows_b("g2"), ALU.mult).then_inc(ln2_affine, 1)
                        dve.wait_ge(ln2_affine, 2 * B - 1)
                        nc.vector.tensor_tensor(post[:, :, :], post[:, :, :], rows_b("be2"), ALU.add).then_inc(ln2_affine, 1)
                if s in ("w20", "w21"):
                    dve.wait_ge(aux_ready, value)
                    dve.wait_ge(x2b_done, n * 1 + 1)
                    nc.vector.tensor_tensor(flat(post[:, tiles, :]), bank, flat(post[:, tiles, :]), ALU.add)\
                        .then_inc(aux_free, 1)
                if s in ("ln3_stats0", "ln3_stats1"):
                    dve.wait_ge(aux_free, value)
                    P2.statistics("last", n, 1, post, k)
                if s in ("ln3_apply0", "ln3_apply1"):
                    P2.apply("last", n, 1, post, k, ln3_applied)
                    if isinstance(n, int) and n == B - 1 and k == 1:
                        dve.wait_ge(ln3_applied, B)
                        nc.vector.tensor_tensor(post[:, :, :], post[:, :, :], rows_b("g3"), ALU.mult).then_inc(ln3_affine, 1)
                        dve.wait_ge(ln3_affine, 2 * B)
                        nc.vector.tensor_tensor(post[:, :, :], post[:, :, :], res, ALU.add).then_inc(res_done, 1)

            def low_unit(bt, u):
                U = bt * UNITS + u
                hold(s_ready, U + 1)
                nc.vector.tensor_tensor_reduce(scores[u % 2], scores[u % 2], off[:, u // H, :], 1.0, -3.0e38, ALU.add,
                                               ALU.max, top[:, u:u + 1]).then_inc(low_done, 1)

            def evac_lo(bt, u):
                q, i, h = u // QU, u % QU // H, u % H
                dve.wait_ge(tlo_ready, bt * UNITS + u + 1)
                g = bt * (T // QT) + q
                if u % QU == 0 and (not isinstance(g, int) or g >= 2):
                    dve.wait_ge(av_done, g - 1)
                nc.vector.tensor_copy(pt[:, q % 2, 0:HT, h, P * i:P * (i + 1)],
                                      banks[:, BANK_T, :].rearrange("p (t n) -> p t n", t=HT)).then_inc(ptlo_done, 1)

            def bias_unit(bt, u):
                dve.wait_ge(low_done, bt * UNITS + u + 1)
                nc.vector.tensor_scalar(ntop[:, u:u + 1], top[:, u:u + 1], -SCALE, None, ALU.mult).then_inc(ntop_done, 1)

            def body(bt, par, bk):
                table, order = beside(bk)
                seen = [base(bt)]

                def aside(half, u):
                    for s in table[u][half]:
                        if s in BANKED:
                            seen[0] = base(bt) + order.index(s) + 1
                        P2.dve_step(s, bt + 1, seen[0]) if s not in POST2 else post_step(s, bt - 1, seen[0], 1 - par)

                for u in range(UNITS):
                    low_unit(bt, u)
                    bias_unit(bt, u)
                    aside(0, u)
                    if (bk != 0 or u >= 2) and late(0, u, 2)[1] not in LO_BY_SCALAR:
                        evac_lo(*late(bt, u, 2))
                    aside(1, u)

            batches(dve, body)
            for u in (UNITS - 2, UNITS - 1):
                if u not in LO_BY_SCALAR:
                    evac_lo(B - 1, u)
            value = base(B - 1) + PER // 2
            for s in POST:
                value += s in BANKED
                post_step(s, B - 1, value, (B - 1) % 2)

        @block.tensor
        def _(pe):
            pe.wait_ge(weights_in, 16 * NV)

            def post_step(s, n, value):
                if s not in BANKED:
                    return
                k = int(s[-1])
                bank = bank_of(s, n)
                if bank is aux:
                    P2.bank_free(value)
                if s in ("or0", "or1"):
                    if k == 0:
                        pe.wait_ge(oT_done, (n + 1) * (T // QT))
                    ins = P2.turn(oT, k, False, bank)
                if s in ("ot0", "ot1"):
                    ins = P2.turn(post, k, True, bank)
                if s in ("wo0", "wo1"):
                    ins = P2.times(wts["o"][:, :], k, bank)
                if s in ("x2t0", "x2t1"):
                    if k == 0:
                        pe.wait_ge(ln2_affine, n * 2 + 2)
                    ins = P2.turn(post, k, True, bank)
                if s in ("w10", "w11", "w12", "w13"):
                    c, half = k // 2, k % 2
                    ins = nc.tensor.matmul(bank, w1_sb[:, P * c:P * (c + 1)], fT[:, HALF * half:HALF * (half + 1)],
                                           start=True, stop=True)
                if s in ("w20", "w21"):
                    if k == 0:
                        pe.wait_ge(gelu_done, n * 1 + 1)
                    for q in range(HT):
                        t = HT * k + q
                        for c in range(HC):
                            ins = nc.tensor.matmul(bank[:, P * q:P * (q + 1)], hidT[:, N * c + P * t:N * c + P * (t + 1)],
                                                   w2_sb[:, c, :], start=(c == 0), stop=(c == HC - 1))
                ins.then_inc(aux_ready, 1)

            def scores_unit(bt, u, par):
                U = bt * UNITS + u
                i, h = u // H, u % H
                if not isinstance(U, int) or U >= 2:
                    pe.wait_ge(exp_done, U - 1)
                for stack, first in ((k1s, True), (k2s, False)):
                    for k in range(2):
                        ins = nc.tensor.matmul(scores[u % 2][:, HALF * k:HALF * (k + 1)], qs[:, par, h, P * i:P * (i + 1)],
                                               stack[:, par, h, HALF * k:HALF * (k + 1)], start=first, stop=not first)
                ins.then_inc(s_ready, 1)

            def transpose_unit(bt, u):
                U = bt * UNITS + u
                pe.wait_ge(exp_done, U + 1)
                for half, (free, ready) in enumerate(((ptlo_done, tlo_ready), (pthi_done, thi_ready))):
                    if not isinstance(U, int) or U >= 1:
                        pe.wait_ge(free, U * 1)
                    for q in range(HT):
                        t = HT * half + q
                        ins = nc.tensor.transpose(banks[:, BANK_T + half, P * q:P * (q + 1)],
                                                  prob[:, u % 2, P * t:P * (t + 1)], ident[:, :])
                    ins.then_inc(ready, 1)

            def values_half(bt, q, par, half):
                g = bt * (T // QT) + q
                if half == 0:
                    pe.wait_ge(ptlo_done, bt * UNITS + (q + 1) * QU)
                    pe.wait_ge(pthi_done, bt * UNITS + (q + 1) * QU)
                    if not isinstance(g, int) or g >= 1:
                        pe.wait_ge(oT_done, g * 1)
                for j in range(HT * half, HT * (half + 1)):
                    for h in range(H):
                        ins = nc.tensor.matmul(banks[HD * h:HD * (h + 1), BANK_O, 0:QN], vrow[:, par, j, HD * h:HD * (h + 1)],
                                               pt[:, q % 2, j, h, :], start=(j == 0), stop=(j == T - 1),
                                               tile_position=(0, HD * h))
                if half == 1:
                    ins.then_inc(av_done, 1)

            pe.wait_ge(zero_done, 2)

            def body(bt, par, bk):
                table, order = beside(bk)

                def aside(half, u):
                    for s in table[u][half]:
                        if s in BANKED or s in ("ag0a", "ag1a"):
                            value = base(bt) + order.index(s) + 1 if s in BANKED else base(bt) + order.index(s[:3])
                            P2.pe_step(s, bt + 1, 1 - par, value) if s not in POST2 else post_step(s, bt - 1, value)

                for u in range(UNITS):
                    if u == 0:
                        pe.wait_ge(stack_in, (bt + 1) * STACKED)
                        if bk != 0:
                            pe.wait_ge(aux_free, base(bt))
                    scores_unit(bt, u, par)
                    aside(0, u)
                    if bk != 0 or u >= 2:
                        transpose_unit(*late(bt, u, 2))
                    for half, at in enumerate(AV_AT):
                        found = quarters(u, at)
                        if found and not (found[1] and bk == 0):
                            q, ago = found
                            values_half(bt - ago, q, par if ago == 0 else 1 - par, half)
                    aside(1, u)

            batches(pe, body)
            for u in (UNITS - 2, UNITS - 1):
                transpose_unit(B - 1, u)
            for half in range(2):
                values_half(B - 1, T // QT - 1, (B - 1) % 2, half)
            value = base(B - 1) + PER // 2
            for s in POST:
                value += s in BANKED
                post_step(s, B - 1, value)


_INS = ["x", "adj", "L0_gnn_W", "L0_gnn_b_lin", "L0_gnn_b", "L1_gnn_Wc", "L1_gnn_bc", "L1_gnn_g1", "L1_gnn_be1", "L1_gnn_Wq",
        "L1_gnn_Wk", "L1_gnn_Wv", "L1_gnn_Wo", "L1_gnn_bo", "L1_gnn_g2", "L1_gnn_be2", "L1_gnn_W1", "L1_gnn_b1", "L1_gnn_W2",
        "L1_gnn_b2", "L1_gnn_g3", "L1_gnn_be3"]


def kernel(**inputs):
    import numpy as _np
    import concourse.bacc as _bacc
    from concourse import mybir as _mybir
    from concourse.bass_utils import run_bass_kernel_spmd as _run

    nc = _bacc.Bacc("TRN2", target_bir_lowering=False, num_devices=1)
    arrays, args = {}, []
    for name in _INS:
        a = _np.ascontiguousarray(inputs[name])
        arrays[f"in_{name}"] = a
        args.append(nc.dram_tensor(f"in_{name}", a.shape, _mybir.dt.from_np(a.dtype), kind="ExternalInput").ap())
    out = nc.dram_tensor("out_x", (B, N, D), F32, kind="ExternalOutput").ap()
    build(nc, *args, out)
    r = _run(nc, [arrays], core_ids=[0])
    return r.results[0]["out_x"]
```
